# Optimizing a Trainium2 kernel written in Bass

```python
import numpy as np
import jax
import jax.numpy as jnp

def _softmax(x, axis=-1):
    return jax.nn.softmax(x, axis=axis)

def _gelu(x):
    return jax.nn.gelu(x, approximate=True)

def _silu(x):
    return jax.nn.silu(x)

def _sigmoid(x):
    return jax.nn.sigmoid(x)

def _layernorm(x, axis=-1, eps=1e-05):
    m = jnp.mean(x, axis=axis, keepdims=True)
    v = jnp.var(x, axis=axis, keepdims=True)
    return (x - m) / jnp.sqrt(v + eps)

def _scatter_add(tgt, idx, src, axis=0):
    return tgt.at[idx].add(src)

def _segment_sum(src, seg, n):
    return jax.ops.segment_sum(src, seg, n)
kernel_name = 'mk_audio_tower_d4_tok_audfeat512_r4_869778'

def setup_inputs(seed: int=0):
    np.random.seed(seed)
    _w = jnp.asarray

    def _rec_inputs():
        import jax
        import jax.numpy as jnp
        _rk = jax.random.key(seed)
        x = -0.000125008 + 0.999885 * jax.random.normal(jax.random.fold_in(_rk, 1), (4, 750, 128), jnp.float32)
        return x
    x = _rec_inputs()

    def _L0_tok_setup():
        import jax, jax.numpy as jnp
        import numpy as np
        CONTEXT = 5
        DILATION = 1
        BN_EPS = 1e-05
        key = jax.random.key(seed)
        k1, k2, k3 = jax.random.split(key, 3)
        B, S, D, O = (64, 256, 128, 128)
        x = jax.random.normal(k1, (B, S, D), dtype=jnp.float32)
        fan_in = D * CONTEXT
        bound = 1.0 / np.sqrt(fan_in)
        W = jax.random.uniform(k2, (O, fan_in), dtype=jnp.float32, minval=-bound, maxval=bound)
        b = jax.random.uniform(k3, (O,), dtype=jnp.float32, minval=-bound, maxval=bound)
        gamma = jnp.ones((O,), dtype=jnp.float32)
        beta = jnp.zeros((O,), dtype=jnp.float32)
        return {'x': x, 'W': W, 'b': b, 'gamma': gamma, 'beta': beta}
    _L0_tok_all = _L0_tok_setup()
    _L0_tok_in = {k: v for k, v in _L0_tok_all.items() if k in ('W', 'b', 'gamma', 'beta')}
    del _L0_tok_all

    def _L0_attn_setup():
        import jax, jax.numpy as jnp
        import numpy as np
        NUM_HEADS = 8
        NUM_GROUPS = 32
        EPS = 0.0001

        def group_norm(x, scale, bias):
            b, l, c = x.shape
            xg = x.reshape(b, l, NUM_GROUPS, c // NUM_GROUPS)
            mean = jnp.mean(xg, axis=(1, 3), keepdims=True)
            var = jnp.var(xg, axis=(1, 3), keepdims=True)
            xg = (xg - mean) * jax.lax.rsqrt(var + EPS)
            return xg.reshape(b, l, c) * scale + bias
        key = jax.random.key(seed)
        ks = jax.random.split(key, 6)
        bs, L, C = (4, 256, 128)
        hf = C // NUM_HEADS
        x = jax.random.normal(ks[0], (bs, L, C), dtype=jnp.float32)
        W_qkv = jax.random.normal(ks[1], (C, C * 2), dtype=jnp.float32) * (1.0 / C)
        gn_qkv_scale = jnp.ones((C * 2,), dtype=jnp.float32)
        gn_qkv_bias = jnp.zeros((C * 2,), dtype=jnp.float32)
        rel_emb = jax.random.normal(ks[2], (hf * 2, 2 * L - 1), dtype=jnp.float32) * (1.0 / hf)
        gn_out_scale = jnp.ones((C,), dtype=jnp.float32)
        gn_out_bias = jnp.zeros((C,), dtype=jnp.float32)
        return {'x': x, 'W_qkv': W_qkv, 'gn_qkv_scale': gn_qkv_scale, 'gn_qkv_bias': gn_qkv_bias, 'rel_emb': rel_emb, 'gn_out_scale': gn_out_scale, 'gn_out_bias': gn_out_bias}
    _L0_attn_all = _L0_attn_setup()
    _L0_attn_in = {k: v for k, v in _L0_attn_all.items() if k in ('W_qkv', 'gn_qkv_scale', 'gn_qkv_bias', 'rel_emb', 'gn_out_scale', 'gn_out_bias')}
    del _L0_attn_all

    def _L0_ffn_setup():
        import jax, jax.numpy as jnp
        import numpy as np
        D_IN, D_HID, E, K = (128, 512, 10, 2)
        KS = (9, 1)

        def conv1d_same(x, w, b):
            y = jax.lax.conv_general_dilated(x, w, window_strides=(1,), padding='SAME', dimension_numbers=('NCH', 'OIH', 'NCH'))
            return y + b[None, :, None]
        key = jax.random.key(seed)
        ks = jax.random.split(key, 16)
        s = 0.02
        B, T = (2, 512)
        return {'x': jax.random.normal(ks[0], (B, T, D_IN), jnp.float32), 'rc_w1': jax.random.normal(ks[1], (D_IN, D_IN, 3), jnp.float32) * s, 'rc_b1': jnp.zeros((D_IN,), jnp.float32), 'rc_w2': jax.random.normal(ks[2], (E, D_IN, 3), jnp.float32) * s, 'rc_b2': jnp.zeros((E,), jnp.float32), 'sh_w1': jax.random.normal(ks[3], (D_HID, D_IN, KS[0]), jnp.float32) * s, 'sh_b1': jnp.zeros((D_HID,), jnp.float32), 'sh_w2': jax.random.normal(ks[4], (D_IN, D_HID, KS[1]), jnp.float32) * s, 'sh_b2': jnp.zeros((D_IN,), jnp.float32), 'e_w1': jax.random.normal(ks[5], (E, D_IN, D_HID), jnp.float32) * s, 'e_b1': jnp.zeros((E, D_HID), jnp.float32), 'e_w2': jax.random.normal(ks[6], (E, D_HID, D_IN), jnp.float32) * s, 'e_b2': jnp.zeros((E, D_IN), jnp.float32), 'ln_g': jnp.ones((D_IN,), jnp.float32), 'ln_b': jnp.zeros((D_IN,), jnp.float32)}
    _L0_ffn_all = _L0_ffn_setup()
    _L0_ffn_in = {k: v for k, v in _L0_ffn_all.items() if k in ('rc_w1', 'rc_b1', 'rc_w2', 'rc_b2', 'sh_w1', 'sh_b1', 'sh_w2', 'sh_b2', 'e_w1', 'e_b1', 'e_w2', 'e_b2', 'ln_g', 'ln_b')}
    del _L0_ffn_all

    def _L1_attn_setup():
        import jax, jax.numpy as jnp
        import numpy as np
        EMBED_DIM = 128
        key = jax.random.key(seed)
        k1, k2, k3 = jax.random.split(key, 3)
        B, T, E = (8, 512, EMBED_DIM)
        x = jax.random.normal(k1, (B, T, E), dtype=jnp.float32)
        Wq = jax.random.normal(k2, (E, E), dtype=jnp.float32) * E ** (-0.5)
        bq = jnp.zeros((E,), dtype=jnp.float32)
        Wk = jax.random.normal(k3, (E, E), dtype=jnp.float32) * E ** (-0.5)
        bk = jnp.zeros((E,), dtype=jnp.float32)
        return {'x': x, 'Wq': Wq, 'bq': bq, 'Wk': Wk, 'bk': bk}
    _L1_attn_all = _L1_attn_setup()
    _L1_attn_in = {k: v for k, v in _L1_attn_all.items() if k in ('Wq', 'bq', 'Wk', 'bk')}
    del _L1_attn_all

    def _L1_ffn_setup():
        import jax, jax.numpy as jnp
        import numpy as np
        B, S, D = (32, 128, 128)
        E, H, O, K = (8, 512, 128, 2)
        key = jax.random.key(seed)
        ks = jax.random.split(key, 5)
        sc = lambda k, shape, scale: jax.random.normal(k, shape, jnp.float32) * scale
        return {'x': sc(ks[0], (B, S, D), 1.0), 'attn_w': sc(ks[1], (D, 1), 0.05), 'attn_b': jnp.zeros((1,), jnp.float32), 'gate_w': sc(ks[2], (D, E), 0.05), 'gate_b': jnp.zeros((E,), jnp.float32), 'w1': sc(ks[3], (E, D, H), 0.02), 'b1': jnp.zeros((E, H), jnp.float32), 'w2': sc(ks[4], (E, H, O), 0.02), 'b2': jnp.zeros((E, O), jnp.float32)}
    _L1_ffn_all = _L1_ffn_setup()
    _L1_ffn_in = {k: v for k, v in _L1_ffn_all.items() if k in ('attn_w', 'attn_b', 'gate_w', 'gate_b', 'w1', 'b1', 'w2', 'b2')}
    del _L1_ffn_all

    def _L2_attn_setup():
        import jax, jax.numpy as jnp
        import numpy as np
        SQRT_DK = np.sqrt(512.0).astype(np.float32)
        key = jax.random.key(seed)
        k1, k2, k3 = jax.random.split(key, 3)
        x = jax.random.normal(k1, (16, 512, 128), dtype=jnp.float32)
        W1 = jax.random.normal(k2, (128, 10), dtype=jnp.float32) * 0.05
        W2 = jax.random.normal(k3, (10, 128), dtype=jnp.float32) * 0.05
        return {'x': x, 'W1': W1, 'W2': W2}
    _L2_attn_all = _L2_attn_setup()
    _L2_attn_in = {k: v for k, v in _L2_attn_all.items() if k in ('W1', 'W2')}
    del _L2_attn_all

    def _L2_ffn_setup():
        import jax, jax.numpy as jnp
        import numpy as np
        S, B, I, O, H, E, K = (128, 32, 128, 128, 128, 8, 2)

        def _expert(x_seq, Wi, Wh, b, Wo, bo):
            Bsz = x_seq.shape[1]
            Hd = Wh.shape[0]

            def step(carry, xt):
                h, c = carry
                gates = xt @ Wi + h @ Wh + b
                i_, f_, g_, o_ = jnp.split(gates, 4, axis=-1)
                c = jax.nn.sigmoid(f_) * c + jax.nn.sigmoid(i_) * jnp.tanh(g_)
                h = jax.nn.sigmoid(o_) * jnp.tanh(c)
                return ((h, c), h @ Wo + bo)
            init = (jnp.zeros((Bsz, Hd), x_seq.dtype), jnp.zeros((Bsz, Hd), x_seq.dtype))
            _, ys = jax.lax.scan(step, init, x_seq)
            return ys
        key = jax.random.key(seed)
        ks = jax.random.split(key, 6)
        s = 0.02
        return {'x': jax.random.normal(ks[0], (S, B, I), dtype=jnp.float32), 'router_w': jax.random.normal(ks[1], (I, E), dtype=jnp.float32) * s, 'router_b': jnp.zeros((E,), dtype=jnp.float32), 'Wi': jax.random.normal(ks[2], (E, I, 4 * H), dtype=jnp.float32) * s, 'Wh': jax.random.normal(ks[3], (E, H, 4 * H), dtype=jnp.float32) * s, 'b': jnp.zeros((E, 4 * H), dtype=jnp.float32), 'Wo': jax.random.normal(ks[4], (E, H, O), dtype=jnp.float32) * s, 'bo': jnp.zeros((E, O), dtype=jnp.float32)}
    _L2_ffn_all = _L2_ffn_setup()
    _L2_ffn_in = {k: v for k, v in _L2_ffn_all.items() if k in ('router_w', 'router_b', 'Wi', 'Wh', 'b', 'Wo', 'bo')}
    del _L2_ffn_all

    def _L3_attn_setup():
        import jax, jax.numpy as jnp
        import numpy as np
        B, S, IN, HD, H = (2, 512, 128, 32, 16)
        key = jax.random.key(seed)
        ks = jax.random.split(key, 9)
        sc = 0.02
        return {'x': jax.random.normal(ks[0], (B, S, IN), jnp.float32), 'Wl': jax.random.normal(ks[1], (H, IN, IN), jnp.float32) * sc, 'bl': jax.random.normal(ks[2], (H, IN), jnp.float32) * sc, 'Wq': jax.random.normal(ks[3], (H, IN, HD), jnp.float32) * sc, 'Wk': jax.random.normal(ks[4], (H, IN, HD), jnp.float32) * sc, 'Wv': jax.random.normal(ks[5], (H, IN, HD), jnp.float32) * sc, 'Wo': jax.random.normal(ks[6], (IN, H * HD), jnp.float32) * sc, 'bo': jax.random.normal(ks[7], (IN,), jnp.float32) * sc}
    _L3_attn_all = _L3_attn_setup()
    _L3_attn_in = {k: v for k, v in _L3_attn_all.items() if k in ('Wl', 'bl', 'Wq', 'Wk', 'Wv', 'Wo', 'bo')}
    del _L3_attn_all

    def _L3_ffn_setup():
        import jax, jax.numpy as jnp
        import numpy as np
        EPS = 1e-05
        TOP_K = 2

        def layer_norm(x, g, b):
            m = x.mean(-1, keepdims=True)
            v = ((x - m) ** 2).mean(-1, keepdims=True)
            return (x - m) / jnp.sqrt(v + EPS) * g + b
        key = jax.random.key(seed)
        ks = jax.random.split(key, 8)
        B, S, D, E, H = (8, 128, 128, 8, 512)
        x = jax.random.normal(ks[0], (B, S, D), dtype=jnp.float32)
        Wg = jax.random.normal(ks[1], (D, E), dtype=jnp.float32) * 0.02
        W1 = jax.random.normal(ks[2], (E, D, H), dtype=jnp.float32) * 0.02
        b1 = jnp.zeros((E, H), dtype=jnp.float32)
        W2 = jax.random.normal(ks[3], (E, H, D), dtype=jnp.float32) * 0.02
        b2 = jnp.zeros((E, D), dtype=jnp.float32)
        ln_g = jnp.ones((D,), dtype=jnp.float32)
        ln_b = jnp.zeros((D,), dtype=jnp.float32)
        out_g = jnp.ones((D,), dtype=jnp.float32)
        out_b = jnp.zeros((D,), dtype=jnp.float32)
        return {'x': x, 'Wg': Wg, 'W1': W1, 'b1': b1, 'W2': W2, 'b2': b2, 'ln_g': ln_g, 'ln_b': ln_b, 'out_g': out_g, 'out_b': out_b}
    _L3_ffn_all = _L3_ffn_setup()
    _L3_ffn_in = {k: v for k, v in _L3_ffn_all.items() if k in ('Wg', 'W1', 'b1', 'W2', 'b2', 'ln_g', 'ln_b', 'out_g', 'out_b')}
    del _L3_ffn_all
    return {'x': x, 'L0_tok_W': _L0_tok_in['W'], 'L0_tok_b': _L0_tok_in['b'], 'L0_tok_gamma': _L0_tok_in['gamma'], 'L0_tok_beta': _L0_tok_in['beta'], 'L0_attn_W_qkv': _L0_attn_in['W_qkv'], 'L0_attn_gn_qkv_scale': _L0_attn_in['gn_qkv_scale'], 'L0_attn_gn_qkv_bias': _L0_attn_in['gn_qkv_bias'], 'L0_attn_rel_emb': _L0_attn_in['rel_emb'], 'L0_attn_gn_out_scale': _L0_attn_in['gn_out_scale'], 'L0_attn_gn_out_bias': _L0_attn_in['gn_out_bias'], 'L0_ffn_rc_w1': _L0_ffn_in['rc_w1'], 'L0_ffn_rc_b1': _L0_ffn_in['rc_b1'], 'L0_ffn_rc_w2': _L0_ffn_in['rc_w2'], 'L0_ffn_rc_b2': _L0_ffn_in['rc_b2'], 'L0_ffn_sh_w1': _L0_ffn_in['sh_w1'], 'L0_ffn_sh_b1': _L0_ffn_in['sh_b1'], 'L0_ffn_sh_w2': _L0_ffn_in['sh_w2'], 'L0_ffn_sh_b2': _L0_ffn_in['sh_b2'], 'L0_ffn_e_w1': _L0_ffn_in['e_w1'], 'L0_ffn_e_b1': _L0_ffn_in['e_b1'], 'L0_ffn_e_w2': _L0_ffn_in['e_w2'], 'L0_ffn_e_b2': _L0_ffn_in['e_b2'], 'L0_ffn_ln_g': _L0_ffn_in['ln_g'], 'L0_ffn_ln_b': _L0_ffn_in['ln_b'], 'L1_attn_Wq': _L1_attn_in['Wq'], 'L1_attn_bq': _L1_attn_in['bq'], 'L1_attn_Wk': _L1_attn_in['Wk'], 'L1_attn_bk': _L1_attn_in['bk'], 'L1_ffn_attn_w': _L1_ffn_in['attn_w'], 'L1_ffn_attn_b': _L1_ffn_in['attn_b'], 'L1_ffn_gate_w': _L1_ffn_in['gate_w'], 'L1_ffn_gate_b': _L1_ffn_in['gate_b'], 'L1_ffn_w1': _L1_ffn_in['w1'], 'L1_ffn_b1': _L1_ffn_in['b1'], 'L1_ffn_w2': _L1_ffn_in['w2'], 'L1_ffn_b2': _L1_ffn_in['b2'], 'L2_attn_W1': _L2_attn_in['W1'], 'L2_attn_W2': _L2_attn_in['W2'], 'L2_ffn_router_w': _L2_ffn_in['router_w'], 'L2_ffn_router_b': _L2_ffn_in['router_b'], 'L2_ffn_Wi': _L2_ffn_in['Wi'], 'L2_ffn_Wh': _L2_ffn_in['Wh'], 'L2_ffn_b': _L2_ffn_in['b'], 'L2_ffn_Wo': _L2_ffn_in['Wo'], 'L2_ffn_bo': _L2_ffn_in['bo'], 'L3_attn_Wl': _L3_attn_in['Wl'], 'L3_attn_bl': _L3_attn_in['bl'], 'L3_attn_Wq': _L3_attn_in['Wq'], 'L3_attn_Wk': _L3_attn_in['Wk'], 'L3_attn_Wv': _L3_attn_in['Wv'], 'L3_attn_Wo': _L3_attn_in['Wo'], 'L3_attn_bo': _L3_attn_in['bo'], 'L3_ffn_Wg': _L3_ffn_in['Wg'], 'L3_ffn_W1': _L3_ffn_in['W1'], 'L3_ffn_b1': _L3_ffn_in['b1'], 'L3_ffn_W2': _L3_ffn_in['W2'], 'L3_ffn_b2': _L3_ffn_in['b2'], 'L3_ffn_ln_g': _L3_ffn_in['ln_g'], 'L3_ffn_ln_b': _L3_ffn_in['ln_b'], 'L3_ffn_out_g': _L3_ffn_in['out_g'], 'L3_ffn_out_b': _L3_ffn_in['out_b']}

def reference(x, L0_tok_W, L0_tok_b, L0_tok_gamma, L0_tok_beta, L0_attn_W_qkv, L0_attn_gn_qkv_scale, L0_attn_gn_qkv_bias, L0_attn_rel_emb, L0_attn_gn_out_scale, L0_attn_gn_out_bias, L0_ffn_rc_w1, L0_ffn_rc_b1, L0_ffn_rc_w2, L0_ffn_rc_b2, L0_ffn_sh_w1, L0_ffn_sh_b1, L0_ffn_sh_w2, L0_ffn_sh_b2, L0_ffn_e_w1, L0_ffn_e_b1, L0_ffn_e_w2, L0_ffn_e_b2, L0_ffn_ln_g, L0_ffn_ln_b, L1_attn_Wq, L1_attn_bq, L1_attn_Wk, L1_attn_bk, L1_ffn_attn_w, L1_ffn_attn_b, L1_ffn_gate_w, L1_ffn_gate_b, L1_ffn_w1, L1_ffn_b1, L1_ffn_w2, L1_ffn_b2, L2_attn_W1, L2_attn_W2, L2_ffn_router_w, L2_ffn_router_b, L2_ffn_Wi, L2_ffn_Wh, L2_ffn_b, L2_ffn_Wo, L2_ffn_bo, L3_attn_Wl, L3_attn_bl, L3_attn_Wq, L3_attn_Wk, L3_attn_Wv, L3_attn_Wo, L3_attn_bo, L3_ffn_Wg, L3_ffn_W1, L3_ffn_b1, L3_ffn_W2, L3_ffn_b2, L3_ffn_ln_g, L3_ffn_ln_b, L3_ffn_out_g, L3_ffn_out_b):
    import jax
    import jax.numpy as jnp

    def _L0_tok_ref(x, W, b, gamma, beta):
        import jax, jax.numpy as jnp
        import numpy as np
        CONTEXT = 5
        DILATION = 1
        BN_EPS = 1e-05
        B, S, D = x.shape
        L = S - (CONTEXT - 1) * DILATION
        windows = jnp.stack([x[:, c * DILATION:c * DILATION + L, :] for c in range(CONTEXT)], axis=2).reshape(B, L, CONTEXT * D)
        y = jnp.einsum('blk,ok->blo', windows, W) + b
        y = jax.nn.relu(y)
        mean = jnp.mean(y, axis=(0, 1))
        var = jnp.mean((y - mean) ** 2, axis=(0, 1))
        y = (y - mean) * jax.lax.rsqrt(var + BN_EPS) * gamma + beta
        return y

    def _L0_attn_ref(x, W_qkv, gn_qkv_scale, gn_qkv_bias, rel_emb, gn_out_scale, gn_out_bias):
        import jax, jax.numpy as jnp
        import numpy as np
        NUM_HEADS = 8
        NUM_GROUPS = 32
        EPS = 0.0001

        def group_norm(x, scale, bias):
            b, l, c = x.shape
            xg = x.reshape(b, l, NUM_GROUPS, c // NUM_GROUPS)
            mean = jnp.mean(xg, axis=(1, 3), keepdims=True)
            var = jnp.var(xg, axis=(1, 3), keepdims=True)
            xg = (xg - mean) * jax.lax.rsqrt(var + EPS)
            return xg.reshape(b, l, c) * scale + bias
        bs, L, C = x.shape
        hf = C // NUM_HEADS
        qkv = x @ W_qkv
        qkv = group_norm(qkv, gn_qkv_scale, gn_qkv_bias)
        qkv = qkv.reshape(bs, L, NUM_HEADS, hf * 2).transpose((0, 2, 3, 1))
        q = qkv[:, :, :hf // 2]
        k = qkv[:, :, hf // 2:hf]
        v = qkv[:, :, hf:]
        rel_idx = jnp.arange(L)[:, None] - jnp.arange(L)[None, :] + (L - 1)
        rpe = rel_emb[:, rel_idx]
        rpe_q = rpe[:hf // 2]
        rpe_k = rpe[hf // 2:hf]
        rpe_v = rpe[hf:]
        logits = jnp.einsum('bhdi,bhdj->bhij', q, k) + jnp.einsum('bhdi,dij->bhij', q, rpe_k) + jnp.einsum('bhdi,dij->bhij', k, rpe_q)
        attn = jax.nn.softmax(logits, axis=3).astype(jnp.float32)
        wv = jnp.einsum('bhij,bhdj->bhdi', attn, v)
        wve = jnp.einsum('bhij,dij->bhdi', attn, rpe_v)
        out = (wv + wve).transpose((0, 3, 1, 2)).reshape(bs, L, C)
        return group_norm(out, gn_out_scale, gn_out_bias)

    def _L0_ffn_ref(x, rc_w1, rc_b1, rc_w2, rc_b2, sh_w1, sh_b1, sh_w2, sh_b2, e_w1, e_b1, e_w2, e_b2, ln_g, ln_b):
        import jax, jax.numpy as jnp
        import numpy as np
        D_IN, D_HID, E, K = (128, 512, 10, 2)
        KS = (9, 1)

        def conv1d_same(x, w, b):
            y = jax.lax.conv_general_dilated(x, w, window_strides=(1,), padding='SAME', dimension_numbers=('NCH', 'OIH', 'NCH'))
            return y + b[None, :, None]
        B, T, d = x.shape
        residual = x
        xt = jnp.transpose(x, (0, 2, 1))
        rc = conv1d_same(xt, rc_w1, rc_b1)
        rc = jax.nn.gelu(rc, approximate=False)
        rc = conv1d_same(rc, rc_w2, rc_b2)
        logits = jnp.transpose(rc, (0, 2, 1)).reshape(-1, E)
        vals, idx = jax.lax.top_k(logits, K)
        gv = jax.nn.softmax(vals, axis=-1)
        N = logits.shape[0]
        gates = jnp.zeros((N, E), x.dtype).at[jnp.arange(N)[:, None], idx].set(gv)
        x2 = x.reshape(-1, d)
        h = jnp.einsum('nd,edh->enh', x2, e_w1) + e_b1[:, None, :]
        h = jax.nn.elu(h)
        eo = jnp.einsum('enh,ehd->end', h, e_w2) + e_b2[:, None, :]
        y = jnp.einsum('end,ne->nd', eo, gates).reshape(B, T, d)
        sh = conv1d_same(xt, sh_w1, sh_b1)
        sh = jax.nn.silu(sh)
        sh = conv1d_same(sh, sh_w2, sh_b2)
        sh = jnp.transpose(sh, (0, 2, 1))
        z = residual + y + sh
        mu = jnp.mean(z, axis=-1, keepdims=True)
        var = jnp.mean(jnp.square(z - mu), axis=-1, keepdims=True)
        return (z - mu) * jax.lax.rsqrt(var + 1e-05) * ln_g + ln_b

    def _L1_attn_ref(x, Wq, bq, Wk, bk):
        import jax, jax.numpy as jnp
        import numpy as np
        EMBED_DIM = 128
        scaling = jnp.float32(EMBED_DIM ** (-0.5))
        q = (x @ Wq + bq) * scaling
        k = x @ Wk + bk
        scores = jnp.einsum('bqe,bke->bqk', q, k)
        attn = jax.nn.softmax(scores, axis=-1)
        return jnp.einsum('bqk,bke->bqe', attn, x)

    def _L1_ffn_ref(x, attn_w, attn_b, gate_w, gate_b, w1, b1, w2, b2):
        import jax, jax.numpy as jnp
        import numpy as np
        B, S, D = (32, 128, 128)
        E, H, O, K = (8, 512, 128, 2)
        scores = x @ attn_w + attn_b
        aw = jax.nn.softmax(scores, axis=1)
        pooled = jnp.sum(x * aw, axis=1)
        gates = jax.nn.softmax(pooled @ gate_w + gate_b, axis=-1)
        _, idx = jax.lax.top_k(gates, K)
        mask = jnp.sum(jax.nn.one_hot(idx, E, dtype=gates.dtype), axis=-2)
        g = gates * mask
        g = g / (jnp.sum(g, axis=-1, keepdims=True) + 1e-09)
        h = jax.nn.gelu(jnp.einsum('bsd,edh->ebsh', x, w1) + b1[:, None, None, :], approximate=False)
        eo = jax.nn.gelu(jnp.einsum('ebsh,eho->ebso', h, w2) + b2[:, None, None, :], approximate=False)
        return jnp.einsum('ebso,be->bso', eo, g)

    def _L2_attn_ref(x, W1, W2):
        import jax, jax.numpy as jnp
        import numpy as np
        SQRT_DK = np.sqrt(512.0).astype(np.float32)
        B, A, D = x.shape
        left = jnp.einsum('bad,dr->bar', x, W1)
        right = jnp.einsum('rd,bcd->brc', W2, x)
        scores = jnp.einsum('bar,brc->bac', left, right)
        attn = jax.nn.softmax(scores / SQRT_DK, axis=-1)
        out = jnp.einsum('bac,bcd->bad', attn, x)
        return out

    def _L2_ffn_ref(x, router_w, router_b, Wi, Wh, b, Wo, bo):
        import jax, jax.numpy as jnp
        import numpy as np
        S, B, I, O, H, E, K = (128, 32, 128, 128, 128, 8, 2)

        def _expert(x_seq, Wi, Wh, b, Wo, bo):
            Bsz = x_seq.shape[1]
            Hd = Wh.shape[0]

            def step(carry, xt):
                h, c = carry
                gates = xt @ Wi + h @ Wh + b
                i_, f_, g_, o_ = jnp.split(gates, 4, axis=-1)
                c = jax.nn.sigmoid(f_) * c + jax.nn.sigmoid(i_) * jnp.tanh(g_)
                h = jax.nn.sigmoid(o_) * jnp.tanh(c)
                return ((h, c), h @ Wo + bo)
            init = (jnp.zeros((Bsz, Hd), x_seq.dtype), jnp.zeros((Bsz, Hd), x_seq.dtype))
            _, ys = jax.lax.scan(step, init, x_seq)
            return ys
        S_, B_, I_ = x.shape
        N = S_ * B_
        flat_x = x.reshape(N, I_)
        logits = flat_x @ router_w + router_b
        top_vals, top_idx = jax.lax.top_k(logits, K)
        rw = jax.nn.softmax(top_vals, axis=1)
        mask = (top_idx.T[:, None, :] == jnp.arange(E)[None, :, None]).astype(x.dtype)
        expert_x = (mask[..., None] * flat_x[None, None]).reshape(K, E, S_, B_, I_)
        run_e = jax.vmap(_expert, in_axes=(0, 0, 0, 0, 0, 0))
        run_ke = jax.vmap(run_e, in_axes=(0, None, None, None, None, None))
        out = run_ke(expert_x, Wi, Wh, b, Wo, bo)
        out = out.reshape(K, E, N, -1)
        y = jnp.einsum('ken,nk,keno->no', mask, rw, out)
        return y.reshape(S_, B_, -1)

    def _L3_attn_ref(x, Wl, bl, Wq, Wk, Wv, Wo, bo):
        import jax, jax.numpy as jnp
        import numpy as np
        B, S, IN, HD, H = (2, 512, 128, 32, 16)
        b, s, _ = x.shape
        h, _, hd = Wq.shape
        xh = jnp.einsum('bsi,hoi->bhso', x, Wl) + bl[None, :, None, :]
        Q = jnp.einsum('bhsi,hid->bhsd', xh, Wq)
        K = jnp.einsum('bhsi,hid->bhsd', xh, Wk)
        V = jnp.einsum('bhsi,hid->bhsd', xh, Wv)
        scores = jnp.einsum('bhsd,bhtd->bhst', Q, K)
        causal = jnp.triu(jnp.ones((s, s), dtype=bool), k=1)
        scores = jnp.where(causal[None, None], -jnp.inf, scores)
        A = jax.nn.softmax(scores, axis=-1)
        F = jnp.einsum('bhst,bhtd->bhsd', A, V)
        cat = jnp.transpose(F, (0, 2, 1, 3)).reshape(b, s, h * hd)
        return cat @ Wo.T + bo

    def _L3_ffn_ref(x, Wg, W1, b1, W2, b2, ln_g, ln_b, out_g, out_b):
        import jax, jax.numpy as jnp
        import numpy as np
        EPS = 1e-05
        TOP_K = 2

        def layer_norm(x, g, b):
            m = x.mean(-1, keepdims=True)
            v = ((x - m) ** 2).mean(-1, keepdims=True)
            return (x - m) / jnp.sqrt(v + EPS) * g + b
        xn = layer_norm(x, ln_g, ln_b)
        logits = jnp.einsum('bsd,de->bse', xn, Wg)
        probs = jax.nn.softmax(logits, axis=-1)
        top_p, top_i = jax.lax.top_k(probs, TOP_K)
        conf = top_p / top_p.sum(-1, keepdims=True)
        h = jax.nn.gelu(jnp.einsum('bsd,edh->bseh', xn, W1) + b1)
        o = jnp.einsum('bseh,ehd->bsed', h, W2) + b2
        sel = jnp.take_along_axis(o, top_i[..., None], axis=2)
        combined = jnp.einsum('bskd,bsk->bsd', sel, conf)
        return layer_norm(x + combined, out_g, out_b)
    h = _L0_tok_ref(x, L0_tok_W, L0_tok_b, L0_tok_gamma, L0_tok_beta)
    h = h + _L0_attn_ref(_layernorm(h, axis=-1), L0_attn_W_qkv, L0_attn_gn_qkv_scale, L0_attn_gn_qkv_bias, L0_attn_rel_emb, L0_attn_gn_out_scale, L0_attn_gn_out_bias)
    h = h + _L0_ffn_ref(_layernorm(h, axis=-1), L0_ffn_rc_w1, L0_ffn_rc_b1, L0_ffn_rc_w2, L0_ffn_rc_b2, L0_ffn_sh_w1, L0_ffn_sh_b1, L0_ffn_sh_w2, L0_ffn_sh_b2, L0_ffn_e_w1, L0_ffn_e_b1, L0_ffn_e_w2, L0_ffn_e_b2, L0_ffn_ln_g, L0_ffn_ln_b)
    h = h + _L1_attn_ref(_layernorm(h, axis=-1), L1_attn_Wq, L1_attn_bq, L1_attn_Wk, L1_attn_bk)
    h = h + _L1_ffn_ref(_layernorm(h, axis=-1), L1_ffn_attn_w, L1_ffn_attn_b, L1_ffn_gate_w, L1_ffn_gate_b, L1_ffn_w1, L1_ffn_b1, L1_ffn_w2, L1_ffn_b2)
    h = h + _L2_attn_ref(_layernorm(h, axis=-1), L2_attn_W1, L2_attn_W2)
    h = h + _L2_ffn_ref(_layernorm(h, axis=-1), L2_ffn_router_w, L2_ffn_router_b, L2_ffn_Wi, L2_ffn_Wh, L2_ffn_b, L2_ffn_Wo, L2_ffn_bo)
    h = h + _L3_attn_ref(_layernorm(h, axis=-1), L3_attn_Wl, L3_attn_bl, L3_attn_Wq, L3_attn_Wk, L3_attn_Wv, L3_attn_Wo, L3_attn_bo)
    h = h + _L3_ffn_ref(_layernorm(h, axis=-1), L3_ffn_Wg, L3_ffn_W1, L3_ffn_b1, L3_ffn_W2, L3_ffn_b2, L3_ffn_ln_g, L3_ffn_ln_b, L3_ffn_out_g, L3_ffn_out_b)
    return h

_drawn_inputs = setup_inputs


def setup_inputs(seed=0):
    import zlib

    import numpy as np

    out = dict(_drawn_inputs(seed))
    spreads = {'L0_tok_gamma': (1.0, 0.2),
     'L0_tok_beta': (0.0, 0.1),
     'L0_attn_gn_qkv_scale': (1.0, 0.2),
     'L0_attn_gn_qkv_bias': (0.0, 0.1),
     'L0_attn_gn_out_scale': (1.0, 0.2),
     'L0_attn_gn_out_bias': (0.0, 0.1),
     'L0_ffn_rc_b1': (0.0, 0.372),
     'L0_ffn_rc_b2': (0.0, 0.1),
     'L0_ffn_sh_b1': (0.0, 0.359),
     'L0_ffn_sh_b2': (0.0, 0.1),
     'L0_ffn_e_b1': (0.0, 0.411),
     'L0_ffn_e_b2': (0.0, 0.1),
     'L0_ffn_ln_g': (1.0, 0.2),
     'L0_ffn_ln_b': (0.0, 0.1),
     'L1_attn_bq': (0.0, 0.8),
     'L1_attn_bk': (0.0, 2.0),
     'L1_ffn_gate_b': (0.0, 0.395),
     'L1_ffn_b1': (0.0, 0.8),
     'L1_ffn_b2': (0.0, 0.415),
     'L2_ffn_router_b': (0.0, 0.502),
     'L2_ffn_b': (0.0, 0.8),
     'L2_ffn_bo': (0.0, 0.299),
     'L3_ffn_b1': (0.0, 0.8),
     'L3_ffn_b2': (0.0, 2.0),
     'L3_ffn_ln_g': (1.0, 0.6),
     'L3_ffn_ln_b': (0.0, 0.8),
     'L3_ffn_out_g': (1.0, 0.6),
     'L3_ffn_out_b': (0.0, 0.946)}
    factors = {'L1_ffn_attn_w': 6.02,
     'L1_ffn_gate_w': 2.97,
     'L1_ffn_w1': 7.001,
     'L1_ffn_w2': 6.253,
     'L2_attn_W1': 8.0,
     'L2_attn_W2': 8.0,
     'L2_ffn_Wi': 8.0,
     'L2_ffn_Wh': 8.0,
     'L2_ffn_Wo': 8.0,
     'L3_attn_Wl': 8.0,
     'L3_attn_bl': 8.0,
     'L3_attn_Wq': 8.0,
     'L3_attn_Wk': 8.0,
     'L3_attn_Wv': 8.0,
     'L3_attn_Wo': 8.0,
     'L3_attn_bo': 29.244,
     'L3_ffn_Wg': 2.744,
     'L3_ffn_W1': 5.218,
     'L3_ffn_W2': 4.848}
    for name, (base, spread) in spreads.items():
        noise = np.random.default_rng([zlib.crc32(name.encode()), seed]).standard_normal(out[name].shape)
        drawn = base * np.exp(spread * noise) if base else spread * noise
        out[name] = jnp.asarray(drawn.astype(out[name].dtype))
    for name, factor in factors.items():
        out[name] = (out[name] * factor).astype(out[name].dtype)
    return out
```

```python
from contextlib import ExitStack

import numpy as np

import concourse.bass as bass
from concourse import mybir

ALU = mybir.AluOpType
ACT = mybir.ActivationFunctionType
AX = mybir.AxisListType
F32 = mybir.dt.float32
BF16 = mybir.dt.bfloat16
U32 = mybir.dt.uint32

P = 128
B = 4
S_IN = 750
CONTEXT = 5
L = S_IN - CONTEXT + 1
HALF = L // 2
CHUNKS = [(b, half) for b in range(B) for half in range(2)]
TILES = -(-L // P)
LP = TILES * P
LEAD = 8
ZW = LEAD + B * LP
BANK = 512



class Chain:

    def __init__(self, eng, sem, turn=0, per_turn=0):
        self.eng, self.sem, self.base, self.per_turn, self.n = eng, sem, turn * per_turn, per_turn, 0

    def link(self, ins):
        self.n += 1
        ins.then_inc(self.sem, 1)
        self.eng.wait_ge(self.sem, self.base + self.n)

    def end(self):
        assert self.n == self.per_turn, (self.n, self.per_turn)


def apart(eng, passed):
    eng.sem_inc(passed, 1)


class Alloc:

    def __init__(self, nc, ctx, stage):
        self.nc, self.ctx, self.stage = nc, ctx, stage
        self.used = []
        ctx.callback(self.clear)

    def clear(self):
        if self.used:
            numbers = sorted(s.num for s in self.used)
            first = numbers[0]
            for n, after in zip(numbers, numbers[1:] + [None]):
                if after != n + 1:
                    self.nc.gpsimd.sem_clear(range(first, n + 1))
                    first = after
            self.nc.all_engine_barrier()

    def sb(self, name, shape, dt=F32):
        return self.ctx.enter_context(self.nc.sbuf_tensor(f"{self.stage}_{name}", shape, dt))

    def ps(self, name, shape, dt=F32):
        return self.ctx.enter_context(self.nc.psum_tensor(f"{self.stage}_{name}", shape, dt))

    def sem(self, name):
        self.used.append(self.ctx.enter_context(self.nc.semaphore(f"{self.stage}_{name}")))
        return self.used[-1]

    def sems(self, name, n):
        return [self.sem(f"{name}{i}") for i in range(n)]


def h_chunk(hT, b, half):
    return hT[:, bass.ds(b * L + half * HALF, HALF)]


def z_chunk(zT, b, half, shift=0):
    return zT[:, bass.ds(b * LP + (half * HALF + LEAD + shift), HALF)]


def load_constants(nc, io, K):
    with ExitStack() as ctx:
        a = Alloc(nc, ctx, "const")
        loaded = a.sem("loaded")
        filled = a.sem("filled")
        block = ctx.enter_context(nc.Block())

        @block.sync
        def _(sp):
            sp.dma_start(K["ident"][:], io["ident"]).then_inc(loaded, 16)
            sp.dma_start(K["mean_all"][:], io["mean_all"]).then_inc(loaded, 16)
            sp.wait_ge(loaded, 32)

        @block.vector
        def _(dve):
            nc.vector.memset(K["zT"][:], 0.0).then_inc(filled, 1)
            nc.vector.memset(K["eps5"][:], 1e-5).then_inc(filled, 1)
            nc.vector.memset(K["eps4"][:], 1e-4).then_inc(filled, 1)
            dve.wait_ge(filled, 3)


def token_conv(nc, io, K):
    hT = K["hT"]
    with ExitStack() as ctx:
        a = Alloc(nc, ctx, "tok")
        x = a.sb("x", [P, B * S_IN])
        w = a.sb("w", [P, CONTEXT, P])
        cols = a.sb("cols", [P, 3])
        stats = a.sb("stats", [P, 2 * B * 6])
        mv = a.sb("mv", [P, 2])
        s = a.sb("s", [P, 4])
        acc = [a.ps(f"acc{i}", [P, BANK]) for i in range(2)]
        x_in, w_in = a.sem("x_in"), a.sem("w_in")
        conv_done, acc_used, y_done, var_done, sd_done, chain = (a.sem(n) for n in (
            "conv_done", "acc_used", "y_done", "var_done", "sd_done", "chain"))
        block = ctx.enter_context(nc.Block())

        @block.sync
        def _(sp):
            sp.dma_start(w[:], io["tok_w"]).then_inc(w_in, 16)
            sp.dma_start(cols[:], io["tok_cols"]).then_inc(w_in, 16)
            sp.dma_start(x[:], io["x"]).then_inc(x_in, 16)

        @block.tensor
        def _(pe):
            pe.wait_ge(w_in, 32)
            pe.wait_ge(x_in, 16)
            with pe.Fori(0, B) as b:
                for half in range(2):
                    pe.wait_ge(acc_used, b * 2 + half + 1)
                    for c in range(CONTEXT):
                        mm = nc.tensor.matmul(acc[half][:, 0:HALF], w[:, c, :],
                                              x[:, bass.ds(b * S_IN + (half * HALF + c), HALF)],
                                              start=(c == 0), stop=(c == CONTEXT - 1))
                    mm.then_inc(conv_done, 1)

        @block.scalar
        def _(act):
            act.sem_inc(acc_used, 2)
            act.wait_ge(w_in, 32)
            with act.Fori(0, B) as b:
                for half in range(2):
                    act.wait_ge(conv_done, b * 2 + half + 1)
                    nc.scalar.activation(h_chunk(hT, b, half), acc[half][:, 0:HALF], ACT.Relu,
                                         bias=cols[:, 0:1]).then_inc(acc_used, 1)
            act.wait_ge(var_done, 1)
            nc.scalar.activation(s[:, 0:1], mv[:, 1:2], ACT.Sqrt, bias=K["eps5"][:, 0:1]).then_inc(sd_done, 1)

        @block.vector
        def _(dve):
            with dve.Fori(0, B) as b:
                for half in range(2):
                    dve.wait_ge(acc_used, b * 2 + half + 3)
                    nc.vector.bn_stats(stats[:, bass.ds(b * 12 + half * 6, 6)],
                                       h_chunk(hT, b, half)).then_inc(y_done, 1)
            dve.wait_ge(y_done, 2 * B)
            nc.vector.bn_aggr(mv[:], stats[:]).then_inc(var_done, 1)
            dve.wait_ge(var_done, 1)
            dve.wait_ge(sd_done, 1)
            c = Chain(dve, chain)
            c.link(nc.vector.reciprocal(s[:, 1:2], s[:, 0:1]))
            c.link(nc.vector.tensor_tensor(s[:, 2:3], s[:, 1:2], cols[:, 1:2], ALU.mult))
            c.link(nc.vector.tensor_tensor(s[:, 3:4], s[:, 2:3], mv[:, 0:1], ALU.mult))
            c.link(nc.vector.tensor_tensor(s[:, 3:4], cols[:, 2:3], s[:, 3:4], ALU.subtract))
            c.link(nc.vector.tensor_scalar(hT[:], hT[:], s[:, 2:3], s[:, 3:4], ALU.mult, ALU.add))


def layer_norm(nc, K, name, src="hT", affine=None, affine_d=None, add=False):
    hT, zT = K["hT"], K["zT"]

    def x_chunk(b, i):
        return z_chunk(zT, b, i) if src == "zT" else h_chunk(hT if src == "hT" else src, b, i)

    with ExitStack() as ctx:
        a = Alloc(nc, ctx, name)
        d = [a.sb(f"d{i}", [P, HALF]) for i in range(2)]
        sq = [a.sb(f"sq{i}", [P, HALF]) for i in range(2)]
        sd = [a.sb(f"sd{i}", [P, HALF]) for i in range(2)]
        mean = [a.ps(f"mean{i}", [P, BANK]) for i in range(2)]
        var = [a.ps(f"var{i}", [P, BANK]) for i in range(2)]
        mean_ready, d_ready, sq_ready, var_ready, sd_ready, out_ready, chain, cols_in = (a.sem(n) for n in (
            "mean_ready", "d_ready", "sq_ready", "var_ready", "sd_ready", "out_ready", "chain", "cols_in"))
        block = ctx.enter_context(nc.Block())

        @block.sync
        def _(sp):
            if affine is not None:
                sp.dma_start(affine[:], affine_d).then_inc(cols_in, 16)

        @block.tensor
        def _(pe):
            with pe.Fori(0, B) as b:
                for i in range(2):
                    pe.wait_ge(out_ready, b * 2 + 1 + i)
                    nc.tensor.matmul(mean[i][:, 0:HALF], K["mean_all"][:], x_chunk(b, i),
                                     start=True, stop=True).then_inc(mean_ready, 1)
                for i in range(2):
                    pe.wait_ge(sq_ready, b * 2 + i + 1)
                    nc.tensor.matmul(var[i][:, 0:HALF], K["mean_all"][:], sq[i][:],
                                     start=True, stop=True).then_inc(var_ready, 1)

        @block.scalar
        def _(act):
            with act.Fori(0, B) as b:
                for i in range(2):
                    act.wait_ge(d_ready, b * 2 + i + 1)
                    nc.scalar.activation(sq[i][:], d[i][:], ACT.Square).then_inc(sq_ready, 1)
                for i in range(2):
                    act.wait_ge(var_ready, b * 2 + i + 1)
                    nc.scalar.activation(sd[i][:], var[i][:, 0:HALF], ACT.Sqrt,
                                         bias=K["eps5"][:, 0:1]).then_inc(sd_ready, 1)

        @block.vector
        def _(dve):
            dve.sem_inc(out_ready, 2)
            if affine is not None:
                dve.wait_ge(cols_in, 16)
            with dve.Fori(0, B) as b:
                c = Chain(dve, chain, b, 2 * (1 + (affine is not None) + add))
                for i in range(2):
                    dve.wait_ge(mean_ready, b * 2 + i + 1)
                    nc.vector.tensor_tensor(d[i][:], x_chunk(b, i), mean[i][:, 0:HALF],
                                            ALU.subtract).then_inc(d_ready, 1)
                for i in range(2):
                    dve.wait_ge(sd_ready, b * 2 + i + 1)
                    c.link(nc.vector.reciprocal(sd[i][:], sd[i][:]))
                    if affine is None:
                        nc.vector.tensor_tensor(z_chunk(zT, b, i), d[i][:], sd[i][:],
                                                ALU.mult).then_inc(out_ready, 1)
                        continue
                    c.link(nc.vector.tensor_tensor(d[i][:], d[i][:], sd[i][:], ALU.mult))
                    out = d[i][:] if add else z_chunk(zT, b, i)
                    scaled = nc.vector.tensor_scalar(out, d[i][:], affine[:, 0:1], affine[:, 1:2], ALU.mult, ALU.add)
                    if add:
                        c.link(scaled)
                        scaled = nc.vector.tensor_tensor(h_chunk(hT, b, i), h_chunk(hT, b, i), d[i][:], ALU.add)
                    scaled.then_inc(out_ready, 1)
                c.end()


STAGES = {}


def audio_tower(nc, io, out, scratch):
    with ExitStack() as ctx:
        a = Alloc(nc, ctx, "tower")
        K = {
            "ident": a.sb("ident", [P, P]),
            "mean_all": a.sb("mean_all", [P, P]),
            "hT": a.sb("hT", [P, B * L]),
            "zT": a.sb("zT", [P, ZW]),
            "eps5": a.sb("eps5", [P, 1]),
            "eps4": a.sb("eps4", [P, 1]),
        }
        K["iota_d"] = io["iota"]
        load_constants(nc, io, K)
        for n in range(len(STAGES)):
            if n > 0:
                layer_norm(nc, K, f"ln{n}")
            STAGES[n](nc, io, K, scratch)
        written = a.sem("written")
        block = ctx.enter_context(nc.Block())

        @block.sync
        def _(sp):
            sp.dma_start(out, K["hT"][:]).then_inc(written, 16)
            sp.wait_ge(written, 16)


STAGES[0] = lambda nc, io, K, scratch: token_conv(nc, io, K)


HEADS0 = 8
HD = P // HEADS0
QD = HD // 2
PAIRS = B * HEADS0
REL_L = 256
REL = 2 * REL_L - 2
FAR = L - 1 - REL
SKEW_TILES = REL // P + 1
SKEW_W = [REL - P * t for t in range(SKEW_TILES)]
SKEW_PAD = [-(-w // P) * P for w in SKEW_W]
SKEW_ROW = BANK + P
LEFT_PART = (0, 0, 1, 1, 0, 2)
RIGHT_PART = (0, 1, 0, 1, 2, 0)
NPART = len(LEFT_PART)


def split3(nc, c, parts, src, rest, done):
    c.link(nc.vector.tensor_copy(parts[0], src))
    c.link(nc.vector.tensor_tensor(rest, src, parts[0], ALU.subtract))
    c.link(nc.vector.tensor_copy(parts[1], rest))
    c.link(nc.vector.tensor_tensor(rest, rest, parts[1], ALU.subtract))
    nc.vector.tensor_copy(parts[2], rest).then_inc(done, 1)


class GroupNorm:

    def __init__(self, a, name, avg, cols, g_ps, eps):
        self.avg, self.cols, self.g_ps, self.eps = avg, cols, g_ps, eps
        self.passed = a.sem(f"{name}_passed")
        self.stats = a.sb(f"{name}_stats", [P, 12])
        self.work = a.sb(f"{name}_work", [P, 8])
        self.mean_in, self.g_mean, self.spread_in, self.g_var, self.sd_done, self.affine_ready = (
            a.sem(f"{name}_{s}") for s in ("mean_in", "g_mean", "spread_in", "g_var", "sd_done", "affine_ready"))

    LINKS = 6

    def dve(self, nc, dve, c, x, n):
        w, g = self.work, self.g_ps
        c.link(nc.vector.bn_stats(self.stats[:, 0:6], x[:, 0:HALF]))
        c.link(nc.vector.bn_stats(self.stats[:, 6:12], x[:, HALF:L]))
        apart(dve, self.passed)
        nc.vector.bn_aggr(w[:, 0:2], self.stats[:]).then_inc(self.mean_in, 1)
        dve.wait_ge(self.mean_in, n + 1)
        dve.wait_ge(self.g_mean, n + 1)
        c.link(nc.vector.tensor_tensor(w[:, 2:3], w[:, 0:1], g[:, 0:1], ALU.subtract))
        nc.vector.scalar_tensor_tensor(out=w[:, 3:4], in0=w[:, 2:3], scalar=w[:, 2:3], in1=w[:, 1:2],
                                       op0=ALU.mult, op1=ALU.add).then_inc(self.spread_in, 1)
        dve.wait_ge(self.sd_done, n + 1)
        c.link(nc.vector.reciprocal(w[:, 5:6], w[:, 4:5]))
        c.link(nc.vector.tensor_tensor(w[:, 6:7], w[:, 5:6], self.cols[:, 0:1], ALU.mult))
        c.link(nc.vector.tensor_tensor(w[:, 7:8], w[:, 6:7], g[:, 0:1], ALU.mult))
        nc.vector.tensor_tensor(w[:, 7:8], self.cols[:, 1:2], w[:, 7:8], ALU.subtract).then_inc(self.affine_ready, 1)

    def pe(self, nc, pe, n):
        pe.wait_ge(self.mean_in, n + 1)
        nc.tensor.matmul(self.g_ps[:, 0:1], self.avg, self.work[:, 0:1], start=True, stop=True).then_inc(self.g_mean, 1)
        pe.wait_ge(self.spread_in, n + 1)
        nc.tensor.matmul(self.g_ps[:, 1:2], self.avg, self.work[:, 3:4], start=True, stop=True).then_inc(self.g_var, 1)

    def act(self, nc, act, n):
        act.wait_ge(self.g_var, n + 1)
        nc.scalar.activation(self.work[:, 4:5], self.g_ps[:, 1:2], ACT.Sqrt, bias=self.eps).then_inc(self.sd_done, 1)


def rel_projection(nc, io, K, scratch, v_tok, rel96, relv):
    zT = K["zT"]
    lhs_d, rhs_d = scratch["rel_lhs"], scratch["rel_rhs"]
    with ExitStack() as ctx:
        a = Alloc(nc, ctx, "relproj")
        w = a.sb("w", [P, 2, P])
        cols = a.sb("cols", [P, 2, 2])
        gavg = a.sb("gavg", [P, P])
        rel16 = a.sb("rel16", [2 * QD, BANK])
        relc = a.sb("relc", [2 * QD, BANK])
        relp = a.sb("relp", [2 * QD, 3, BANK], BF16)
        relv0 = a.sb("relv0", [P, HD])
        relv_col = a.sb("relv_col", [P, 1])
        zeros = a.sb("zeros", [P, SKEW_ROW])
        qk = a.sb("qk", [P, LP])
        rest = a.sb("rest", [P, LP])
        parts = a.sb("parts", [P, 3, LP], BF16)
        v = a.sb("v", [P, LP])
        qk_ps = a.ps("qk_ps", [P, 2 * BANK])
        v_ps = a.ps("v_ps", [P, 2 * BANK])
        turn_ps = a.ps("turn_ps", [P, 2 * BANK])
        g_ps = [a.ps(f"g_ps{i}", [P, BANK]) for i in range(2)]
        gn = [GroupNorm(a, ("qk", "v")[j], gavg[:], cols[:, j, :], g_ps[j], K["eps4"][:, 0:1]) for j in range(2)]
        x_ps = (qk_ps, v_ps)
        w_in, proj_done, norm_done, split_done, turned, turn_used, chain, filled, stacked, rel_in, rel_split, zeroed, rel_stacked, once = (
            a.sem(n) for n in ("w_in", "proj_done", "norm_done", "split_done", "turned", "turn_used", "chain",
                               "filled", "stacked", "rel_in", "rel_split", "zeroed", "rel_stacked", "once"))
        block = ctx.enter_context(nc.Block())

        @block.sync
        def _(sp):
            sp.dma_start(w[:], io["rel_w"]).then_inc(w_in, 16)
            sp.dma_start(cols[:], io["rel_gn"]).then_inc(w_in, 16)
            sp.dma_start(gavg[:], io["avg8"]).then_inc(w_in, 16)
            sp.dma_start(relv_col[:], io["relv_col"]).then_inc(w_in, 16)
            sp.dma_start(rel16[:], io["rel16"]).then_inc(rel_in, 16)
            sp.dma_start(relv[:], io["relv"]).then_inc(rel_in, 16)
            sp.dma_start(relv0[:], io["relv0"]).then_inc(rel_in, 16)
            sp.wait_ge(filled, 3)
            for name in ("rel_bias", "rel_probs"):
                for slot in range(2):
                    for t in range(SKEW_TILES):
                        sp.dma_start(scratch[name][slot, t], zeros[:]).then_inc(zeroed, 16)
            sp.wait_ge(rel_split, 1)
            for side in range(2):
                for s in range(NPART):
                    row = (side * NPART + s) * QD
                    sp.dma_start(rel96[row:row + QD, :], relp[side * QD:side * QD + QD, RIGHT_PART[s], :]
                                 ).then_inc(rel_stacked, 16)
            with sp.Fori(0, B) as b:
                sp.wait_ge(split_done, b + 2)
                for s in range(NPART):
                    for dst, row, src, part in ((lhs_d, s, 0, LEFT_PART[s]), (lhs_d, s + NPART, 1, LEFT_PART[s]),
                                                (rhs_d, s, 1, RIGHT_PART[s])):
                        sp.dma_start(dst[bass.ds(b * HEADS0, HEADS0), row * QD:row * QD + QD, :],
                                     parts[src * 64:src * 64 + 64, part, :]).then_inc(stacked, 16)
            sp.wait_ge(stacked, B * 3 * NPART * 16 + 16)
            sp.wait_ge(zeroed, 4 * SKEW_TILES * 16)
            sp.wait_ge(rel_stacked, 2 * NPART * 16)

        @block.tensor
        def _(pe):
            pe.wait_ge(w_in, 64)
            with pe.Fori(0, B) as b:
                pe.wait_ge(norm_done, b * 2 + 2)
                for j in range(2):
                    nc.tensor.matmul(x_ps[j][:, 0:BANK], w[:, j, :], zT[:, bass.ds(b * LP + LEAD, BANK)],
                                     start=True, stop=True)
                    nc.tensor.matmul(x_ps[j][:, BANK:L], w[:, j, :], zT[:, bass.ds(b * LP + (LEAD + BANK), L - BANK)],
                                     start=True, stop=True).then_inc(proj_done, 1)
                for j in range(2):
                    gn[j].pe(nc, pe, b)
                pe.wait_ge(norm_done, b * 2 + 4)
                pe.wait_ge(turn_used, b + 1)
                for t in range(TILES):
                    mm = nc.tensor.transpose(turn_ps[:, t * P:(t + 1) * P], v[:, t * P:(t + 1) * P], K["ident"][:])
                mm.then_inc(turned, 1)

        @block.scalar
        def _(act):
            act.sem_inc(norm_done, 2)
            act.wait_ge(filled, 3)
            with act.Fori(0, B) as b:
                for j in range(2):
                    gn[j].act(nc, act, b)
                act.wait_ge(gn[0].affine_ready, b + 1)
                act.wait_ge(split_done, b + 1)
                nc.scalar.activation(qk[:, 0:L], qk_ps[:, 0:L], ACT.Identity, bias=gn[0].work[:, 7:8],
                                     scale=gn[0].work[:, 6:7]).then_inc(norm_done, 1)
                act.wait_ge(gn[1].affine_ready, b + 1)
                act.wait_ge(turn_used, b + 1)
                nc.scalar.activation(v[:, 0:L], v_ps[:, 0:L], ACT.Identity, bias=gn[1].work[:, 7:8],
                                     scale=gn[1].work[:, 6:7]).then_inc(norm_done, 1)

        @block.vector
        def _(dve):
            dve.sem_inc(turn_used, 1)
            dve.sem_inc(split_done, 1)
            dve.sem_inc(stacked, 16)
            nc.vector.memset(zeros[:], 0.0).then_inc(filled, 1)
            nc.vector.memset(qk[:], 0.0).then_inc(filled, 1)
            nc.vector.memset(v[:], 0.0).then_inc(filled, 1)
            dve.wait_ge(rel_in, 48)
            dve.wait_ge(w_in, 64)
            c = Chain(dve, once)
            c.link(nc.vector.tensor_scalar(relc[:], rel16[:], rel16[:, REL:REL + 1], None, ALU.subtract))
            split3(nc, c, [relp[:, i, :] for i in range(3)], relc[:], rel16[:], rel_split)
            c.link(nc.vector.tensor_tensor(cols[:, 1, 1:2], cols[:, 1, 1:2], relv_col[:], ALU.add))
            for t in range(SKEW_TILES):
                c.link(nc.vector.tensor_tensor(relv[:, t, :], relv[:, t, :], relv0[:], ALU.subtract))
            with dve.Fori(0, B) as b:
                c = Chain(dve, chain, b, 2 * GroupNorm.LINKS + 4)
                for j in range(2):
                    dve.wait_ge(proj_done, b * 2 + j + 1)
                    gn[j].dve(nc, dve, c, x_ps[j], b)
                dve.wait_ge(norm_done, b * 2 + 3)
                dve.wait_ge(stacked, b * (3 * NPART * 16) + 16)
                split3(nc, c, [parts[:, i, :] for i in range(3)], qk[:], rest[:], split_done)
                dve.wait_ge(turned, b + 1)
                nc.vector.tensor_copy(v_tok[:, :, bass.ds(b * P, P)],
                                      turn_ps[:, 0:LP].rearrange("p (t c) -> p t c", t=TILES)).then_inc(turn_used, 1)
                c.end()


class Turn:

    def __init__(self, m, k):
        self.n, self.slot, self.turn = m * 2 + k, k % 2, m + k // 2
        self.first = isinstance(m, int) and self.n == 0
        self.early = isinstance(m, int) and self.n < 2


def rel_attention(nc, io, K, scratch, v_tok, rel96, relv, o_tok):
    with ExitStack() as ctx:
        a = Alloc(nc, ctx, "rel")
        lhs = [a.sb(f"lhs{i}", [2 * NPART * QD, LP], BF16) for i in range(2)]
        rhs = [a.sb(f"rhs{i}", [NPART * QD, LP], BF16) for i in range(2)]
        r_sb = [a.sb(f"r_sb{i}", [P, SKEW_TILES, BANK]) for i in range(2)]
        bias = [[a.sb(f"bias{i}_{t}", [P, SKEW_W[t]]) for t in range(SKEW_TILES)] for i in range(2)]
        probs = [a.sb(f"probs{i}", [P, TILES, LP]) for i in range(2)]
        shear = [[a.sb(f"shear{i}_{t}", [P, SKEW_PAD[t]]) for t in range(SKEW_TILES)] for i in range(2)]
        probsT = [a.sb(f"probsT{i}", [P, TILES, LP]) for i in range(2)]
        shearT = a.sb("shearT", [P, SKEW_TILES, BANK])
        nmax = [a.sb(f"nmax{i}", [P, TILES]) for i in range(2)]
        sums = [a.sb(f"sums{i}", [P, TILES]) for i in range(2)]
        rsum = a.sb("rsum", [P, TILES])
        s_ps = [a.ps(f"s_ps{i}", [P, 2 * BANK]) for i in range(2)]
        t_ps = a.ps("t_ps", [P, 2 * BANK])
        x_ps = a.ps("x_ps", [P, BANK])
        o_ps = a.ps("o_ps", [P, BANK])
        in_sem = a.sems("pair_in", 2)
        bias_out, bias_in = a.sems("bias_out", 2), a.sems("bias_in", 2)
        probs_out, shear_in = a.sems("probs_out", 2), a.sems("shear_in", 2)
        passed = a.sem("passed")
        r_full, r_copied, a_full, a_copied, s_full, biased, max_ready, exp_done, t_full, t_copied, o_full, o_done, rs_ready, filled = (
            a.sem(n) for n in ("r_full", "r_copied", "a_full", "a_copied", "s_full", "biased", "max_ready",
                               "exp_done", "t_full", "t_copied", "o_full", "o_done", "rs_ready", "filled"))
        NS = SKEW_TILES
        blocks_of = [w // P for w in SKEW_PAD]
        block = ctx.enter_context(nc.Block())

        def turns(eng, body):
            t = [Turn(0, k) for k in range(PAIRS)]
            body(t[0], None, None)
            body(t[1], t[0], None)
            body(t[2], t[1], t[0])
            with eng.Fori(0, (PAIRS - 4) // 2) as m:
                for k in range(2):
                    body(Turn(m, k + 3), Turn(m, k + 2), Turn(m, k + 1))
            body(t[PAIRS - 1], t[PAIRS - 2], t[PAIRS - 3])
            body(None, t[PAIRS - 1], t[PAIRS - 2])
            body(None, None, t[PAIRS - 1])

        def sheared(name, slot, t, step, width):
            rows = scratch[name]
            at = (slot * SKEW_TILES + t) * P * SKEW_ROW
            return bass.AP(rows.tensor, rows.offset + at, [[step, P], [1, width]])

        def copy_turned(eng, copy, now, t):
            if t < 2 and not now.early:
                eng.wait_ge(o_full, now.n - 1)
            eng.wait_ge(t_full, now.n * TILES + t + 1)
            copy(probsT[now.slot][:, t, :], t_ps[:, 0:LP]).then_inc(t_copied, 1)

        @block.sync
        def _(sp):
            def load(pair):
                sp.dma_start(lhs[pair.slot][:], scratch["rel_lhs"][bass.ds(pair.n, 1), :, :].squeeze(0)).then_inc(in_sem[pair.slot], 16)
                sp.dma_start(rhs[pair.slot][:], scratch["rel_rhs"][bass.ds(pair.n, 1), :, :].squeeze(0)).then_inc(in_sem[pair.slot], 16)

            def body(new, now, old):
                if new is not None:
                    if old is not None:
                        sp.wait_ge(s_full, old.n * TILES + TILES)
                    load(new)
                if old is not None and new is not None:
                    sp.wait_ge(bias_in[new.slot], new.turn * (16 * NS))
                if old is not None and now is not None:
                    sp.wait_ge(shear_in[now.slot], now.turn * (16 * NS))
                for t in range(NS):
                    if now is not None:
                        sp.wait_ge(exp_done, now.n * TILES + t + 1)
                        sp.dma_start(scratch["rel_probs"][now.slot, t, :, 0:SKEW_W[t]],
                                     probs[now.slot][:, t, L - SKEW_W[t]:L]).then_inc(probs_out[now.slot], 16)
                    if new is not None:
                        sp.wait_ge(r_copied, new.n * NS + t + 1)
                        sp.dma_start(scratch["rel_bias"][new.slot, t, :, 0:SKEW_W[t]], r_sb[new.slot][:, t, 0:SKEW_W[t]]
                                     ).then_inc(bias_out[new.slot], 16)
                if new is not None:
                    sp.wait_ge(bias_out[new.slot], new.turn * (16 * NS) + 16 * NS)
                    apart(sp, passed)
                    if old is not None:
                        sp.wait_ge(biased, old.n * NS + NS)
                    for t in range(NS):
                        sp.dma_start(bias[new.slot][t][:], sheared("rel_bias", new.slot, t, SKEW_ROW - 1, SKEW_W[t])
                                     ).then_inc(bias_in[new.slot], 16)
                if now is not None:
                    sp.wait_ge(probs_out[now.slot], now.turn * (16 * NS) + 16 * NS)
                    apart(sp, passed)
                    if old is not None:
                        sp.wait_ge(a_full, now.n * NS - NS)
                    for t in range(NS):
                        sp.dma_start(shear[now.slot][t][:], sheared("rel_probs", now.slot, t, SKEW_ROW + 1, SKEW_PAD[t])
                                     ).then_inc(shear_in[now.slot], 16)

            turns(sp, body)

        @block.tensor
        def _(pe):
            def position(new, now, old, t):
                if now is not None or t > 0:
                    pe.wait_ge(r_copied, new.n * NS + t)
                if old is not None and (t > 0 or not old.first):
                    pe.wait_ge(a_copied, old.n * NS + t)
                if t == 0:
                    pe.wait_ge(in_sem[new.slot], new.turn * 32 + 32)
                nc.tensor.matmul(x_ps[:, 0:SKEW_W[t]], lhs[new.slot][:, t * P:(t + 1) * P], rel96[:, 0:SKEW_W[t]],
                                 start=True, stop=True).then_inc(r_full, 1)

            def scores(now, t):
                i = t % 2
                if t >= 2 or not now.first:
                    pe.wait_ge(exp_done, now.n * TILES + t - 1)
                nc.tensor.matmul(s_ps[i][:, 0:BANK], lhs[now.slot][0:NPART * QD, t * P:(t + 1) * P],
                                 rhs[now.slot][:, 0:BANK], start=True, stop=True)
                nc.tensor.matmul(s_ps[i][:, BANK:L], lhs[now.slot][0:NPART * QD, t * P:(t + 1) * P],
                                 rhs[now.slot][:, BANK:L], start=True, stop=True).then_inc(s_full, 1)

            def turn_probs(now, t):
                pe.wait_ge(exp_done, now.n * TILES + t + 1)
                if t > 0 or not now.first:
                    pe.wait_ge(t_copied, now.n * TILES + t)
                for j in range(TILES):
                    mm = nc.tensor.transpose(t_ps[:, j * P:(j + 1) * P], probs[now.slot][:, t, j * P:(j + 1) * P],
                                             K["ident"][:])
                mm.then_inc(t_full, 1)

            def turn_shear(new, old, t):
                if t == 0:
                    pe.wait_ge(shear_in[old.slot], old.turn * (16 * NS) + 16 * NS)
                if new is not None:
                    pe.wait_ge(r_copied, new.n * NS + t + 1)
                if t > 0 or not old.first:
                    pe.wait_ge(a_copied, old.n * NS + t)
                for j in range(blocks_of[t]):
                    mm = nc.tensor.transpose(x_ps[:, j * P:(j + 1) * P], shear[old.slot][t][:, j * P:(j + 1) * P],
                                             K["ident"][:])
                mm.then_inc(a_full, 1)

            def output(old):
                pe.wait_ge(t_copied, old.n * TILES + TILES)
                pe.wait_ge(a_copied, old.n * NS + NS)
                if not old.first:
                    pe.wait_ge(o_done, old.n)
                for t in range(TILES):
                    o = o_ps[:, t * HD:(t + 1) * HD]
                    for j in range(TILES):
                        last = j == TILES - 1 and t >= NS
                        mm = nc.tensor.matmul(o, probsT[old.slot][:, t, j * P:(j + 1) * P],
                                              v_tok[:, j, bass.ds(old.n * HD, HD)], start=(j == 0), stop=last)
                    if t < NS:
                        for j in range(blocks_of[t]):
                            mm = nc.tensor.matmul(o, shearT[:, t, j * P:(j + 1) * P], relv[:, j, :],
                                                  start=False, stop=(j == blocks_of[t] - 1))
                mm.then_inc(o_full, 1)

            def body(new, now, old):
                for t in range(TILES):
                    if now is not None:
                        scores(now, t)
                    if new is not None and 1 <= t <= NS:
                        position(new, now, old, t - 1)
                    if now is not None and t >= 1:
                        turn_probs(now, t - 1)
                    if old is not None and 1 <= t <= NS:
                        turn_shear(new, old, t - 1)
                if now is not None:
                    turn_probs(now, TILES - 1)
                if old is not None:
                    output(old)

            pe.wait_ge(filled, 2)
            turns(pe, body)

        @block.scalar
        def _(act):
            def body(new, now, old):
                for t in range(TILES):
                    if now is not None:
                        act.wait_ge(max_ready, now.n * TILES + t + 1)
                        if t == 0 and old is not None:
                            act.wait_ge(t_full, now.n * TILES - TILES)
                            act.wait_ge(probs_out[now.slot], now.turn * (16 * NS))
                            act.wait_ge(rs_ready, now.n - 1)
                        nc.scalar.activation(probs[now.slot][:, t, 0:L], s_ps[t % 2][:, 0:L], ACT.Exp,
                                             bias=nmax[now.slot][:, t:t + 1],
                                             accum_out=sums[now.slot][:, t:t + 1]).then_inc(exp_done, 1)
                    if new is not None and 1 <= t <= NS:
                        if t == 1 and old is not None:
                            act.wait_ge(bias_out[new.slot], new.turn * (16 * NS))
                        act.wait_ge(r_full, new.n * NS + t)
                        nc.scalar.activation(r_sb[new.slot][:, t - 1, 0:SKEW_W[t - 1]], x_ps[:, 0:SKEW_W[t - 1]],
                                             ACT.Identity).then_inc(r_copied, 1)
                    if now is not None and t >= 1 and (t - 1) % 2 == 0:
                        copy_turned(act, nc.scalar.copy, now, t - 1)
                    if old is not None and 1 <= t <= NS:
                        if t == 1 and not old.first:
                            act.wait_ge(o_full, old.n)
                        act.wait_ge(a_full, old.n * NS + t)
                        w = SKEW_PAD[t - 1]
                        nc.scalar.copy(shearT[:, t - 1, 0:w], x_ps[:, 0:w]).then_inc(a_copied, 1)

            turns(act, body)

        @block.vector
        def _(dve):
            def body(new, now, old):
                for t in range(TILES):
                    if now is not None:
                        dve.wait_ge(s_full, now.n * TILES + t + 1)
                        if t < NS:
                            if t == 0:
                                dve.wait_ge(bias_in[now.slot], now.turn * (16 * NS) + 16 * NS)
                            s = s_ps[t % 2][:, L - SKEW_W[t]:L]
                            nc.vector.tensor_tensor(s, s, bias[now.slot][t][:], ALU.add).then_inc(biased, 1)
                            dve.wait_ge(biased, now.n * NS + t + 1)
                        if t == 0 and old is not None:
                            dve.wait_ge(exp_done, now.n * TILES - TILES)
                        nc.vector.tensor_reduce(nmax[now.slot][:, t:t + 1], s_ps[t % 2][:, 0:L], AX.X, ALU.max,
                                                negate=True).then_inc(max_ready, 1)
                        if t >= 1 and (t - 1) % 2 == 1:
                            copy_turned(dve, nc.vector.tensor_copy, now, t - 1)
                if now is not None:
                    copy_turned(dve, nc.vector.tensor_copy, now, TILES - 1)
                if old is not None:
                    dve.wait_ge(exp_done, old.n * TILES + TILES)
                    if not old.first:
                        dve.wait_ge(o_done, old.n)
                    nc.vector.reciprocal(rsum[:], sums[old.slot][:]).then_inc(rs_ready, 1)
                    dve.wait_ge(rs_ready, old.n + 1)
                    dve.wait_ge(o_full, old.n + 1)
                    nc.vector.tensor_tensor(o_tok[:, :, bass.ds(old.n * HD, HD)],
                                            o_ps[:, 0:TILES * HD].rearrange("p (t d) -> p t d", t=TILES),
                                            rsum[:, :].unsqueeze(2).to_broadcast([P, TILES, HD]),
                                            ALU.mult).then_inc(o_done, 1)

            for i in range(2):
                nc.vector.memset(probs[i][:, :, L:LP], 0.0).then_inc(filled, 1)
            turns(dve, body)


def rel_output(nc, io, K, o_tok):
    hT = K["hT"]
    with ExitStack() as ctx:
        a = Alloc(nc, ctx, "relout")
        gavg = a.sb("gavg", [P, P])
        cols = a.sb("cols", [P, 2])
        y = a.sb("y", [P, L])
        o_ps = [a.ps(f"o_ps{i}", [P, 2 * BANK]) for i in range(2)]
        g_ps = a.ps("g_ps", [P, BANK])
        gn = GroupNorm(a, "out", gavg[:], cols[:], g_ps, K["eps4"][:, 0:1])
        w_in, turned, scaled, added, chain = (a.sem(n) for n in ("w_in", "turned", "scaled", "added", "chain"))
        block = ctx.enter_context(nc.Block())

        @block.sync
        def _(sp):
            sp.dma_start(gavg[:], io["avg4"]).then_inc(w_in, 16)
            sp.dma_start(cols[:], io["relout_gn"]).then_inc(w_in, 16)

        @block.tensor
        def _(pe):
            pe.wait_ge(w_in, 32)
            for b in range(B):
                if b >= 2:
                    pe.wait_ge(scaled, b - 1)
                for t in range(TILES):
                    mm = nc.tensor.transpose(o_ps[b % 2][:, t * P:(t + 1) * P], o_tok[:, t, b * P:(b + 1) * P],
                                             K["ident"][:])
                mm.then_inc(turned, 1)
                gn.pe(nc, pe, b)

        @block.scalar
        def _(act):
            for b in range(B):
                gn.act(nc, act, b)
                act.wait_ge(gn.affine_ready, b + 1)
                if b >= 1:
                    act.wait_ge(added, b)
                nc.scalar.activation(y[:], o_ps[b % 2][:, 0:L], ACT.Identity, bias=gn.work[:, 7:8],
                                     scale=gn.work[:, 6:7]).then_inc(scaled, 1)

        @block.vector
        def _(dve):
            dve.wait_ge(w_in, 32)
            c = Chain(dve, chain)
            for b in range(B):
                dve.wait_ge(turned, b + 1)
                gn.dve(nc, dve, c, o_ps[b % 2], b)
                dve.wait_ge(scaled, b + 1)
                h = hT[:, b * L:(b + 1) * L]
                nc.vector.tensor_tensor(h, h, y[:], ALU.add).then_inc(added, 1)
                dve.wait_ge(added, b + 1)


def stage1(nc, io, K, scratch):
    with ExitStack() as ctx:
        a = Alloc(nc, ctx, "stage1")
        o_tok = a.sb("o_tok", [P, TILES, PAIRS * HD])
        v_tok = a.sb("v_tok", [P, TILES, PAIRS * HD])
        rel96 = a.sb("rel96", [2 * NPART * QD, BANK], BF16)
        relv = a.sb("relv", [P, SKEW_TILES, HD])
        scratch["rel_lhs"] = nc.dram_tensor("rel_lhs", (PAIRS, 2 * NPART * QD, LP), BF16, kind="Internal").ap()
        scratch["rel_rhs"] = nc.dram_tensor("rel_rhs", (PAIRS, NPART * QD, LP), BF16, kind="Internal").ap()
        scratch["rel_bias"] = nc.dram_tensor("rel_bias", (2, SKEW_TILES, P, SKEW_ROW), F32, kind="Internal").ap()
        scratch["rel_probs"] = nc.dram_tensor("rel_probs", (2, SKEW_TILES, P, SKEW_ROW), F32, kind="Internal").ap()
        rel_projection(nc, io, K, scratch, v_tok, rel96, relv)
        rel_attention(nc, io, K, scratch, v_tok, rel96, relv, o_tok)
        rel_output(nc, io, K, o_tok)


STAGES[1] = stage1


def group_average(size):
    return np.kron(np.eye(P // size, dtype=np.float32), np.full((size, size), 1.0 / size, np.float32))


def stage1_layout(f):
    chan = np.arange(2 * P).reshape(HEADS0, 4, QD)
    qk = np.concatenate([chan[:, 0].ravel(), chan[:, 1].ravel()])
    v = chan[:, 2:].ravel()
    gn = np.stack([f["L0_attn_gn_qkv_scale"], f["L0_attn_gn_qkv_bias"]], 1)
    rel = f["L0_attn_rel_emb"]
    col = np.minimum(np.arange(BANK), REL)
    rev = np.where(col < REL, REL - 1 - col, REL)
    relq, relk, relv = rel[:QD], rel[QD:2 * QD], rel[2 * QD:]
    return {
        "rel_w": np.stack([f["L0_attn_W_qkv"][:, qk], f["L0_attn_W_qkv"][:, v]], 1),
        "rel_gn": np.stack([gn[qk], gn[v]], 1),
        "avg8": group_average(8),
        "avg4": group_average(4),
        "relout_gn": np.stack([f["L0_attn_gn_out_scale"], f["L0_attn_gn_out_bias"]], 1),
        "rel16": np.concatenate([relk, relq])[:, rev],
        "relv": relv[:, rev].T.reshape(SKEW_TILES, P, HD).transpose(1, 0, 2),
        "relv0": np.broadcast_to(relv[:, REL], (P, HD)),
        "relv_col": np.tile(relv[:, REL], HEADS0)[:, None],
    }


TOK_TILES = B * TILES
NCH = len(CHUNKS)
HID = 512
HJ = HID // P


def top2_gates(nc, K, a, block, lg, lg_ready, E, gates, pack, pack_ps, packT, gates_d):
    W = E if pack == "sum" else 4 * E
    best = a.sb("best", [P, TOK_TILES, 8])
    at = a.sb("at", [P, TOK_TILES, 8], U32)
    atf = a.sb("atf", [P, TOK_TILES, 2])
    iota = a.sb("iota", [P, TOK_TILES, E])
    g = a.sb("g", [P, 2, TOK_TILES])
    e = a.sb("e", [P, 2, TOK_TILES])
    one = a.sb("one", [P, TOK_TILES, E])
    iota_in, found, diff_ready, exp_ready, packed, turned, copied, chain = (a.sem(f"top2_{n}") for n in (
        "iota_in", "found", "diff_ready", "exp_ready", "packed", "turned", "copied", "chain"))
    gates_out = a.sem("top2_gates_out")

    @block.sync
    def _(sp):
        sp.dma_start(iota[:], K["iota_d"][:, :, 0:E]).then_inc(iota_in, 16)
        for b in range(B):
            sp.wait_ge(copied, b + 1)
            sp.dma_start(gates_d[:, b * LP:(b + 1) * LP], packT[:, b * LP:(b + 1) * LP]).then_inc(gates_out, 16)
        sp.wait_ge(gates_out, B * 16)

    @block.scalar
    def _(act):
        act.wait_ge(diff_ready, 1)
        nc.scalar.activation(e[:, 0, :], g[:, 0, :], ACT.Exp).then_inc(exp_ready, 1)

    @block.vector
    def _(dve):
        c = Chain(dve, chain)
        dve.wait_ge(lg_ready[0], lg_ready[1])
        for t in range(TOK_TILES):
            c.link(nc.vector.max(best[:, t, :], lg[:, t, :]))
            nc.vector.max_index(at[:, t, :], best[:, t, :], lg[:, t, :]).then_inc(found, 1)
        dve.wait_ge(found, TOK_TILES)
        nc.vector.tensor_tensor(g[:, 0, :].unsqueeze(2), best[:, :, 1:2], best[:, :, 0:1], ALU.subtract).then_inc(diff_ready, 1)
        c.link(nc.vector.tensor_copy(atf[:], at[:, :, 0:2]))
        dve.wait_ge(exp_ready, 1)
        c.link(nc.vector.tensor_scalar(e[:, 1, :], e[:, 0, :], 1.0, None, ALU.add))
        c.link(nc.vector.reciprocal(g[:, 0, :], e[:, 1, :]))
        c.link(nc.vector.tensor_tensor(g[:, 1, :], g[:, 0, :], e[:, 0, :], ALU.mult))
        dve.wait_ge(iota_in, 16)
        full = [P, TOK_TILES, E]
        for k in range(2):
            mask = one[:] if pack == "sum" else gates[:, :, k * E:(k + 1) * E]
            out = gates[:, :, 0:E] if pack == "sum" and k == 0 else one[:] if pack == "sum" else gates[:, :, (2 + k) * E:(3 + k) * E]
            c.link(nc.vector.tensor_tensor(mask, iota[:], atf[:, :, k:k + 1].to_broadcast(full), ALU.is_equal))
            c.link(nc.vector.tensor_tensor(out, mask, g[:, k, :].unsqueeze(2).to_broadcast(full), ALU.mult))
        if pack == "sum":
            c.link(nc.vector.tensor_tensor(gates[:], gates[:], one[:], ALU.add))
        dve.sem_inc(packed, 1)
        for b in range(B):
            dve.wait_ge(turned, b + 1)
            nc.vector.tensor_copy(packT[:, b * LP:(b + 1) * LP], pack_ps[0:W, 0:LP]).then_inc(copied, 1)

    @block.tensor
    def _(pe):
        pe.wait_ge(packed, 1)
        for b in range(B):
            if b >= 1:
                pe.wait_ge(copied, b)
            for t in range(TILES):
                mm = nc.tensor.transpose(pack_ps[0:W, t * P:(t + 1) * P], gates[:, b * TILES + t, :], K["ident"][:])
            mm.then_inc(turned, 1)


def experts(nc, K, scratch, name, E, kind, weights, b2, gates_d, y):
    zT = K["zT"]
    with ExitStack() as ctx:
        a = Alloc(nc, ctx, name)
        w = [a.sb(f"w{i}", [P, 2 * HID + HJ]) for i in range(2)]
        gate = [a.sb(f"gate{i}", [P, B * LP]) for i in range(2)]
        b2_sb = a.sb("b2", [E, P])
        gT = a.sb("gT", [E, B * LP])
        ex = [a.sb(f"ex{j}", [P, HALF]) for j in range(HJ)]
        hid = [a.sb(f"hid{i}", [P, HJ, HALF]) for i in range(2)]
        part = a.sb("part", [P, HALF])
        h_ps = [a.ps(f"h_ps{j}", [P, BANK]) for j in range(HJ)]
        o_ps = [a.ps(f"o_ps{i}", [P, BANK]) for i in range(2)]
        w_in = a.sems("w_in", 2)
        rows_in, b_full, y_set, h_full, ex_done, low_done, h_done, o_full, y_done, part_done = (a.sem(n) for n in (
            "rows_in", "b_full", "y_set", "h_full", "ex_done", "low_done", "h_done", "o_full", "y_done", "part_done"))
        block = ctx.enter_context(nc.Block())
        PAIR = 2 * NCH

        def zc(c):
            b, half = CHUNKS[c]
            return zT[:, LEAD + b * LP + half * HALF:LEAD + b * LP + half * HALF + HALF]

        def yc(c):
            return y[:, c * HALF:(c + 1) * HALF]

        def gc(s, c):
            b, half = CHUNKS[c]
            return gate[s][:, b * LP + half * HALF:b * LP + half * HALF + HALF]

        @block.sync
        def _(sp):
            sp.dma_start(b2_sb[:], b2).then_inc(rows_in, 16)
            sp.dma_start(gT[:], gates_d).then_inc(rows_in, 16)
            with sp.Fori(0, E // 2) as m:
                for s in range(2):
                    sp.wait_ge(y_done, m * PAIR + (s * NCH + NCH))
                    sp.dma_start(w[s][:], weights[bass.ds(m * 2 + s, 1), :, :].squeeze(0)).then_inc(w_in[s], 16)
                    sp.dma_start(gate[s][:], gates_d[bass.ds(m * 2 + s, 1), :].to_broadcast([P, B * LP])).then_inc(w_in[s], 16)

        @block.tensor
        def _(pe):
            pe.wait_ge(rows_in, 32)
            for c in range(NCH):
                if c >= 2:
                    pe.wait_ge(y_set, c - 1)
                b, half = CHUNKS[c]
                nc.tensor.matmul(o_ps[c % 2][:, 0:HALF], b2_sb[:], gT[:, b * LP + half * HALF:b * LP + half * HALF + HALF],
                                 start=True, stop=True).then_inc(b_full, 1)
            pe.wait_ge(y_set, NCH)

            def first(m, i):
                s, c = i // NCH, i % NCH
                if c == 0:
                    pe.wait_ge(w_in[s], m * 32 + 32)
                for j in range(HJ):
                    pe.wait_ge(h_done, m * (PAIR * HJ) + (i * HJ + j + 1))
                    nc.tensor.matmul(h_ps[j][:, 0:HALF], w[s][:, j * P:(j + 1) * P], zc(c),
                                     start=True, stop=True).then_inc(h_full, 1)

            def second(m, i):
                s = i // NCH
                pe.wait_ge(h_done, m * (PAIR * HJ) + (i * HJ + 2 * HJ))
                pe.wait_ge(y_done, m * PAIR + (i + PAIR - 1))
                for j in range(HJ):
                    mm = nc.tensor.matmul(o_ps[i % 2][:, 0:HALF], w[s][:, HID + j * P:HID + (j + 1) * P],
                                          hid[i % 2][:, j, :], start=(j == 0), stop=(j == HJ - 1))
                mm.then_inc(o_full, 1)

            with pe.Fori(0, E // 2) as m:
                for i in range(PAIR):
                    first(m, i)
                    if i >= 1:
                        second(m, i - 1)
                second(m, PAIR - 1)

        @block.scalar
        def _(act):
            with act.Fori(0, E // 2) as m:
                for i in range(PAIR):
                    s = i // NCH
                    if kind != "elu":
                        act.wait_ge(o_full, m * PAIR + (i + 1))
                    for j in range(HJ):
                        act.wait_ge(h_full, m * (PAIR * HJ) + (i * HJ + j + 1))
                        b1 = w[s][:, 2 * HID + j:2 * HID + j + 1]
                        if kind == "elu":
                            nc.scalar.activation(ex[j][:], h_ps[j][:, 0:HALF], ACT.Exp, bias=b1).then_inc(ex_done, 1)
                        else:
                            nc.scalar.activation(hid[i % 2][:, j, :], h_ps[j][:, 0:HALF], kind, bias=b1).then_inc(h_done, 1)

        @block.vector
        def _(dve):
            dve.sem_inc(h_done, HJ)
            dve.sem_inc(o_full, 2)
            dve.sem_inc(y_done, PAIR)
            for c in range(NCH):
                dve.wait_ge(b_full, c + 1)
                nc.vector.tensor_copy(yc(c), o_ps[c % 2][:, 0:HALF]).then_inc(y_set, 1)

            def gather(m, i):
                s, c = i // NCH, i % NCH
                if c == 0:
                    dve.wait_ge(w_in[s], m * 32 + 32)
                dve.wait_ge(y_done, m * PAIR + (i + PAIR))
                dve.wait_ge(o_full, m * PAIR + (i + 3))
                nc.vector.tensor_tensor(part[:], o_ps[i % 2][:, 0:HALF], gc(s, c), ALU.mult).then_inc(part_done, 1)
                dve.wait_ge(part_done, m * PAIR + (i + 1))
                nc.vector.tensor_tensor(yc(c), yc(c), part[:], ALU.add).then_inc(y_done, 1)

            with dve.Fori(0, E // 2) as m:
                for i in range(PAIR):
                    s = i // NCH
                    if kind == "elu":
                        dve.wait_ge(o_full, m * PAIR + (i + 1))
                        for j in range(HJ):
                            n = m * (PAIR * HJ) + (i * HJ + j + 1)
                            dve.wait_ge(ex_done, n)
                            nc.vector.tensor_scalar(ex[j][:], ex[j][:], 1.0, -1.0, ALU.min, ALU.add).then_inc(low_done, 1)
                            dve.wait_ge(low_done, n)
                            nc.vector.scalar_tensor_tensor(out=hid[i % 2][:, j, :], in0=h_ps[j][:, 0:HALF],
                                                           scalar=w[s][:, 2 * HID + j:2 * HID + j + 1], in1=ex[j][:],
                                                           op0=ALU.add, op1=ALU.max).then_inc(h_done, 1)
                    if i >= 1:
                        gather(m, i - 1)
                gather(m, PAIR - 1)


E0 = 10
TAPS_R, TAPS_S = 3, 9


def conv_router(nc, io, K, gates_d):
    zT = K["zT"]
    with ExitStack() as ctx:
        a = Alloc(nc, ctx, "router")
        w1 = a.sb("w1", [P, TAPS_R, P])
        w2 = a.sb("w2", [P, TAPS_R, E0])
        b1 = a.sb("b1", [P, 1])
        b2 = a.sb("b2", [P, E0])
        rc = a.sb("rc", [P, 1 + LP + 1])
        lg = a.sb("lg", [P, TOK_TILES, E0])
        gates = a.sb("gates", [P, TOK_TILES, E0])
        packT = a.sb("packT", [E0, B * LP])
        c_ps = [a.ps(f"c_ps{i}", [P, BANK]) for i in range(2)]
        l_ps = a.ps("l_ps", [P, TILES, E0])
        pack_ps = a.ps("pack_ps", [P, 2 * BANK])
        w_in, filled, conv_done, rc_done, l_done, lg_ready = (a.sem(n) for n in (
            "w_in", "filled", "conv_done", "rc_done", "l_done", "lg_ready"))
        block = ctx.enter_context(nc.Block())

        @block.sync
        def _(sp):
            for dst, src in ((w1, "rc_w1"), (w2, "rc_w2"), (b1, "rc_b1"), (b2, "rc_b2")):
                sp.dma_start(dst[:], io[src]).then_inc(w_in, 16)

        @block.tensor
        def _(pe):
            pe.wait_ge(w_in, 64)
            with pe.Fori(0, B) as b:
                for half in range(2):
                    pe.wait_ge(rc_done, b * 2 + half + 1)
                    for k in range(TAPS_R):
                        mm = nc.tensor.matmul(c_ps[half][:, 0:HALF], w1[:, k, :], z_chunk(zT, b, half, k - TAPS_R // 2),
                                              start=(k == 0), stop=(k == TAPS_R - 1))
                    mm.then_inc(conv_done, 1)
                pe.wait_ge(rc_done, b * 2 + 4)
                pe.wait_ge(lg_ready, b + 1)
                for t in range(TILES):
                    for k in range(TAPS_R):
                        mm = nc.tensor.matmul(l_ps[:, t, :], rc[:, t * P + k:t * P + k + P], w2[:, k, :],
                                              start=(k == 0), stop=(k == TAPS_R - 1))
                mm.then_inc(l_done, 1)

        @block.scalar
        def _(act):
            act.sem_inc(rc_done, 2)
            act.wait_ge(w_in, 64)
            act.wait_ge(filled, 1)
            with act.Fori(0, B) as b:
                act.wait_ge(lg_ready, b + 1)
                for half in range(2):
                    act.wait_ge(conv_done, b * 2 + half + 1)
                    nc.scalar.activation(rc[:, 1 + half * HALF:1 + half * HALF + HALF], c_ps[half][:, 0:HALF],
                                         ACT.Gelu, bias=b1[:, 0:1]).then_inc(rc_done, 1)

        @block.vector
        def _(dve):
            dve.sem_inc(lg_ready, 1)
            nc.vector.memset(rc[:], 0.0).then_inc(filled, 1)
            dve.wait_ge(w_in, 64)
            with dve.Fori(0, B) as b:
                dve.wait_ge(l_done, b + 1)
                nc.vector.tensor_tensor(lg[:, bass.ds(b * TILES, TILES), :], l_ps[:],
                                        b2[:, :].unsqueeze(1).to_broadcast([P, TILES, E0]), ALU.add).then_inc(lg_ready, 1)

        top2_gates(nc, K, a, block, lg, (lg_ready, B + 1), E0, gates, "sum", pack_ps, packT, gates_d)


def shared_conv(nc, io, K, y):
    zT = K["zT"]
    with ExitStack() as ctx:
        a = Alloc(nc, ctx, "shared")
        w1 = a.sb("w1", [P, TAPS_S, HID])
        w2 = a.sb("w2", [P, HJ, P])
        b1 = a.sb("b1", [P, HJ])
        b2 = a.sb("b2", [P, 1])
        hid = [a.sb(f"hid{i}", [P, HJ, HALF]) for i in range(2)]
        part = a.sb("part", [P, HALF])
        h_ps = [a.ps(f"h_ps{j}", [P, BANK]) for j in range(HJ)]
        o_ps = [a.ps(f"o_ps{i}", [P, BANK]) for i in range(2)]
        w_in, h_full, h_done, o_full, y_done, part_done = (a.sem(n) for n in (
            "w_in", "h_full", "h_done", "o_full", "y_done", "part_done"))
        block = ctx.enter_context(nc.Block())

        @block.sync
        def _(sp):
            for dst, src in ((w1, "sh_w1"), (w2, "sh_w2"), (b1, "sh_b1"), (b2, "sh_b2")):
                sp.dma_start(dst[:], io[src]).then_inc(w_in, 16)

        @block.tensor
        def _(pe):
            pe.wait_ge(w_in, 64)

            def first(b, i):
                for j in range(HJ):
                    pe.wait_ge(h_done, b * (2 * HJ) + (i * HJ + j + 1))
                    for k in range(TAPS_S):
                        mm = nc.tensor.matmul(h_ps[j][:, 0:HALF], w1[:, k, j * P:(j + 1) * P],
                                              z_chunk(zT, b, i, k - TAPS_S // 2), start=(k == 0), stop=(k == TAPS_S - 1))
                    mm.then_inc(h_full, 1)

            def second(b, i):
                pe.wait_ge(h_done, b * (2 * HJ) + (i * HJ + 2 * HJ))
                pe.wait_ge(y_done, b * 2 + (i + 1))
                for j in range(HJ):
                    mm = nc.tensor.matmul(o_ps[i][:, 0:HALF], w2[:, j, :], hid[i][:, j, :],
                                          start=(j == 0), stop=(j == HJ - 1))
                mm.then_inc(o_full, 1)

            with pe.Fori(0, B) as b:
                first(b, 0)
                first(b, 1)
                second(b, 0)
                second(b, 1)

        @block.scalar
        def _(act):
            act.sem_inc(h_done, HJ)
            act.sem_inc(o_full, 2)
            with act.Fori(0, B) as b:
                for i in range(2):
                    act.wait_ge(o_full, b * 2 + (i + 1))
                    for j in range(HJ):
                        act.wait_ge(h_full, b * (2 * HJ) + (i * HJ + j + 1))
                        nc.scalar.activation(hid[i][:, j, :], h_ps[j][:, 0:HALF], ACT.Silu,
                                             bias=b1[:, j:j + 1]).then_inc(h_done, 1)

        @block.vector
        def _(dve):
            dve.sem_inc(y_done, 2)
            dve.wait_ge(w_in, 64)
            with dve.Fori(0, B) as b:
                for i in range(2):
                    dve.wait_ge(y_done, b * 2 + (i + 2))
                    dve.wait_ge(o_full, b * 2 + (i + 3))
                    nc.vector.scalar_tensor_tensor(out=part[:], in0=o_ps[i][:, 0:HALF], scalar=b2[:, 0:1],
                                                   in1=z_chunk(zT, b, i), op0=ALU.add, op1=ALU.add).then_inc(part_done, 1)
                    dve.wait_ge(part_done, b * 2 + (i + 1))
                    nc.vector.tensor_tensor(h_chunk(y, b, i), h_chunk(y, b, i), part[:], ALU.add).then_inc(y_done, 1)


def stage2(nc, io, K, scratch):
    gates_d = nc.dram_tensor("gates0", (E0, B * LP), F32, kind="Internal").ap()
    conv_router(nc, io, K, gates_d)
    with ExitStack() as ctx:
        a = Alloc(nc, ctx, "stage2")
        y = a.sb("y", [P, B * L])
        cols = a.sb("ln_cols", [P, 2])
        experts(nc, K, scratch, "moe0", E0, "elu", io["moe0_w"], io["moe0_b2"], gates_d, y)
        shared_conv(nc, io, K, y)
        layer_norm(nc, K, "ln_ffn0", src=y, affine=cols, affine_d=io["ln_ffn0"], add=True)


STAGES[2] = stage2


def expert_layout(w1, b1, w2):
    n = w1.shape[0]
    return np.concatenate([w1, w2.reshape(n, HJ, P, P).transpose(0, 2, 1, 3).reshape(n, P, HID),
                           b1.reshape(n, HJ, P).transpose(0, 2, 1)], 2)


def stage2_layout(f):
    return {
        "iota": np.broadcast_to(np.arange(16, dtype=np.float32), (P, TOK_TILES, 16)),
        "rc_w1": f["L0_ffn_rc_w1"].transpose(1, 2, 0),
        "rc_w2": f["L0_ffn_rc_w2"].transpose(1, 2, 0),
        "rc_b1": f["L0_ffn_rc_b1"][:, None],
        "rc_b2": np.broadcast_to(f["L0_ffn_rc_b2"], (P, E0)),
        "sh_w1": f["L0_ffn_sh_w1"].transpose(1, 2, 0),
        "sh_w2": f["L0_ffn_sh_w2"][:, :, 0].T.reshape(HJ, P, P).transpose(1, 0, 2),
        "sh_b1": f["L0_ffn_sh_b1"].reshape(HJ, P).T,
        "sh_b2": f["L0_ffn_sh_b2"][:, None],
        "moe0_w": expert_layout(f["L0_ffn_e_w1"], f["L0_ffn_e_b1"], f["L0_ffn_e_w2"]),
        "moe0_b2": f["L0_ffn_e_b2"],
        "ln_ffn0": np.stack([f["L0_ffn_ln_g"], f["L0_ffn_ln_b"]], 1),
    }


E3 = 8


def plain_router(nc, io, K, name, E, w_name, b_name, gates_d, pack):
    zT = K["zT"]
    with ExitStack() as ctx:
        a = Alloc(nc, ctx, name)
        W = E if pack == "sum" else 4 * E
        w = a.sb("w", [P, E])
        bias = a.sb("bias", [P, E])
        lg = a.sb("lg", [P, TOK_TILES, E])
        gates = a.sb("gates", [P, TOK_TILES, W])
        packT = a.sb("packT", [W, B * LP])
        l_ps = a.ps("l_ps", [P, TOK_TILES, E])
        pack_ps = a.ps("pack_ps", [P, 2 * BANK])
        w_in, l_done, lg_ready = (a.sem(n) for n in ("w_in", "l_done", "lg_ready"))
        block = ctx.enter_context(nc.Block())

        @block.sync
        def _(sp):
            sp.dma_start(w[:], io[w_name]).then_inc(w_in, 16)
            if b_name:
                sp.dma_start(bias[:], io[b_name]).then_inc(w_in, 16)

        @block.tensor
        def _(pe):
            pe.wait_ge(w_in, 32 if b_name else 16)
            for b in range(B):
                for t in range(TILES):
                    at = LEAD + b * LP + t * P
                    mm = nc.tensor.matmul(l_ps[:, b * TILES + t, :], zT[:, at:at + P], w[:], start=True, stop=True)
            mm.then_inc(l_done, 1)

        @block.vector
        def _(dve):
            dve.wait_ge(l_done, 1)
            if b_name:
                dve.wait_ge(w_in, 32)
                nc.vector.tensor_tensor(lg[:], l_ps[:], bias[:, :].unsqueeze(1).to_broadcast([P, TOK_TILES, E]),
                                        ALU.add).then_inc(lg_ready, 1)
            else:
                nc.vector.tensor_copy(lg[:], l_ps[:]).then_inc(lg_ready, 1)

        top2_gates(nc, K, a, block, lg, (lg_ready, 1), E, gates, pack, pack_ps, packT, gates_d)


def stage8(nc, io, K, scratch):
    gates_d = nc.dram_tensor("gates3", (E3, B * LP), F32, kind="Internal").ap()
    with ExitStack() as ctx:
        a = Alloc(nc, ctx, "stage8")
        y = a.sb("y", [P, B * L])
        cols = a.sb("ln_cols", [P, 2])
        keep = a.sb("keep", [P, B * LP])
        with ExitStack() as ctx2:
            a2 = Alloc(nc, ctx2, "keepz")
            kept = a2.sem("kept")
            block = ctx2.enter_context(nc.Block())

            @block.vector
            def _(dve):
                nc.vector.tensor_copy(keep[:], K["zT"][:, LEAD:ZW]).then_inc(kept, 1)
                dve.wait_ge(kept, 1)

        layer_norm(nc, K, "ln_in3", affine=cols, affine_d=io["ln_in3"], src="zT")
        plain_router(nc, io, K, "router3", E3, "wg3", None, gates_d, "sum")
        experts(nc, K, scratch, "moe3", E3, ACT.Gelu_apprx_tanh, io["moe3_w"], io["moe3_b2"], gates_d, y)
        with ExitStack() as ctx2:
            a2 = Alloc(nc, ctx2, "resid3")
            done = a2.sem("done")
            block = ctx2.enter_context(nc.Block())

            @block.vector
            def _(dve):
                for b in range(B):
                    yb = y[:, b * L:(b + 1) * L]
                    nc.vector.tensor_tensor(yb, yb, keep[:, b * LP:b * LP + L], ALU.add).then_inc(done, 1)
                dve.wait_ge(done, B)
        layer_norm(nc, K, "ln_out3", src=y, affine=cols, affine_d=io["ln_out3"], add=True)


STAGES[8] = stage8


def stage8_layout(f):
    return {
        "wg3": f["L3_ffn_Wg"],
        "moe3_w": expert_layout(f["L3_ffn_W1"], f["L3_ffn_b1"], f["L3_ffn_W2"]),
        "moe3_b2": f["L3_ffn_b2"],
        "ln_in3": np.stack([f["L3_ffn_ln_g"], f["L3_ffn_ln_b"]], 1),
        "ln_out3": np.stack([f["L3_ffn_out_g"], f["L3_ffn_out_b"]], 1),
    }

def dense_attention(nc, io, K, name, R, w_name, b_name, scale):
    hT, zT = K["hT"], K["zT"]
    with ExitStack() as ctx:
        a = Alloc(nc, ctx, name)
        w = a.sb("w", [P, 2, R])
        bias = a.sb("bias", [R, 2])
        zb = a.sb("zb", [P, LP])
        z_tok = a.sb("z_tok", [P, TILES, P])
        qk = [a.sb(f"qk{j}", [R, LP]) for j in range(2)]
        probs = [a.sb(f"probs{i}", [P, LP]) for i in range(2)]
        probsT = a.sb("probsT", [P, TILES, LP])
        nmax = a.sb("nmax", [P, TILES])
        sums = a.sb("sums", [P, TILES])
        rsum = a.sb("rsum", [P, TILES])
        s_ps = [a.ps(f"s_ps{i}", [P, 2 * BANK]) for i in range(2)]
        t_ps = a.ps("t_ps", [P, 2 * BANK])
        o_ps = [a.ps(f"o_ps{i}", [P, BANK]) for i in range(2)]
        names = ("w_in", "filled", "zb_ready", "p_full", "p_copied", "zt_full", "zt_copied", "s_full", "max_ready", "exp_done",
                 "rs_ready", "scaled", "t_full", "t_copied", "o_full", "o_added")
        (w_in, filled, zb_ready, p_full, p_copied, zt_full, zt_copied, s_full, max_ready, exp_done,
         rs_ready, scaled, t_full, t_copied, o_full, o_added) = (a.sem(n) for n in names)
        block = ctx.enter_context(nc.Block())
        T = TILES

        @block.sync
        def _(sp):
            sp.dma_start(w[:], io[w_name]).then_inc(w_in, 16)
            if b_name:
                sp.dma_start(bias[:], io[b_name]).then_inc(w_in, 16)

        @block.tensor
        def _(pe):
            pe.wait_ge(w_in, 32 if b_name else 16)
            with pe.Fori(0, B) as b:
                pe.wait_ge(zb_ready, b + 1)
                for j in range(2):
                    for half in range(2):
                        if j == 0:
                            pe.wait_ge(o_added, b * 2 + (half + 1))
                        else:
                            pe.wait_ge(p_copied, b * 4 + (half + 1))
                        nc.tensor.matmul(o_ps[half][0:R, 0:HALF], w[:, j, :], zb[:, half * HALF:half * HALF + HALF],
                                         start=True, stop=True).then_inc(p_full, 1)
                pe.wait_ge(t_copied, b * T + 1)
                for t in range(T):
                    mm = nc.tensor.transpose(t_ps[:, t * P:(t + 1) * P], zb[:, t * P:(t + 1) * P], K["ident"][:])
                mm.then_inc(zt_full, 1)
                pe.wait_ge(p_copied, b * 4 + 4)
                for t in range(T + 1):
                    if t < T:
                        pe.wait_ge(exp_done, b * T + (t + 1))
                        nc.tensor.matmul(s_ps[t % 2][:, 0:BANK], qk[0][:, t * P:(t + 1) * P], qk[1][:, 0:BANK],
                                         start=True, stop=True)
                        nc.tensor.matmul(s_ps[t % 2][:, BANK:L], qk[0][:, t * P:(t + 1) * P], qk[1][:, BANK:L],
                                         start=True, stop=True).then_inc(s_full, 1)
                    if t >= 1:
                        i = t - 1
                        pe.wait_ge(scaled, b * T + (i + 1))
                        if i == 0:
                            pe.wait_ge(zt_copied, b + 1)
                        else:
                            pe.wait_ge(t_copied, b * T + (i + 1))
                        for j in range(T):
                            mm = nc.tensor.transpose(t_ps[:, j * P:(j + 1) * P], probs[i % 2][:, j * P:(j + 1) * P],
                                                     K["ident"][:])
                        mm.then_inc(t_full, 1)
                pe.wait_ge(t_copied, b * T + (T + 1))
                for half in range(2):
                    for j in range(T):
                        mm = nc.tensor.matmul(o_ps[half][:, 0:HALF], z_tok[:, j, :],
                                              probsT[:, j, half * HALF:half * HALF + HALF], start=(j == 0), stop=(j == T - 1))
                    mm.then_inc(o_full, 1)

        def copy_turned(eng, copy, b, t):
            eng.wait_ge(t_full, b * T + (t + 1))
            copy(probsT[:, :, t * P:(t + 1) * P], t_ps[:, 0:LP].rearrange("p (j i) -> p j i", j=T)).then_inc(t_copied, 1)

        @block.scalar
        def _(act):
            act.sem_inc(exp_done, 2)
            act.wait_ge(filled, 4)
            with act.Fori(0, B) as b:
                for t in range(T):
                    act.wait_ge(max_ready, b * T + (t + 1))
                    act.wait_ge(t_full, b * T + (t + 1 - 2)) if t >= 2 else act.wait_ge(o_full, b * 2 + 2)
                    nc.scalar.activation(probs[t % 2][:, 0:L], s_ps[t % 2][:, 0:L], ACT.Exp, bias=nmax[:, t:t + 1],
                                         accum_out=sums[:, t:t + 1]).then_inc(exp_done, 1)
                    if t >= 1 and t % 2 == 0:
                        copy_turned(act, nc.scalar.copy, b, t - 1)
                copy_turned(act, nc.scalar.copy, b, T - 1)

        @block.vector
        def _(dve):
            dve.sem_inc(o_added, 2)
            dve.sem_inc(t_copied, 1)
            dve.sem_inc(o_full, 2)
            for x in (probs[0][:, L:LP], probs[1][:, L:LP], qk[0][:, L:LP], bias[:] if not b_name else nmax[:]):
                nc.vector.memset(x, 0.0).then_inc(filled, 1)
            dve.wait_ge(filled, 4)
            dve.wait_ge(w_in, 32 if b_name else 16)
            with dve.Fori(0, B) as b:
                dve.wait_ge(o_full, b * 2 + 2)
                nc.vector.tensor_copy(zb[:], zT[:, bass.ds(b * LP + LEAD, LP)]).then_inc(zb_ready, 1)
                for j in range(2):
                    for half in range(2):
                        dve.wait_ge(p_full, b * 4 + (j * 2 + half + 1))
                        nc.vector.tensor_scalar(qk[j][:, half * HALF:half * HALF + HALF], o_ps[half][0:R, 0:HALF],
                                                bias[:, j:j + 1], (scale, 1.0)[j], ALU.add, ALU.mult).then_inc(p_copied, 1)
                dve.wait_ge(zt_full, b + 1)
                nc.vector.tensor_copy(z_tok[:], t_ps[:, 0:LP].rearrange("p (t c) -> p t c", t=T)).then_inc(zt_copied, 1)
                for t in range(T + 1):
                    if t < T:
                        dve.wait_ge(s_full, b * T + (t + 1))
                        nc.vector.tensor_reduce(nmax[:, t:t + 1], s_ps[t % 2][:, 0:L], AX.X, ALU.max,
                                                negate=True).then_inc(max_ready, 1)
                    if t >= 1:
                        i = t - 1
                        dve.wait_ge(exp_done, b * T + (i + 3))
                        nc.vector.reciprocal(rsum[:, i:i + 1], sums[:, i:i + 1]).then_inc(rs_ready, 1)
                        dve.wait_ge(rs_ready, b * T + (i + 1))
                        nc.vector.tensor_scalar(probs[i % 2][:, 0:L], probs[i % 2][:, 0:L], rsum[:, i:i + 1], None,
                                                ALU.mult).then_inc(scaled, 1)
                        if i % 2 == 0:
                            copy_turned(dve, nc.vector.tensor_copy, b, i)
                for half in range(2):
                    dve.wait_ge(o_full, b * 2 + (half + 3))
                    nc.vector.tensor_tensor(h_chunk(hT, b, half), h_chunk(hT, b, half), o_ps[half][:, 0:HALF],
                                            ALU.add).then_inc(o_added, 1)


STAGES[3] = lambda nc, io, K, scratch: dense_attention(nc, io, K, "attn1", P, "attn1_w", "attn1_b", float(P) ** -0.5)
STAGES[5] = lambda nc, io, K, scratch: dense_attention(nc, io, K, "attn2", 10, "attn2_w", None, 512.0 ** -0.5)


def dense_attention_layout(f):
    return {
        "attn1_w": np.stack([f["L1_attn_Wq"], f["L1_attn_Wk"]], 1),
        "attn1_b": np.stack([f["L1_attn_bq"], f["L1_attn_bk"]], 1),
        "attn2_w": np.stack([f["L2_attn_W1"], f["L2_attn_W2"].T], 1),
    }


E1 = 8
PICKS = 2 * B


def pooled_gates(nc, io, K, weight_cols, expert_at):
    zT = K["zT"]
    with ExitStack() as ctx:
        a = Alloc(nc, ctx, "pool")
        aw = a.sb("aw", [P, 1])
        ab = a.sb("ab", [1, 1])
        gw = a.sb("gw", [P, E1])
        gb = a.sb("gb", [1, E1])
        ones = a.sb("ones", [1, P])
        row = a.sb("row", [1, L])
        mx = a.sb("mx", [1, 4])
        aw_all = a.sb("aw_all", [P, L])
        prod = a.sb("prod", [P, L])
        pooled = a.sb("pooled", [P, B])
        g = a.sb("g", [1, E1])
        best = a.sb("best", [1, 8])
        at = a.sb("at", [1, 8], U32)
        w8 = a.sb("w8", [1, 4])
        wts = a.sb("wts", [1, PICKS])
        s_ps = a.ps("s_ps", [P, 2 * BANK])
        b_ps = a.ps("b_ps", [P, 2 * BANK])
        g_ps = a.ps("g_ps", [P, BANK])
        w_ps = a.ps("w_ps", [P, BANK])
        w_in, s_full, exp_in, exp_done, row_ready, b_full, pooled_ready, g_full, gexp_in, gexp_done, wts_ready, w_full, chain, chain2, filled = (
            a.sem(n) for n in ("w_in", "s_full", "exp_in", "exp_done", "row_ready", "b_full", "pooled_ready", "g_full",
                               "gexp_in", "gexp_done", "wts_ready", "w_full", "chain", "chain2", "filled"))
        block = ctx.enter_context(nc.Block())

        @block.sync
        def _(sp):
            for dst, src in ((aw, "pool_w"), (ab, "pool_b"), (gw, "gate1_w"), (gb, "gate1_b")):
                sp.dma_start(dst[:], io[src]).then_inc(w_in, 16)

        @block.tensor
        def _(pe):
            pe.wait_ge(w_in, 64)
            pe.wait_ge(filled, 1)
            for b in range(B):
                z0 = LEAD + b * LP
                if b >= 1:
                    pe.wait_ge(exp_done, b)
                nc.tensor.matmul(s_ps[0:1, 0:BANK], aw[:], zT[:, z0:z0 + BANK], start=True, stop=True)
                nc.tensor.matmul(s_ps[0:1, BANK:L], aw[:], zT[:, z0 + BANK:z0 + L], start=True, stop=True).then_inc(s_full, 1)
                pe.wait_ge(row_ready, b + 1)
                nc.tensor.matmul(b_ps[:, 0:BANK], ones[:], row[:, 0:BANK], start=True, stop=True)
                nc.tensor.matmul(b_ps[:, BANK:L], ones[:], row[:, BANK:L], start=True, stop=True).then_inc(b_full, 1)
                pe.wait_ge(pooled_ready, b + 1)
                nc.tensor.matmul(g_ps[0:1, 0:E1], pooled[:, b:b + 1], gw[:], start=True, stop=True).then_inc(g_full, 1)
            pe.wait_ge(wts_ready, 1)
            nc.tensor.matmul(w_ps[:, 0:PICKS], ones[:], wts[:], start=True, stop=True).then_inc(w_full, 1)

        @block.scalar
        def _(act):
            for b in range(B):
                act.wait_ge(exp_in, b + 1)
                nc.scalar.activation(row[:], row[:], ACT.Exp, bias=mx[:, 0:1],
                                     accum_out=mx[:, 1:2]).then_inc(exp_done, 1)
                act.wait_ge(gexp_in, b + 1)
                nc.scalar.activation(g[:], g[:], ACT.Exp, bias=mx[:, 2:3], accum_out=mx[:, 3:4]).then_inc(gexp_done, 1)

        @block.vector
        def _(dve):
            nc.vector.memset(ones[:], 1.0).then_inc(filled, 1)
            dve.wait_ge(w_in, 64)
            c = Chain(dve, chain)
            for b in range(B):
                dve.wait_ge(s_full, b + 1)
                c.link(nc.vector.tensor_scalar(row[:], s_ps[0:1, 0:L], ab[:, 0:1], None, ALU.add))
                nc.vector.tensor_reduce(mx[:, 0:1], row[:], AX.X, ALU.max, negate=True).then_inc(exp_in, 1)
                dve.wait_ge(exp_done, b + 1)
                c.link(nc.vector.reciprocal(w8[:, 0:1], mx[:, 1:2]))
                nc.vector.tensor_scalar(row[:], row[:], w8[:, 0:1], None, ALU.mult).then_inc(row_ready, 1)
                dve.wait_ge(b_full, b + 1)
                z0 = LEAD + b * LP
                c.link(nc.vector.tensor_tensor(prod[:], zT[:, z0:z0 + L], b_ps[:, 0:L], ALU.mult))
                nc.vector.reduce_sum(pooled[:, b:b + 1], prod[:], AX.X).then_inc(pooled_ready, 1)
                dve.wait_ge(g_full, b + 1)
                c.link(nc.vector.tensor_tensor(g[:], g_ps[0:1, 0:E1], gb[:], ALU.add))
                nc.vector.tensor_reduce(mx[:, 2:3], g[:], AX.X, ALU.max, negate=True).then_inc(gexp_in, 1)
                dve.wait_ge(gexp_done, b + 1)
                c.link(nc.vector.reciprocal(w8[:, 1:2], mx[:, 3:4]))
                c.link(nc.vector.tensor_scalar(g[:], g[:], w8[:, 1:2], None, ALU.mult))
                c.link(nc.vector.max(best[:], g[:]))
                c.link(nc.vector.max_index(at[:], best[:], g[:]))
                c.link(nc.vector.tensor_copy(expert_at[:, 2 * b:2 * b + 2], at[:, 0:2]))
                c.link(nc.vector.tensor_tensor(w8[:, 2:3], best[:, 0:1], best[:, 1:2], ALU.add))
                c.link(nc.vector.tensor_scalar(w8[:, 2:3], w8[:, 2:3], 1e-9, None, ALU.add))
                c.link(nc.vector.reciprocal(w8[:, 3:4], w8[:, 2:3]))
                c.link(nc.vector.tensor_scalar(wts[:, 2 * b:2 * b + 2], best[:, 0:2], w8[:, 3:4], None, ALU.mult))
            dve.sem_inc(wts_ready, 1)
            dve.wait_ge(w_full, 1)
            c.link(nc.vector.tensor_copy(weight_cols[:], w_ps[:, 0:PICKS]))


def picked_experts(nc, io, K, weight_cols, expert_at):
    hT, zT = K["hT"], K["zT"]
    with ExitStack() as ctx:
        a = Alloc(nc, ctx, "picked")
        WID = 2 * HID + HJ + 1
        w = [a.sb(f"w{i}", [P, WID]) for i in range(2)]
        hid = [a.sb(f"hid{i}", [P, HJ, HALF]) for i in range(2)]
        eo = [a.sb(f"eo{i}", [P, HALF]) for i in range(2)]
        h_ps = [a.ps(f"h_ps{j}", [P, BANK]) for j in range(HJ)]
        o_ps = [a.ps(f"o_ps{i}", [P, BANK]) for i in range(2)]
        w_in = a.sems("w_in", 2)
        h_full, h_done, o_full, eo_done, added, passed = (a.sem(n) for n in ("h_full", "h_done", "o_full", "eo_done", "added", "passed"))
        block = ctx.enter_context(nc.Block())

        @block.sync
        def _(sp):
            for n in range(PICKS):
                if n >= 2:
                    sp.wait_ge(added, 2 * (n - 1))
                e = sp.value_load(expert_at[0:1, n:n + 1], min_val=0, max_val=E1 - 1)
                sp.dma_start(w[n % 2][:], io["moe1_w"][bass.ds(e, 1), :, :].squeeze(0)).then_inc(w_in[n % 2], 16)

        @block.tensor
        def _(pe):
            def first(n, i):
                b, q = n // 2, 2 * n + i
                if i == 0:
                    pe.wait_ge(w_in[n % 2], 16 * (n // 2 + 1))
                for j in range(HJ):
                    if q >= 1:
                        pe.wait_ge(h_done, (q - 1) * HJ + j + 1)
                    at = LEAD + b * LP + i * HALF
                    nc.tensor.matmul(h_ps[j][:, 0:HALF], w[n % 2][:, j * P:(j + 1) * P], zT[:, at:at + HALF],
                                     start=True, stop=True).then_inc(h_full, 1)

            def second(n, i):
                q = 2 * n + i
                pe.wait_ge(h_done, q * HJ + HJ)
                if q >= 2:
                    pe.wait_ge(eo_done, q - 1)
                for j in range(HJ):
                    mm = nc.tensor.matmul(o_ps[i][:, 0:HALF], w[n % 2][:, HID + j * P:HID + (j + 1) * P],
                                          hid[i][:, j, :], start=(j == 0), stop=(j == HJ - 1))
                mm.then_inc(o_full, 1)

            items = [(n, i) for n in range(PICKS) for i in range(2)]
            for x, (n, i) in enumerate(items):
                first(n, i)
                if x >= 1:
                    second(*items[x - 1])
            second(*items[-1])

        @block.scalar
        def _(act):
            def output(q):
                n, i = q // 2, q % 2
                act.wait_ge(o_full, q + 1)
                if q >= 2:
                    act.wait_ge(added, q - 1)
                nc.scalar.activation(eo[i][:], o_ps[i][:, 0:HALF], ACT.Gelu,
                                     bias=w[n % 2][:, 2 * HID + HJ:2 * HID + HJ + 1]).then_inc(eo_done, 1)

            for q in range(2 * PICKS):
                n, i = q // 2, q % 2
                for j in range(HJ):
                    act.wait_ge(h_full, q * HJ + j + 1)
                    nc.scalar.activation(hid[i][:, j, :], h_ps[j][:, 0:HALF], ACT.Gelu,
                                         bias=w[n % 2][:, 2 * HID + j:2 * HID + j + 1]).then_inc(h_done, 1)
                if q >= 1:
                    output(q - 1)
            output(2 * PICKS - 1)

        @block.vector
        def _(dve):
            for q in range(2 * PICKS):
                n, i = q // 2, q % 2
                b = n // 2
                if q >= 2:
                    dve.wait_ge(added, q - 1)
                dve.wait_ge(eo_done, q + 1)
                h = hT[:, b * L + i * HALF:b * L + (i + 1) * HALF]
                nc.vector.scalar_tensor_tensor(out=h, in0=eo[i][:], scalar=weight_cols[:, n:n + 1], in1=h,
                                               op0=ALU.mult, op1=ALU.add).then_inc(added, 1)


def stage4(nc, io, K, scratch):
    with ExitStack() as ctx:
        a = Alloc(nc, ctx, "stage4")
        weight_cols = a.sb("weight_cols", [P, PICKS])
        expert_at = a.sb("expert_at", [1, PICKS], U32)
        pooled_gates(nc, io, K, weight_cols, expert_at)
        picked_experts(nc, io, K, weight_cols, expert_at)


STAGES[4] = stage4


def stage4_layout(f):
    w = expert_layout(f["L1_ffn_w1"], f["L1_ffn_b1"], f["L1_ffn_w2"])
    return {
        "pool_w": f["L1_ffn_attn_w"],
        "pool_b": f["L1_ffn_attn_b"][None, :],
        "gate1_w": f["L1_ffn_gate_w"],
        "gate1_b": f["L1_ffn_gate_b"][None, :],
        "moe1_w": np.concatenate([w, f["L1_ffn_b2"][:, :, None]], 2),
    }

E2 = 8
STEPS = B
GATES = (0, 2, 3, 1)
RING = 6


def recurrent_experts(nc, io, K, gates_d):
    hT, zT = K["hT"], K["zT"]
    with ExitStack() as ctx:
        a = Alloc(nc, ctx, "lstm")
        WID = 4 * P + 4 * P + P + 4
        w = [a.sb(f"w{i}", [P, WID]) for i in range(2)]
        rows = [[a.sb(f"row{i}_{r}", [P, B * LP]) for r in range(4)] for i in range(2)]
        bo = a.sb("bo", [2 * E2, P])
        gT = a.sb("gT", [2 * E2, B * LP])
        xm = [a.sb(f"xm{i}", [P, HALF]) for i in range(4)]
        gate = [[a.sb(f"gate{i}_{g}", [P, HALF]) for g in range(4)] for i in range(2)]
        cell = [a.sb(f"cell{i}", [P, HALF]) for i in range(4)]
        state = [a.sb(f"state{i}", [P, HALF]) for i in range(4)]
        wstate = [a.sb(f"wstate{i}", [P, HALF]) for i in range(4)]
        tc = [a.sb(f"tc{i}", [P, HALF]) for i in range(2)]
        tmp = a.sb("tmp", [P, HALF])
        g_ps = [a.ps(f"g_ps{i}", [P, BANK]) for i in range(RING)]
        o_ps = [a.ps(f"o_ps{i}", [P, BANK]) for i in range(2)]
        w_in = a.sems("w_in", 2)
        names = ("rows_in", "b_full", "b_added", "xm_ready", "g_full", "g_read", "c_ready", "tc_ready", "h_ready",
                 "hw_ready", "o_full", "y_done", "chain")
        (rows_in, b_full, b_added, xm_ready, g_full, g_read, c_ready, tc_ready, h_ready,
         hw_ready, o_full, y_done, chain) = (a.sem(n) for n in names)
        block = ctx.enter_context(nc.Block())

        PER = 4 * STEPS
        ITEMS = 2 * PER
        GPE = 3 * 4 + 4 * (PER - 4)
        GPT = 2 * GPE
        OPT = 2 * 2 * STEPS

        def parts(x):
            q = x % PER
            return x // PER, q // 4, q // 2 % 2, q % 2

        def gates_of(x):
            return GATES[:3] if parts(x)[1] == 0 else GATES

        def g_base(x):
            e, q = x // PER, x % PER
            return e * GPE + (3 * q if q < 4 else 12 + 4 * (q - 4))

        def out_index(e, s, i):
            return e * 2 * STEPS + 2 * s + i

        def cols(s, i):
            return slice(s * LP + i * HALF, s * LP + i * HALF + HALF)

        def h_cols(s, i):
            return hT[:, s * L + i * HALF:s * L + i * HALF + HALF]

        @block.sync
        def _(sp):
            sp.dma_start(bo[:], io["lstm_bo"]).then_inc(rows_in, 16)
            sp.dma_start(gT[:], gates_d[2 * E2:4 * E2, :]).then_inc(rows_in, 16)
            with sp.Fori(0, E2 // 2) as m:
                for e in range(2):
                    sp.wait_ge(y_done, m * OPT + (e * 2 * STEPS + 2 * STEPS))
                    sp.dma_start(w[e][:], io["lstm_w"][bass.ds(m * 2 + e, 1), :, :].squeeze(0)).then_inc(w_in[e], 16)
                    for r in range(4):
                        sp.dma_start(rows[e][r][:], gates_d[bass.ds(m * 2 + (r * E2 + e), 1), :].to_broadcast([P, B * LP])
                                     ).then_inc(w_in[e], 16)

        @block.gpsimd
        def _(pool):
            pool.sem_inc(hw_ready, 4)

            def mask(m, x):
                e, s, k, i = parts(x)
                if x % PER == 0:
                    pool.wait_ge(w_in[e], m * 80 + 80)
                back = g_base(x - 4) + len(gates_of(x - 4))
                pool.wait_ge(g_full, m * GPT + (back + GPT))
                nc.gpsimd.tensor_tensor(xm[x % 4][:], zT[:, LEAD + s * LP + i * HALF:LEAD + s * LP + i * HALF + HALF],
                                        rows[e][k][:, cols(s, i)], ALU.mult).then_inc(xm_ready, 1)

            def weigh(m, x):
                e, s, k, i = parts(x)
                pool.wait_ge(h_ready, m * ITEMS + (x + 3))
                pool.wait_ge(o_full, m * OPT + (out_index(e, s, i) + 1))
                nc.gpsimd.tensor_tensor(wstate[2 * k + i][:], state[2 * k + i][:], rows[e][2 + k][:, cols(s, i)],
                                        ALU.mult).then_inc(hw_ready, 1)

            with pool.Fori(0, E2 // 2) as m:
                mask(m, 0)
                mask(m, 1)
                for x in range(ITEMS):
                    if x + 2 < ITEMS:
                        mask(m, x + 2)
                    if x >= 1:
                        weigh(m, x - 1)
                weigh(m, ITEMS - 1)

        @block.tensor
        def _(pe):
            pe.wait_ge(rows_in, 32)
            for c, (b, half) in enumerate(CHUNKS):
                if c >= 2:
                    pe.wait_ge(b_added, c - 1)
                nc.tensor.matmul(o_ps[c % 2][:, 0:HALF], bo[:], gT[:, cols(b, half)], start=True, stop=True).then_inc(b_full, 1)
            pe.wait_ge(b_added, NCH)

            def gates(m, x):
                e, s, k, i = parts(x)
                if x % PER == 0:
                    pe.wait_ge(w_in[e], m * 80 + 80)
                pe.wait_ge(xm_ready, m * ITEMS + (x + 1))
                for y, g in enumerate(gates_of(x)):
                    n = g_base(x) + y
                    bank = g_ps[n % RING][:, 0:HALF]
                    pe.wait_ge(g_read, m * GPT + (n + 1))
                    mm = nc.tensor.matmul(bank, w[e][:, g * P:(g + 1) * P], xm[x % 4][:], start=True, stop=(s == 0))
                    if s > 0:
                        if y == 0:
                            pe.wait_ge(h_ready, m * ITEMS + (x - 4 + 3))
                        mm = nc.tensor.matmul(bank, w[e][:, 4 * P + g * P:4 * P + (g + 1) * P], state[2 * k + i][:],
                                              start=False, stop=True)
                    mm.then_inc(g_full, 1)

            def output(m, e, s, i):
                n = out_index(e, s, i)
                pe.wait_ge(hw_ready, m * ITEMS + (e * PER + 4 * s + 2 + i + 5))
                pe.wait_ge(y_done, m * OPT + (n + OPT - 1))
                for k in range(2):
                    mm = nc.tensor.matmul(o_ps[i][:, 0:HALF], w[e][:, 8 * P:9 * P], wstate[2 * k + i][:],
                                          start=(k == 0), stop=(k == 1))
                mm.then_inc(o_full, 1)

            with pe.Fori(0, E2 // 2) as m:
                for x in range(ITEMS):
                    gates(m, x)
                    if x >= 4 and x % 4 < 2:
                        e, s, k, i = parts(x - 4)
                        output(m, e, s, i)
                for i in range(2):
                    output(m, 1, STEPS - 1, i)

        @block.scalar
        def _(act):
            act.sem_inc(g_read, RING)
            act.sem_inc(tc_ready, 4)

            def squash(m, x):
                act.wait_ge(c_ready, m * ITEMS + (x + 1))
                nc.scalar.activation(tc[x % 2][:], cell[x % 4][:], ACT.Tanh).then_inc(tc_ready, 1)

            with act.Fori(0, E2 // 2) as m:
                for x in range(ITEMS):
                    e, s, k, i = parts(x)
                    act.wait_ge(h_ready, m * ITEMS + (x + 1))
                    for y, g in enumerate(gates_of(x)):
                        n = g_base(x) + y
                        act.wait_ge(g_full, m * GPT + (n + 1 + GPT))
                        nc.scalar.activation(gate[x % 2][g][:], g_ps[n % RING][:, 0:HALF], ACT.Tanh if g == 2 else ACT.Sigmoid,
                                             bias=w[e][:, 9 * P + g:9 * P + g + 1]).then_inc(g_read, 1)
                    if x >= 1:
                        squash(m, x - 1)
                squash(m, ITEMS - 1)

        @block.vector
        def _(dve):
            dve.sem_inc(g_full, GPT)
            dve.sem_inc(h_ready, 2)
            dve.sem_inc(o_full, 2)
            dve.sem_inc(y_done, OPT)
            for c, (b, half) in enumerate(CHUNKS):
                dve.wait_ge(b_full, c + 1)
                h = h_cols(b, half)
                nc.vector.tensor_tensor(h, h, o_ps[c % 2][:, 0:HALF], ALU.add).then_inc(b_added, 1)
            dve.wait_ge(b_added, NCH)

            def cells(m, x, c):
                e, s, k, i = parts(x)
                dve.wait_ge(g_read, m * GPT + (g_base(x) + len(gates_of(x)) + RING))
                dve.wait_ge(tc_ready, m * ITEMS + (x + 1))
                g = gate[x % 2]
                if s == 0:
                    nc.vector.tensor_tensor(cell[x % 4][:], g[0][:], g[2][:], ALU.mult).then_inc(c_ready, 1)
                else:
                    nc.vector.tensor_tensor(cell[x % 4][:], g[1][:], cell[x % 4][:], ALU.mult)
                    c.link(nc.vector.tensor_tensor(tmp[:], g[0][:], g[2][:], ALU.mult))
                    nc.vector.tensor_tensor(cell[x % 4][:], cell[x % 4][:], tmp[:], ALU.add).then_inc(c_ready, 1)

            def states(m, x):
                e, s, k, i = parts(x)
                dve.wait_ge(tc_ready, m * ITEMS + (x + 5))
                dve.wait_ge(hw_ready, m * ITEMS + (x + 1))
                nc.vector.tensor_tensor(state[x % 4][:], gate[x % 2][3][:], tc[x % 2][:], ALU.mult).then_inc(h_ready, 1)

            def add(m, e, s, i):
                n = out_index(e, s, i)
                dve.wait_ge(o_full, m * OPT + (n + 3))
                h = h_cols(s, i)
                nc.vector.tensor_tensor(h, h, o_ps[i][:, 0:HALF], ALU.add).then_inc(y_done, 1)

            with dve.Fori(0, E2 // 2) as m:
                c = Chain(dve, chain, m, 2 * (PER - 4))
                for x in range(ITEMS):
                    cells(m, x, c)
                    if x >= 1:
                        states(m, x - 1)
                    if x >= 5 and x % 4 in (1, 2):
                        e, s, k, i = parts(x - 5)
                        add(m, e, s, i)
                states(m, ITEMS - 1)
                for i in range(2):
                    add(m, 1, STEPS - 1, i)
                c.end()


def stage6(nc, io, K, scratch):
    gates_d = nc.dram_tensor("gates2", (4 * E2, B * LP), F32, kind="Internal").ap()
    plain_router(nc, io, K, "router2", E2, "router2_w", "router2_b", gates_d, "slots")
    recurrent_experts(nc, io, K, gates_d)


STAGES[6] = stage6


def stage6_layout(f):
    return {
        "router2_w": f["L2_ffn_router_w"],
        "router2_b": np.broadcast_to(f["L2_ffn_router_b"], (P, E2)),
        "lstm_w": np.concatenate([f["L2_ffn_Wi"], f["L2_ffn_Wh"], f["L2_ffn_Wo"],
                                  f["L2_ffn_b"].reshape(E2, 4, P).transpose(0, 2, 1)], 2),
        "lstm_bo": np.concatenate([f["L2_ffn_bo"], f["L2_ffn_bo"]], 0),
    }


HEADS3 = 16
D3 = P // 4
GROUPS = 4
HPG = HEADS3 // GROUPS
WM = 3 * P + 2


def causal_weights(nc, io, K, merged_d):
    with ExitStack() as ctx:
        a = Alloc(nc, ctx, "causw")
        wl = a.sb("wl", [P, HEADS3, P])
        bl = a.sb("bl", [P, HEADS3])
        wqkv = a.sb("wqkv", [P, HEADS3, 3 * D3])
        wo = a.sb("wo", [P, GROUPS, P])
        bo = a.sb("bo", [P, 1])
        merged = a.sb("merged", [P, GROUPS, WM])
        bv = a.sb("bv", [P, GROUPS])
        shift = a.sb("shift", [P, 1])
        m_ps = [a.ps(f"m_ps{g}", [P, BANK]) for g in range(GROUPS)]
        b_ps = [a.ps(f"b_ps{j}", [P, BANK]) for j in range(3)]
        o_ps = a.ps("o_ps", [P, BANK])
        w_in, m_full, b_full, m_copied, bv_ready, o_full, shifted, stored, chain = (a.sem(n) for n in (
            "w_in", "m_full", "b_full", "m_copied", "bv_ready", "o_full", "shifted", "stored", "chain"))
        block = ctx.enter_context(nc.Block())

        @block.sync
        def _(sp):
            for dst, src in ((wl, "caus_wl"), (bl, "caus_bl"), (wqkv, "caus_wqkv"), (wo, "caus_wo"), (bo, "caus_bo")):
                sp.dma_start(dst[:], io[src]).then_inc(w_in, 16)
            sp.wait_ge(m_copied, GROUPS + 2)
            sp.dma_start(merged_d.rearrange("g p w -> p g w"), merged[:]).then_inc(stored, 16)
            sp.wait_ge(stored, 16)

        @block.tensor
        def _(pe):
            pe.wait_ge(w_in, 80)
            for g in range(GROUPS):
                for hh in range(HPG):
                    h = g * HPG + hh
                    mm = nc.tensor.matmul(m_ps[g][:, hh * 3 * D3:(hh + 1) * 3 * D3], wl[:, h, :], wqkv[:, h, :],
                                          start=True, stop=True)
                mm.then_inc(m_full, 1)
            for j in range(3):
                for h in range(HEADS3):
                    g, hh = h // HPG, h % HPG
                    mm = nc.tensor.matmul(b_ps[j][hh * D3:(hh + 1) * D3, g:g + 1], wqkv[:, h, j * D3:(j + 1) * D3],
                                          bl[:, h:h + 1], start=True, stop=True)
                mm.then_inc(b_full, 1)
            pe.wait_ge(bv_ready, 1)
            for g in range(GROUPS):
                mm = nc.tensor.matmul(o_ps[:, 0:1], wo[:, g, :], bv[:, g:g + 1], start=(g == 0), stop=(g == GROUPS - 1))
            mm.then_inc(o_full, 1)

        @block.vector
        def _(dve):
            for g in range(GROUPS):
                dve.wait_ge(m_full, g + 1)
                nc.vector.tensor_copy(merged[:, g, 0:3 * P].rearrange("p (j h d) -> p h j d", j=3, h=HPG),
                                      m_ps[g][:, 0:3 * P].rearrange("p (h j d) -> p h j d", h=HPG, j=3)).then_inc(m_copied, 1)
            dve.wait_ge(b_full, 3)
            for j in range(2):
                nc.vector.tensor_copy(merged[:, :, 3 * P + j:3 * P + j + 1], b_ps[j][:, 0:GROUPS].unsqueeze(2)).then_inc(m_copied, 1)
            nc.vector.tensor_copy(bv[:], b_ps[2][:, 0:GROUPS]).then_inc(bv_ready, 1)
            dve.wait_ge(o_full, 1)
            dve.wait_ge(w_in, 80)
            nc.vector.tensor_tensor(shift[:], o_ps[:, 0:1], bo[:], ALU.add).then_inc(chain, 1)
            dve.wait_ge(chain, 1)
            nc.vector.tensor_scalar(K["hT"][:], K["hT"][:], shift[:, 0:1], None, ALU.add).then_inc(shifted, 1)


def causal_attention(nc, io, K, merged_d):
    hT, zT = K["hT"], K["zT"]
    with ExitStack() as ctx:
        a = Alloc(nc, ctx, "caus")
        T = TILES
        W = [min((t + 1) * P, L) for t in range(T)]
        wm = [a.sb(f"wm{i}", [P, WM]) for i in range(2)]
        wo = [a.sb(f"wo{i}", [P, P]) for i in range(2)]
        identb = a.sb("identb", [P, P], BF16)
        mask32 = a.sb("mask32", [P, P])
        mask = a.sb("mask", [P, P], BF16)
        zb = a.sb("zb", [P, LP])
        q_sb = a.sb("q_sb", [P, LP])
        k_sb = a.sb("k_sb", [P, LP])
        v_tok = a.sb("v_tok", [P, T, P])
        probs = [a.sb(f"probs{i}", [P, LP]) for i in range(2)]
        probsT = [a.sb(f"probsT{i}", [P, T, LP]) for i in range(2)]
        nmax = a.sb("nmax", [P, HPG * T])
        sums = a.sb("sums", [P, HPG * T])
        rsum = a.sb("rsum", [P, HPG * T])
        f_tok = a.sb("f_tok", [P, T, P])
        fT = a.sb("fT", [P, LP])
        s_ps = [a.ps(f"s_ps{i}", [P, 2 * BANK]) for i in range(2)]
        t_ps = a.ps("t_ps", [P, 2 * BANK])
        f_ps = [a.ps(f"f_ps{i}", [P, BANK]) for i in range(2)]
        w_in = a.sems("w_in", 2)
        passed = a.sem("passed")
        names = ("masks_in", "filled", "zb_ready", "qk_full", "qk_copied", "v_full", "v_copied", "s_full", "max_ready",
                 "exp_done", "t_full", "t_copied", "f_full", "rs_ready", "f_copied", "ft_full", "ft_copied", "o_full", "h_added")
        (masks_in, filled, zb_ready, qk_full, qk_copied, v_full, v_copied, s_full, max_ready,
         exp_done, t_full, t_copied, f_full, rs_ready, f_copied, ft_full, ft_copied, o_full, h_added) = (a.sem(n) for n in names)
        block = ctx.enter_context(nc.Block())
        X = HPG * T
        DELAY = 2

        def turns(eng, body):
            with eng.Fori(0, B) as b:
                with eng.Fori(0, GROUPS // 2) as m:
                    for slot in range(2):
                        body(b, m, slot, b * GROUPS + m * 2 + slot, b * (GROUPS // 2) + m)

        @block.sync
        def _(sp):
            sp.dma_start(mask32[:], io["causal_mask"]).then_inc(masks_in, 16)

            def body(b, m, slot, n, use):
                sp.wait_ge(h_added, n + 1)
                sp.dma_start(wm[slot][:], merged_d[bass.ds(m * 2 + slot, 1), :, :].squeeze(0)).then_inc(w_in[slot], 16)
                sp.dma_start(wo[slot][:], io["caus_wo_g"][bass.ds(m * 2 + slot, 1), :, :].squeeze(0)).then_inc(w_in[slot], 16)

            turns(sp, body)

        @block.tensor
        def _(pe):
            pe.wait_ge(filled, 6)

            def body(b, m, slot, n, use):
                w = wm[slot]
                pe.wait_ge(w_in[slot], use * 32 + 32)
                pe.wait_ge(zb_ready, n + 1)
                pe.wait_ge(h_added, n + 2)
                for j in range(2):
                    nc.tensor.matmul(s_ps[j][:, 0:BANK], w[:, j * P:(j + 1) * P], zb[:, 0:BANK], start=True, stop=True)
                    nc.tensor.matmul(s_ps[j][:, BANK:L], w[:, j * P:(j + 1) * P], zb[:, BANK:L], start=True,
                                     stop=True).then_inc(qk_full, 1)
                pe.wait_ge(ft_copied, n + 1)
                for t in range(T):
                    mm = nc.tensor.matmul(t_ps[:, t * P:(t + 1) * P], zb[:, t * P:(t + 1) * P], w[:, 2 * P:3 * P],
                                          start=True, stop=True)
                mm.then_inc(v_full, 1)
                pe.wait_ge(qk_copied, n * 2 + 2)

                def scores(x):
                    hh, t = x // T, x % T
                    rows = slice(hh * D3, (hh + 1) * D3)
                    s = s_ps[x % 2]
                    if x >= 2:
                        pe.wait_ge(exp_done, n * X + (x - 1))
                    for c0 in range(0, W[t], BANK):
                        c1 = min(c0 + BANK, W[t])
                        diag = c0 <= t * P < c1
                        mm = nc.tensor.matmul(s[:, c0:c1], q_sb[rows, t * P:(t + 1) * P], k_sb[rows, c0:c1],
                                              start=True, stop=not diag, tile_position=(hh * D3, 0))
                        if diag:
                            mm = nc.tensor.matmul(s[:, t * P:W[t]], identb[:], mask[:, 0:W[t] - t * P],
                                                  start=False, stop=True)
                    mm.then_inc(s_full, 1)

                def turn_probs(x):
                    hh, t = x // T, x % T
                    pe.wait_ge(exp_done, n * X + (x + 1))
                    if x == 0:
                        pe.wait_ge(v_copied, n + 1)
                    else:
                        pe.wait_ge(t_copied, n * X + x)
                    for j in range(t + 1):
                        mm = nc.tensor.transpose(t_ps[:, j * P:(j + 1) * P], probs[x % 2][:, j * P:(j + 1) * P], K["ident"][:])
                    mm.then_inc(t_full, 1)

                def values(hh):
                    pe.wait_ge(t_copied, n * X + (hh * T + T))
                    pe.wait_ge(f_copied, n * HPG + (hh + 1))
                    for t in range(T):
                        for j in range(t + 1):
                            mm = nc.tensor.matmul(f_ps[hh % 2][:, t * D3:(t + 1) * D3], probsT[hh % 2][:, t, j * P:(j + 1) * P],
                                                  v_tok[:, j, hh * D3:(hh + 1) * D3], start=(j == 0), stop=(j == t))
                    mm.then_inc(f_full, 1)

                for x in range(X):
                    scores(x)
                    if x >= 1:
                        turn_probs(x - 1)
                    if x >= T + DELAY and (x - DELAY) % T == 0:
                        values((x - DELAY) // T - 1)
                turn_probs(X - 1)
                values(HPG - 1)
                pe.wait_ge(f_copied, n * HPG + (HPG + 2))
                for t in range(T):
                    mm = nc.tensor.transpose(t_ps[:, t * P:(t + 1) * P], f_tok[:, t, :], K["ident"][:])
                mm.then_inc(ft_full, 1)
                pe.wait_ge(ft_copied, n + 2)
                nc.tensor.matmul(s_ps[0][:, 0:BANK], wo[slot][:], fT[:, 0:BANK], start=True, stop=True)
                nc.tensor.matmul(s_ps[0][:, BANK:L], wo[slot][:], fT[:, BANK:L], start=True, stop=True).then_inc(o_full, 1)

            turns(pe, body)

        def copy_turned(eng, copy, n, x):
            hh, t = x // T, x % T
            if t < 2:
                eng.wait_ge(f_full, n * HPG + (hh + 1))
            eng.wait_ge(t_full, n * X + (x + 1))
            w = (t + 1) * P
            copy(probsT[hh % 2][:, t, 0:w], t_ps[:, 0:w]).then_inc(t_copied, 1)

        @block.scalar
        def _(act):
            act.wait_ge(filled, 6)

            def body(b, m, slot, n, use):
                for j, dst in ((0, q_sb), (1, k_sb)):
                    act.wait_ge(qk_full, n * 2 + (j + 1))
                    nc.scalar.activation(dst[:, 0:L], s_ps[j][:, 0:L], ACT.Identity,
                                         bias=wm[slot][:, 3 * P + j:3 * P + j + 1]).then_inc(qk_copied, 1)
                for x in range(X):
                    act.wait_ge(max_ready, n * X + (x + 1))
                    if x >= 2:
                        act.wait_ge(t_full, n * X + (x - 1))
                    if x == 0:
                        act.wait_ge(f_copied, n * HPG + 2)
                        act.wait_ge(h_added, n + 2)
                    w = W[x % T]
                    nc.scalar.activation(probs[x % 2][:, 0:w], s_ps[x % 2][:, 0:w], ACT.Exp, bias=nmax[:, x:x + 1],
                                         accum_out=sums[:, x:x + 1]).then_inc(exp_done, 1)
                    if x >= 1 and x % 2 == 0:
                        copy_turned(act, nc.scalar.copy, n, x - 1)
                copy_turned(act, nc.scalar.copy, n, X - 1)
                act.wait_ge(ft_full, n + 1)
                nc.scalar.copy(fT[:], t_ps[:, 0:LP]).then_inc(ft_copied, 1)

            turns(act, body)

        @block.vector
        def _(dve):
            dve.sem_inc(h_added, 2)
            dve.sem_inc(ft_copied, 1)
            dve.sem_inc(f_copied, 2)
            dve.sem_inc(f_full, 2)
            for x in (probs[0], probs[1], q_sb, k_sb):
                nc.vector.memset(x[:], 0.0).then_inc(filled, 1)
            nc.vector.tensor_copy(identb[:], K["ident"][:]).then_inc(filled, 1)
            dve.wait_ge(masks_in, 16)
            nc.vector.tensor_copy(mask[:], mask32[:]).then_inc(filled, 1)
            dve.wait_ge(filled, 6)

            def body(b, m, slot, n, use):
                nc.vector.tensor_copy(zb[:], zT[:, bass.ds(b * LP + LEAD, LP)]).then_inc(zb_ready, 1)
                dve.wait_ge(v_full, n + 1)
                nc.vector.tensor_copy(v_tok[:], t_ps[:, 0:LP].rearrange("p (t c) -> p t c", t=T)).then_inc(v_copied, 1)

                def heads(hh):
                    cols = slice(hh * T, (hh + 1) * T)
                    dve.wait_ge(exp_done, n * X + (hh * T + T))
                    nc.vector.reciprocal(rsum[:, cols], sums[:, cols]).then_inc(rs_ready, 1)
                    dve.wait_ge(rs_ready, n * HPG + (hh + 1))
                    dve.wait_ge(f_full, n * HPG + (hh + 3))
                    nc.vector.tensor_tensor(f_tok[:, :, hh * D3:(hh + 1) * D3],
                                            f_ps[hh % 2][:, 0:T * D3].rearrange("p (t d) -> p t d", t=T),
                                            rsum[:, cols].unsqueeze(2).to_broadcast([P, T, D3]), ALU.mult).then_inc(f_copied, 1)

                for x in range(X):
                    dve.wait_ge(s_full, n * X + (x + 1))
                    nc.vector.tensor_reduce(nmax[:, x:x + 1], s_ps[x % 2][:, 0:W[x % T]], AX.X, ALU.max,
                                            negate=True).then_inc(max_ready, 1)
                    if x >= 1 and x % 2 == 1:
                        copy_turned(dve, nc.vector.tensor_copy, n, x - 1)
                    if x >= T + DELAY + 1 and (x - DELAY - 1) % T == 0:
                        heads((x - DELAY - 1) // T - 1)
                heads(HPG - 1)
                dve.wait_ge(o_full, n + 1)
                h = hT[:, bass.ds(b * L, L)]
                nc.vector.tensor_tensor(h, h, s_ps[0][:, 0:L], ALU.add).then_inc(h_added, 1)
                dve.wait_ge(h_added, n + 3)
                apart(dve, passed)

            turns(dve, body)


def stage7(nc, io, K, scratch):
    merged_d = nc.dram_tensor("merged", (GROUPS, P, WM), F32, kind="Internal").ap()
    causal_weights(nc, io, K, merged_d)
    causal_attention(nc, io, K, merged_d)


STAGES[7] = stage7


def stage7_layout(f):
    qkv = np.concatenate([f["L3_attn_Wq"], f["L3_attn_Wk"], f["L3_attn_Wv"]], 2)
    wo = f["L3_attn_Wo"].T.reshape(GROUPS, P, P)
    late = np.arange(P)[None, :] > np.arange(P)[:, None]
    return {
        "caus_wl": f["L3_attn_Wl"].transpose(1, 0, 2),
        "caus_bl": f["L3_attn_bl"].T,
        "caus_wqkv": qkv.transpose(1, 0, 2),
        "caus_wo": wo.transpose(1, 0, 2),
        "caus_wo_g": wo,
        "caus_bo": f["L3_attn_bo"][:, None],
        "causal_mask": np.where(late, -1e30, 0.0).astype(np.float32),
    }


def laid_out(inputs):
    f = {k: np.asarray(v) for k, v in inputs.items()}
    io = {
        "ident": np.eye(P, dtype=np.float32),
        "mean_all": np.full((P, P), 1.0 / P, np.float32),
        "x": f["x"].transpose(2, 0, 1).reshape(P, B * S_IN),
        "tok_w": f["L0_tok_W"].reshape(P, CONTEXT, P).transpose(2, 1, 0),
        "tok_cols": np.stack([f["L0_tok_b"], f["L0_tok_gamma"], f["L0_tok_beta"]], 1),
    }
    for more in LAYOUTS:
        io.update(more(f))
    return {k: np.ascontiguousarray(v) for k, v in io.items()}


LAYOUTS = [stage1_layout, stage2_layout, stage8_layout, dense_attention_layout, stage4_layout,
           stage6_layout, stage7_layout]


def kernel(**inputs):
    import concourse.bacc as _bacc
    from concourse.bass_utils import run_bass_kernel_spmd as _run

    nc = _bacc.Bacc("TRN2", target_bir_lowering=False, num_devices=1)
    arrays, io = {}, {}
    for name, v in laid_out(inputs).items():
        arrays[f"in_{name}"] = v
        io[name] = nc.dram_tensor(f"in_{name}", v.shape, mybir.dt.from_np(v.dtype), kind="ExternalInput").ap()
    out = nc.dram_tensor("out_h", (P, B * L), F32, kind="ExternalOutput").ap()
    scratch = {}
    audio_tower(nc, io, out, scratch)
    r = _run(nc, [arrays], core_ids=[0])
    return r.results[0]["out_h"].reshape(P, B, L).transpose(1, 2, 0)
```

```python
from contextlib import ExitStack

import numpy as np

import concourse.bass as bass
from concourse import mybir

ALU = mybir.AluOpType
ACT = mybir.ActivationFunctionType
AX = mybir.AxisListType
F32 = mybir.dt.float32
BF16 = mybir.dt.bfloat16
U32 = mybir.dt.uint32

P = 128
B = 4
S_IN = 750
CONTEXT = 5
L = S_IN - CONTEXT + 1
HALF = L // 2
CHUNKS = [(b, half) for b in range(B) for half in range(2)]
TILES = -(-L // P)
LP = TILES * P
LEAD = 8
ZW = LEAD + B * LP
BANK = 512



class Chain:

    def __init__(self, eng, sem, turn=0, per_turn=0):
        self.eng, self.sem, self.base, self.per_turn, self.n = eng, sem, turn * per_turn, per_turn, 0

    def link(self, ins):
        self.n += 1
        ins.then_inc(self.sem, 1)
        self.eng.wait_ge(self.sem, self.base + self.n)

    def end(self):
        assert self.n == self.per_turn, (self.n, self.per_turn)


def apart(eng, passed):
    eng.sem_inc(passed, 1)


class Alloc:

    def __init__(self, nc, ctx, stage):
        self.nc, self.ctx, self.stage = nc, ctx, stage
        self.used = []
        ctx.callback(self.clear)

    def clear(self):
        if self.used:
            numbers = sorted(s.num for s in self.used)
            first = numbers[0]
            for n, after in zip(numbers, numbers[1:] + [None]):
                if after != n + 1:
                    self.nc.gpsimd.sem_clear(range(first, n + 1))
                    first = after
            self.nc.all_engine_barrier()

    def sb(self, name, shape, dt=F32):
        return self.ctx.enter_context(self.nc.sbuf_tensor(f"{self.stage}_{name}", shape, dt))

    def ps(self, name, shape, dt=F32):
        return self.ctx.enter_context(self.nc.psum_tensor(f"{self.stage}_{name}", shape, dt))

    def sem(self, name):
        self.used.append(self.ctx.enter_context(self.nc.semaphore(f"{self.stage}_{name}")))
        return self.used[-1]

    def sems(self, name, n):
        return [self.sem(f"{name}{i}") for i in range(n)]


def h_chunk(hT, b, half):
    return hT[:, bass.ds(b * L + half * HALF, HALF)]


def z_chunk(zT, b, half, shift=0):
    return zT[:, bass.ds(b * LP + (half * HALF + LEAD + shift), HALF)]


def load_constants(nc, io, K):
    with ExitStack() as ctx:
        a = Alloc(nc, ctx, "const")
        loaded = a.sem("loaded")
        filled = a.sem("filled")
        block = ctx.enter_context(nc.Block())

        @block.sync
        def _(sp):
            sp.dma_start(K["ident"][:], io["ident"]).then_inc(loaded, 16)
            sp.dma_start(K["mean_all"][:], io["mean_all"]).then_inc(loaded, 16)
            sp.wait_ge(loaded, 32)

        @block.vector
        def _(dve):
            nc.vector.memset(K["zT"][:], 0.0).then_inc(filled, 1)
            nc.vector.memset(K["eps5"][:], 1e-5).then_inc(filled, 1)
            nc.vector.memset(K["eps4"][:], 1e-4).then_inc(filled, 1)
            dve.wait_ge(filled, 3)


def token_conv(nc, io, K):
    hT = K["hT"]
    with ExitStack() as ctx:
        a = Alloc(nc, ctx, "tok")
        x = a.sb("x", [P, B * S_IN])
        w = a.sb("w", [P, CONTEXT, P])
        cols = a.sb("cols", [P, 3])
        stats = a.sb("stats", [P, 2 * B * 6])
        mv = a.sb("mv", [P, 2])
        s = a.sb("s", [P, 4])
        acc = [a.ps(f"acc{i}", [P, BANK]) for i in range(2)]
        x_in, w_in = a.sem("x_in"), a.sem("w_in")
        conv_done, acc_used, y_done, var_done, sd_done, chain = (a.sem(n) for n in (
            "conv_done", "acc_used", "y_done", "var_done", "sd_done", "chain"))
        block = ctx.enter_context(nc.Block())

        @block.sync
        def _(sp):
            sp.dma_start(w[:], io["tok_w"]).then_inc(w_in, 16)
            sp.dma_start(cols[:], io["tok_cols"]).then_inc(w_in, 16)
            sp.dma_start(x[:], io["x"]).then_inc(x_in, 16)

        @block.tensor
        def _(pe):
            pe.wait_ge(w_in, 32)
            pe.wait_ge(x_in, 16)
            with pe.Fori(0, B) as b:
                for half in range(2):
                    pe.wait_ge(acc_used, b * 2 + half + 1)
                    for c in range(CONTEXT):
                        mm = nc.tensor.matmul(acc[half][:, 0:HALF], w[:, c, :],
                                              x[:, bass.ds(b * S_IN + (half * HALF + c), HALF)],
                                              start=(c == 0), stop=(c == CONTEXT - 1))
                    mm.then_inc(conv_done, 1)

        @block.scalar
        def _(act):
            act.sem_inc(acc_used, 2)
            act.wait_ge(w_in, 32)
            with act.Fori(0, B) as b:
                for half in range(2):
                    act.wait_ge(conv_done, b * 2 + half + 1)
                    nc.scalar.activation(h_chunk(hT, b, half), acc[half][:, 0:HALF], ACT.Relu,
                                         bias=cols[:, 0:1]).then_inc(acc_used, 1)
            act.wait_ge(var_done, 1)
            nc.scalar.activation(s[:, 0:1], mv[:, 1:2], ACT.Sqrt, bias=K["eps5"][:, 0:1]).then_inc(sd_done, 1)

        @block.vector
        def _(dve):
            with dve.Fori(0, B) as b:
                for half in range(2):
                    dve.wait_ge(acc_used, b * 2 + half + 3)
                    nc.vector.bn_stats(stats[:, bass.ds(b * 12 + half * 6, 6)],
                                       h_chunk(hT, b, half)).then_inc(y_done, 1)
            dve.wait_ge(y_done, 2 * B)
            nc.vector.bn_aggr(mv[:], stats[:]).then_inc(var_done, 1)
            dve.wait_ge(var_done, 1)
            dve.wait_ge(sd_done, 1)
            c = Chain(dve, chain)
            c.link(nc.vector.reciprocal(s[:, 1:2], s[:, 0:1]))
            c.link(nc.vector.tensor_tensor(s[:, 2:3], s[:, 1:2], cols[:, 1:2], ALU.mult))
            c.link(nc.vector.tensor_tensor(s[:, 3:4], s[:, 2:3], mv[:, 0:1], ALU.mult))
            c.link(nc.vector.tensor_tensor(s[:, 3:4], cols[:, 2:3], s[:, 3:4], ALU.subtract))
            c.link(nc.vector.tensor_scalar(hT[:], hT[:], s[:, 2:3], s[:, 3:4], ALU.mult, ALU.add))


def layer_norm(nc, K, name, src="hT", affine=None, affine_d=None, add=False):
    hT, zT = K["hT"], K["zT"]

    def x_chunk(b, i):
        return z_chunk(zT, b, i) if src == "zT" else h_chunk(hT if src == "hT" else src, b, i)

    with ExitStack() as ctx:
        a = Alloc(nc, ctx, name)
        d = [a.sb(f"d{i}", [P, HALF]) for i in range(2)]
        sq = [a.sb(f"sq{i}", [P, HALF]) for i in range(2)]
        sd = [a.sb(f"sd{i}", [P, HALF]) for i in range(2)]
        mean = [a.ps(f"mean{i}", [P, BANK]) for i in range(2)]
        var = [a.ps(f"var{i}", [P, BANK]) for i in range(2)]
        mean_ready, d_ready, sq_ready, var_ready, sd_ready, out_ready, chain, cols_in = (a.sem(n) for n in (
            "mean_ready", "d_ready", "sq_ready", "var_ready", "sd_ready", "out_ready", "chain", "cols_in"))
        block = ctx.enter_context(nc.Block())

        @block.sync
        def _(sp):
            if affine is not None:
                sp.dma_start(affine[:], affine_d).then_inc(cols_in, 16)

        @block.tensor
        def _(pe):
            with pe.Fori(0, B) as b:
                for i in range(2):
                    pe.wait_ge(out_ready, b * 2 + 1 + i)
                    nc.tensor.matmul(mean[i][:, 0:HALF], K["mean_all"][:], x_chunk(b, i),
                                     start=True, stop=True).then_inc(mean_ready, 1)
                for i in range(2):
                    pe.wait_ge(sq_ready, b * 2 + i + 1)
                    nc.tensor.matmul(var[i][:, 0:HALF], K["mean_all"][:], sq[i][:],
                                     start=True, stop=True).then_inc(var_ready, 1)

        @block.scalar
        def _(act):
            with act.Fori(0, B) as b:
                for i in range(2):
                    act.wait_ge(d_ready, b * 2 + i + 1)
                    nc.scalar.activation(sq[i][:], d[i][:], ACT.Square).then_inc(sq_ready, 1)
                for i in range(2):
                    act.wait_ge(var_ready, b * 2 + i + 1)
                    nc.scalar.activation(sd[i][:], var[i][:, 0:HALF], ACT.Sqrt,
                                         bias=K["eps5"][:, 0:1]).then_inc(sd_ready, 1)

        @block.vector
        def _(dve):
            dve.sem_inc(out_ready, 2)
            if affine is not None:
                dve.wait_ge(cols_in, 16)
            with dve.Fori(0, B) as b:
                c = Chain(dve, chain, b, 2 * (1 + (affine is not None) + add))
                for i in range(2):
                    dve.wait_ge(mean_ready, b * 2 + i + 1)
                    nc.vector.tensor_tensor(d[i][:], x_chunk(b, i), mean[i][:, 0:HALF],
                                            ALU.subtract).then_inc(d_ready, 1)
                for i in range(2):
                    dve.wait_ge(sd_ready, b * 2 + i + 1)
                    c.link(nc.vector.reciprocal(sd[i][:], sd[i][:]))
                    if affine is None:
                        nc.vector.tensor_tensor(z_chunk(zT, b, i), d[i][:], sd[i][:],
                                                ALU.mult).then_inc(out_ready, 1)
                        continue
                    c.link(nc.vector.tensor_tensor(d[i][:], d[i][:], sd[i][:], ALU.mult))
                    out = d[i][:] if add else z_chunk(zT, b, i)
                    scaled = nc.vector.tensor_scalar(out, d[i][:], affine[:, 0:1], affine[:, 1:2], ALU.mult, ALU.add)
                    if add:
                        c.link(scaled)
                        scaled = nc.vector.tensor_tensor(h_chunk(hT, b, i), h_chunk(hT, b, i), d[i][:], ALU.add)
                    scaled.then_inc(out_ready, 1)
                c.end()


STAGES = {}


def audio_tower(nc, io, out, scratch):
    with ExitStack() as ctx:
        a = Alloc(nc, ctx, "tower")
        K = {
            "ident": a.sb("ident", [P, P]),
            "mean_all": a.sb("mean_all", [P, P]),
            "hT": a.sb("hT", [P, B * L]),
            "zT": a.sb("zT", [P, ZW]),
            "eps5": a.sb("eps5", [P, 1]),
            "eps4": a.sb("eps4", [P, 1]),
        }
        K["iota_d"] = io["iota"]
        load_constants(nc, io, K)
        for n in range(len(STAGES)):
            if n > 0:
                layer_norm(nc, K, f"ln{n}")
            STAGES[n](nc, io, K, scratch)
        written = a.sem("written")
        block = ctx.enter_context(nc.Block())

        @block.sync
        def _(sp):
            sp.dma_start(out, K["hT"][:]).then_inc(written, 16)
            sp.wait_ge(written, 16)


STAGES[0] = lambda nc, io, K, scratch: token_conv(nc, io, K)


HEADS0 = 8
HD = P // HEADS0
QD = HD // 2
PAIRS = B * HEADS0
REL_L = 256
REL = 2 * REL_L - 2
FAR = L - 1 - REL
SKEW_TILES = REL // P + 1
SKEW_W = [REL - P * t for t in range(SKEW_TILES)]
SKEW_PAD = [-(-w // P) * P for w in SKEW_W]
SKEW_ROW = BANK + P
LEFT_PART = (0, 0, 1, 1, 0, 2)
RIGHT_PART = (0, 1, 0, 1, 2, 0)
NPART = len(LEFT_PART)


def split3(nc, c, parts, src, rest, done):
    c.link(nc.vector.tensor_copy(parts[0], src))
    c.link(nc.vector.tensor_tensor(rest, src, parts[0], ALU.subtract))
    c.link(nc.vector.tensor_copy(parts[1], rest))
    c.link(nc.vector.tensor_tensor(rest, rest, parts[1], ALU.subtract))
    nc.vector.tensor_copy(parts[2], rest).then_inc(done, 1)


class GroupNorm:

    def __init__(self, a, name, avg, cols, g_ps, eps):
        self.avg, self.cols, self.g_ps, self.eps = avg, cols, g_ps, eps
        self.passed = a.sem(f"{name}_passed")
        self.stats = a.sb(f"{name}_stats", [P, 12])
        self.work = a.sb(f"{name}_work", [P, 8])
        self.mean_in, self.g_mean, self.spread_in, self.g_var, self.sd_done, self.affine_ready = (
            a.sem(f"{name}_{s}") for s in ("mean_in", "g_mean", "spread_in", "g_var", "sd_done", "affine_ready"))

    LINKS = 6

    def dve(self, nc, dve, c, x, n):
        w, g = self.work, self.g_ps
        c.link(nc.vector.bn_stats(self.stats[:, 0:6], x[:, 0:HALF]))
        c.link(nc.vector.bn_stats(self.stats[:, 6:12], x[:, HALF:L]))
        apart(dve, self.passed)
        nc.vector.bn_aggr(w[:, 0:2], self.stats[:]).then_inc(self.mean_in, 1)
        dve.wait_ge(self.mean_in, n + 1)
        dve.wait_ge(self.g_mean, n + 1)
        c.link(nc.vector.tensor_tensor(w[:, 2:3], w[:, 0:1], g[:, 0:1], ALU.subtract))
        nc.vector.scalar_tensor_tensor(out=w[:, 3:4], in0=w[:, 2:3], scalar=w[:, 2:3], in1=w[:, 1:2],
                                       op0=ALU.mult, op1=ALU.add).then_inc(self.spread_in, 1)
        dve.wait_ge(self.sd_done, n + 1)
        c.link(nc.vector.reciprocal(w[:, 5:6], w[:, 4:5]))
        c.link(nc.vector.tensor_tensor(w[:, 6:7], w[:, 5:6], self.cols[:, 0:1], ALU.mult))
        c.link(nc.vector.tensor_tensor(w[:, 7:8], w[:, 6:7], g[:, 0:1], ALU.mult))
        nc.vector.tensor_tensor(w[:, 7:8], self.cols[:, 1:2], w[:, 7:8], ALU.subtract).then_inc(self.affine_ready, 1)

    def pe(self, nc, pe, n):
        pe.wait_ge(self.mean_in, n + 1)
        nc.tensor.matmul(self.g_ps[:, 0:1], self.avg, self.work[:, 0:1], start=True, stop=True).then_inc(self.g_mean, 1)
        pe.wait_ge(self.spread_in, n + 1)
        nc.tensor.matmul(self.g_ps[:, 1:2], self.avg, self.work[:, 3:4], start=True, stop=True).then_inc(self.g_var, 1)

    def act(self, nc, act, n):
        act.wait_ge(self.g_var, n + 1)
        nc.scalar.activation(self.work[:, 4:5], self.g_ps[:, 1:2], ACT.Sqrt, bias=self.eps).then_inc(self.sd_done, 1)


def rel_projection(nc, io, K, scratch, v_tok, rel96, relv):
    zT = K["zT"]
    lhs_d, rhs_d = scratch["rel_lhs"], scratch["rel_rhs"]
    with ExitStack() as ctx:
        a = Alloc(nc, ctx, "relproj")
        w = a.sb("w", [P, 2, P])
        cols = a.sb("cols", [P, 2, 2])
        gavg = a.sb("gavg", [P, P])
        rel16 = a.sb("rel16", [2 * QD, BANK])
        relc = a.sb("relc", [2 * QD, BANK])
        relp = a.sb("relp", [2 * QD, 3, BANK], BF16)
        relv0 = a.sb("relv0", [P, HD])
        relv_col = a.sb("relv_col", [P, 1])
        zeros = a.sb("zeros", [P, SKEW_ROW])
        qk = a.sb("qk", [P, LP])
        rest = a.sb("rest", [P, LP])
        parts = a.sb("parts", [P, 3, LP], BF16)
        v = a.sb("v", [P, LP])
        qk_ps = a.ps("qk_ps", [P, 2 * BANK])
        v_ps = a.ps("v_ps", [P, 2 * BANK])
        turn_ps = a.ps("turn_ps", [P, 2 * BANK])
        g_ps = [a.ps(f"g_ps{i}", [P, BANK]) for i in range(2)]
        gn = [GroupNorm(a, ("qk", "v")[j], gavg[:], cols[:, j, :], g_ps[j], K["eps4"][:, 0:1]) for j in range(2)]
        x_ps = (qk_ps, v_ps)
        w_in, proj_done, norm_done, split_done, turned, turn_used, chain, filled, stacked, rel_in, rel_split, zeroed, rel_stacked, once = (
            a.sem(n) for n in ("w_in", "proj_done", "norm_done", "split_done", "turned", "turn_used", "chain",
                               "filled", "stacked", "rel_in", "rel_split", "zeroed", "rel_stacked", "once"))
        block = ctx.enter_context(nc.Block())

        @block.sync
        def _(sp):
            sp.dma_start(w[:], io["rel_w"]).then_inc(w_in, 16)
            sp.dma_start(cols[:], io["rel_gn"]).then_inc(w_in, 16)
            sp.dma_start(gavg[:], io["avg8"]).then_inc(w_in, 16)
            sp.dma_start(relv_col[:], io["relv_col"]).then_inc(w_in, 16)
            sp.dma_start(rel16[:], io["rel16"]).then_inc(rel_in, 16)
            sp.dma_start(relv[:], io["relv"]).then_inc(rel_in, 16)
            sp.dma_start(relv0[:], io["relv0"]).then_inc(rel_in, 16)
            sp.wait_ge(filled, 3)
            for name in ("rel_bias", "rel_probs"):
                for slot in range(2):
                    for t in range(SKEW_TILES):
                        sp.dma_start(scratch[name][slot, t], zeros[:]).then_inc(zeroed, 16)
            sp.wait_ge(rel_split, 1)
            for side in range(2):
                for s in range(NPART):
                    row = (side * NPART + s) * QD
                    sp.dma_start(rel96[row:row + QD, :], relp[side * QD:side * QD + QD, RIGHT_PART[s], :]
                                 ).then_inc(rel_stacked, 16)
            with sp.Fori(0, B) as b:
                sp.wait_ge(split_done, b + 2)
                for s in range(NPART):
                    for dst, row, src, part in ((lhs_d, s, 0, LEFT_PART[s]), (lhs_d, s + NPART, 1, LEFT_PART[s]),
                                                (rhs_d, s, 1, RIGHT_PART[s])):
                        sp.dma_start(dst[bass.ds(b * HEADS0, HEADS0), row * QD:row * QD + QD, :],
                                     parts[src * 64:src * 64 + 64, part, :]).then_inc(stacked, 16)
            sp.wait_ge(stacked, B * 3 * NPART * 16 + 16)
            sp.wait_ge(zeroed, 4 * SKEW_TILES * 16)
            sp.wait_ge(rel_stacked, 2 * NPART * 16)

        @block.tensor
        def _(pe):
            pe.wait_ge(w_in, 64)
            with pe.Fori(0, B) as b:
                pe.wait_ge(norm_done, b * 2 + 2)
                for j in range(2):
                    nc.tensor.matmul(x_ps[j][:, 0:BANK], w[:, j, :], zT[:, bass.ds(b * LP + LEAD, BANK)],
                                     start=True, stop=True)
                    nc.tensor.matmul(x_ps[j][:, BANK:L], w[:, j, :], zT[:, bass.ds(b * LP + (LEAD + BANK), L - BANK)],
                                     start=True, stop=True).then_inc(proj_done, 1)
                for j in range(2):
                    gn[j].pe(nc, pe, b)
                pe.wait_ge(norm_done, b * 2 + 4)
                pe.wait_ge(turn_used, b + 1)
                for t in range(TILES):
                    mm = nc.tensor.transpose(turn_ps[:, t * P:(t + 1) * P], v[:, t * P:(t + 1) * P], K["ident"][:])
                mm.then_inc(turned, 1)

        @block.scalar
        def _(act):
            act.sem_inc(norm_done, 2)
            act.wait_ge(filled, 3)
            with act.Fori(0, B) as b:
                for j in range(2):
                    gn[j].act(nc, act, b)
                act.wait_ge(gn[0].affine_ready, b + 1)
                act.wait_ge(split_done, b + 1)
                nc.scalar.activation(qk[:, 0:L], qk_ps[:, 0:L], ACT.Identity, bias=gn[0].work[:, 7:8],
                                     scale=gn[0].work[:, 6:7]).then_inc(norm_done, 1)
                act.wait_ge(gn[1].affine_ready, b + 1)
                act.wait_ge(turn_used, b + 1)
                nc.scalar.activation(v[:, 0:L], v_ps[:, 0:L], ACT.Identity, bias=gn[1].work[:, 7:8],
                                     scale=gn[1].work[:, 6:7]).then_inc(norm_done, 1)

        @block.vector
        def _(dve):
            dve.sem_inc(turn_used, 1)
            dve.sem_inc(split_done, 1)
            dve.sem_inc(stacked, 16)
            nc.vector.memset(zeros[:], 0.0).then_inc(filled, 1)
            nc.vector.memset(qk[:], 0.0).then_inc(filled, 1)
            nc.vector.memset(v[:], 0.0).then_inc(filled, 1)
            dve.wait_ge(rel_in, 48)
            dve.wait_ge(w_in, 64)
            c = Chain(dve, once)
            c.link(nc.vector.tensor_scalar(relc[:], rel16[:], rel16[:, REL:REL + 1], None, ALU.subtract))
            split3(nc, c, [relp[:, i, :] for i in range(3)], relc[:], rel16[:], rel_split)
            c.link(nc.vector.tensor_tensor(cols[:, 1, 1:2], cols[:, 1, 1:2], relv_col[:], ALU.add))
            for t in range(SKEW_TILES):
                c.link(nc.vector.tensor_tensor(relv[:, t, :], relv[:, t, :], relv0[:], ALU.subtract))
            with dve.Fori(0, B) as b:
                c = Chain(dve, chain, b, 2 * GroupNorm.LINKS + 4)
                for j in range(2):
                    dve.wait_ge(proj_done, b * 2 + j + 1)
                    gn[j].dve(nc, dve, c, x_ps[j], b)
                dve.wait_ge(norm_done, b * 2 + 3)
                dve.wait_ge(stacked, b * (3 * NPART * 16) + 16)
                split3(nc, c, [parts[:, i, :] for i in range(3)], qk[:], rest[:], split_done)
                dve.wait_ge(turned, b + 1)
                nc.vector.tensor_copy(v_tok[:, :, bass.ds(b * P, P)],
                                      turn_ps[:, 0:LP].rearrange("p (t c) -> p t c", t=TILES)).then_inc(turn_used, 1)
                c.end()


class Turn:

    def __init__(self, m, k):
        self.n, self.slot, self.turn = m * 2 + k, k % 2, m + k // 2
        self.first = isinstance(m, int) and self.n == 0
        self.early = isinstance(m, int) and self.n < 2


def rel_attention(nc, io, K, scratch, v_tok, rel96, relv):
    with ExitStack() as ctx:
        a = Alloc(nc, ctx, "rel")
        lhs = [a.sb(f"lhs{i}", [2 * NPART * QD, LP], BF16) for i in range(2)]
        rhs = [a.sb(f"rhs{i}", [NPART * QD, LP], BF16) for i in range(2)]
        r_sb = [a.sb(f"r_sb{i}", [P, SKEW_TILES, BANK]) for i in range(2)]
        bias = [[a.sb(f"bias{i}_{t}", [P, SKEW_W[t]]) for t in range(SKEW_TILES)] for i in range(2)]
        probs = [a.sb(f"probs{i}", [P, TILES, LP]) for i in range(2)]
        shear = [[a.sb(f"shear{i}_{t}", [P, SKEW_PAD[t]]) for t in range(SKEW_TILES)] for i in range(2)]
        probsT = [a.sb(f"probsT{i}", [P, TILES, LP]) for i in range(2)]
        shearT = a.sb("shearT", [P, SKEW_TILES, BANK])
        v_pad = [a.sb(f"v_pad{i}", [P, TILES, 2 * HD]) for i in range(2)]
        relv_pad = [a.sb(f"relv_pad{i}", [P, SKEW_TILES, 2 * HD]) for i in range(2)]
        o_sb = a.sb("o_sb", [4 * HD, HALF])
        nmax = [a.sb(f"nmax{i}", [P, TILES]) for i in range(2)]
        sums = [a.sb(f"sums{i}", [P, TILES]) for i in range(2)]
        rsum = [a.sb(f"rsum{i}", [P, TILES]) for i in range(2)]
        s_ps = [a.ps(f"s_ps{i}", [P, 2 * BANK]) for i in range(2)]
        t_ps = a.ps("t_ps", [P, 2 * BANK])
        x_ps = a.ps("x_ps", [P, BANK])
        o_ps = a.ps("o_ps", [P, BANK])
        in_sem = a.sems("pair_in", 2)
        bias_out, bias_in = a.sems("bias_out", 2), a.sems("bias_in", 2)
        probs_out, shear_in = a.sems("probs_out", 2), a.sems("shear_in", 2)
        names = ("r_full", "r_copied", "a_full", "a_copied", "s_full", "biased", "max_ready", "exp_done", "rs_ready",
                 "scaled", "t_full", "t_copied", "v_ready", "o_full", "o_copied", "o_stored", "filled", "passed")
        (r_full, r_copied, a_full, a_copied, s_full, biased, max_ready, exp_done, rs_ready,
         scaled, t_full, t_copied, v_ready, o_full, o_copied, o_stored, filled, passed) = (a.sem(n) for n in names)
        NS, T = SKEW_TILES, TILES
        LAG = 2
        blocks_of = [w // P for w in SKEW_PAD]
        block = ctx.enter_context(nc.Block())

        def turns(eng, body):
            t = [Turn(0, k) for k in range(PAIRS)]
            body(t[0], None, None)
            body(t[1], t[0], None)
            body(t[2], t[1], t[0])
            with eng.Fori(0, (PAIRS - 4) // 2) as m:
                for k in range(2):
                    body(Turn(m, k + 3), Turn(m, k + 2), Turn(m, k + 1))
            body(t[PAIRS - 1], t[PAIRS - 2], t[PAIRS - 3])
            body(None, t[PAIRS - 1], t[PAIRS - 2])
            body(None, None, t[PAIRS - 1])

        def sheared(name, slot, t, step, width):
            rows = scratch[name]
            at = (slot * SKEW_TILES + t) * P * SKEW_ROW
            return bass.AP(rows.tensor, rows.offset + at, [[step, P], [1, width]])

        def copy_turned(eng, copy, now, t):
            if not now.early:
                eng.wait_ge(o_full, now.n - 1)
            eng.wait_ge(t_full, now.n * T + t + 1)
            copy(probsT[now.slot][:, :, t * P:(t + 1) * P],
                 t_ps[:, 0:LP].rearrange("p (j i) -> p j i", j=T)).then_inc(t_copied, 1)

        @block.sync
        def _(sp):
            def load(pair):
                sp.dma_start(lhs[pair.slot][:], scratch["rel_lhs"][bass.ds(pair.n, 1), :, :].squeeze(0)).then_inc(in_sem[pair.slot], 16)
                sp.dma_start(rhs[pair.slot][:], scratch["rel_rhs"][bass.ds(pair.n, 1), :, :].squeeze(0)).then_inc(in_sem[pair.slot], 16)

            def body(new, now, old):
                if new is not None:
                    if old is not None:
                        sp.wait_ge(s_full, old.n * T + T)
                    load(new)
                if old is not None and new is not None:
                    sp.wait_ge(bias_in[new.slot], new.turn * (16 * NS))
                if old is not None and now is not None and not now.early:
                    sp.wait_ge(shear_in[now.slot], now.turn * (16 * NS))
                for t in range(NS):
                    if new is not None:
                        sp.wait_ge(r_copied, new.n * NS + t + 1)
                        sp.dma_start(scratch["rel_bias"][new.slot, t, :, 0:SKEW_W[t]], r_sb[new.slot][:, t, 0:SKEW_W[t]]
                                     ).then_inc(bias_out[new.slot], 16)
                    if now is not None:
                        sp.wait_ge(scaled, now.n * T + t + 1)
                        sp.dma_start(scratch["rel_probs"][now.slot, t, :, 0:SKEW_W[t]],
                                     probs[now.slot][:, t, L - SKEW_W[t]:L]).then_inc(probs_out[now.slot], 16)
                if new is not None:
                    sp.wait_ge(bias_out[new.slot], new.turn * (16 * NS) + 16 * NS)
                    apart(sp, passed)
                    if old is not None:
                        sp.wait_ge(biased, old.n * NS + NS)
                    for t in range(NS):
                        sp.dma_start(bias[new.slot][t][:], sheared("rel_bias", new.slot, t, SKEW_ROW - 1, SKEW_W[t])
                                     ).then_inc(bias_in[new.slot], 16)
                if now is not None:
                    sp.wait_ge(probs_out[now.slot], now.turn * (16 * NS) + 16 * NS)
                    apart(sp, passed)
                    if not now.early:
                        sp.wait_ge(a_full, now.n * NS - NS)
                    for t in range(NS):
                        sp.dma_start(shear[now.slot][t][:], sheared("rel_probs", now.slot, t, SKEW_ROW + 1, SKEW_PAD[t])
                                     ).then_inc(shear_in[now.slot], 16)
                if old is not None and old.slot == 1:
                    sp.wait_ge(o_copied, old.turn + 1)
                    for half in range(2):
                        sp.dma_start(scratch["rel_out"][bass.ds(old.turn, 1), :, half, :].squeeze(0),
                                     o_sb[half * 2 * HD:(half + 1) * 2 * HD, :]).then_inc(o_stored, 16)

            turns(sp, body)
            sp.wait_ge(o_stored, PAIRS * 16)

        @block.gpsimd
        def _(pool):
            for i in range(2):
                nc.gpsimd.memset(v_pad[i][:], 0.0).then_inc(filled, 1)
                nc.gpsimd.memset(relv_pad[i][:], 0.0).then_inc(filled, 1)
            pool.wait_ge(filled, 6)
            for i in range(2):
                nc.gpsimd.tensor_copy(relv_pad[i][:, :, i * HD:(i + 1) * HD], relv[:]).then_inc(filled, 1)

            def body(new, now, old):
                if now is None:
                    return
                if not now.early:
                    pool.wait_ge(o_full, now.n - 1)
                    apart(pool, passed)
                nc.gpsimd.tensor_copy(v_pad[now.slot][:, :, now.slot * HD:(now.slot + 1) * HD],
                                      v_tok[:, :, bass.ds(now.n * HD, HD)]).then_inc(v_ready, 1)

            turns(pool, body)

        @block.tensor
        def _(pe):
            def position(new, now, old, t):
                if now is not None or t > 0:
                    pe.wait_ge(r_copied, new.n * NS + t)
                if old is not None and (t > 0 or not old.first):
                    pe.wait_ge(a_copied, old.n * NS + t)
                if t == 0:
                    pe.wait_ge(in_sem[new.slot], new.turn * 32 + 32)
                nc.tensor.matmul(x_ps[:, 0:SKEW_W[t]], lhs[new.slot][:, t * P:(t + 1) * P], rel96[:, 0:SKEW_W[t]],
                                 start=True, stop=True).then_inc(r_full, 1)

            def scores(now, t):
                i = t % 2
                if t >= 2 or not now.first:
                    pe.wait_ge(exp_done, now.n * T + t - 1)
                nc.tensor.matmul(s_ps[i][:, 0:BANK], lhs[now.slot][0:NPART * QD, t * P:(t + 1) * P],
                                 rhs[now.slot][:, 0:BANK], start=True, stop=True)
                nc.tensor.matmul(s_ps[i][:, BANK:L], lhs[now.slot][0:NPART * QD, t * P:(t + 1) * P],
                                 rhs[now.slot][:, BANK:L], start=True, stop=True).then_inc(s_full, 1)

            def turn_probs(now, t):
                pe.wait_ge(scaled, now.n * T + t + 1)
                if t > 0 or not now.first:
                    pe.wait_ge(t_copied, now.n * T + t)
                for j in range(T):
                    mm = nc.tensor.transpose(t_ps[:, j * P:(j + 1) * P], probs[now.slot][:, t, j * P:(j + 1) * P],
                                             K["ident"][:])
                mm.then_inc(t_full, 1)

            def turn_shear(new, old, t):
                if t == 0:
                    pe.wait_ge(shear_in[old.slot], old.turn * (16 * NS) + 16 * NS)
                if new is not None:
                    pe.wait_ge(r_copied, new.n * NS + t + 1)
                if t > 0 or not old.first:
                    pe.wait_ge(a_copied, old.n * NS + t)
                for j in range(blocks_of[t]):
                    mm = nc.tensor.transpose(x_ps[:, j * P:(j + 1) * P], shear[old.slot][t][:, j * P:(j + 1) * P],
                                             K["ident"][:])
                mm.then_inc(a_full, 1)

            def values(old, j):
                if j == 0:
                    pe.wait_ge(t_copied, old.n * T + T)
                    pe.wait_ge(v_ready, old.n + 1)
                    if old.slot == 0 and not old.first:
                        pe.wait_ge(o_copied, old.turn)
                for half in range(2):
                    nc.tensor.matmul(o_ps[half * 2 * HD:(half + 1) * 2 * HD, 0:HALF], v_pad[old.slot][:, j, :],
                                     probsT[old.slot][:, j, half * HALF:(half + 1) * HALF],
                                     start=(j == 0 and old.slot == 0), stop=False, skip_group_check=True)

            def positions(old):
                pe.wait_ge(a_copied, old.n * NS + NS)
                for half in range(2):
                    for j in range(NS):
                        lo, hi = half * HALF, min((half + 1) * HALF, (NS - j) * P)
                        if lo < hi:
                            mm = nc.tensor.matmul(o_ps[half * 2 * HD:(half + 1) * 2 * HD, 0:hi - lo], relv_pad[old.slot][:, j, :],
                                                  shearT[:, j, lo:hi], start=False, stop=(old.slot == 1), skip_group_check=True)
                mm.then_inc(o_full, 1)

            def body(new, now, old):
                for t in range(T + LAG):
                    if now is not None and t < T:
                        scores(now, t)
                    if new is not None and t < NS:
                        position(new, now, old, t)
                    if old is not None and t < T:
                        values(old, t)
                    if now is not None and t >= LAG:
                        turn_probs(now, t - LAG)
                    if old is not None and t < NS:
                        turn_shear(new, old, t)
                if old is not None:
                    positions(old)

            pe.wait_ge(filled, 8)
            turns(pe, body)

        @block.scalar
        def _(act):
            def body(new, now, old):
                for t in range(T + LAG):
                    if now is not None and t < T:
                        act.wait_ge(max_ready, now.n * T + t + 1)
                        if t == 0 and not now.early:
                            act.wait_ge(t_full, now.n * T - T)
                            act.wait_ge(probs_out[now.slot], now.turn * (16 * NS))
                            act.wait_ge(rs_ready, now.n * T - T)
                        nc.scalar.activation(probs[now.slot][:, t, 0:L], s_ps[t % 2][:, 0:L], ACT.Exp,
                                             bias=nmax[now.slot][:, t:t + 1],
                                             accum_out=sums[now.slot][:, t:t + 1]).then_inc(exp_done, 1)
                    if new is not None and t < NS:
                        if t == 0 and old is not None:
                            act.wait_ge(bias_out[new.slot], new.turn * (16 * NS))
                        act.wait_ge(r_full, new.n * NS + t + 1)
                        nc.scalar.copy(r_sb[new.slot][:, t, 0:SKEW_W[t]], x_ps[:, 0:SKEW_W[t]]).then_inc(r_copied, 1)
                    if now is not None and t >= LAG and t % 2 == 0:
                        copy_turned(act, nc.scalar.copy, now, t - LAG)
                    if old is not None and t < NS:
                        if t == 0 and not old.first:
                            act.wait_ge(o_full, old.n)
                        act.wait_ge(a_full, old.n * NS + t + 1)
                        n = blocks_of[t]
                        nc.scalar.copy(shearT[:, 0:n, t * P:(t + 1) * P],
                                       x_ps[:, 0:n * P].rearrange("p (j i) -> p j i", j=n)).then_inc(a_copied, 1)

            turns(act, body)

        @block.vector
        def _(dve):
            def scale(now, t):
                n = now.n * T + t + 1
                dve.wait_ge(exp_done, n)
                nc.vector.reciprocal(rsum[now.slot][:, t:t + 1], sums[now.slot][:, t:t + 1]).then_inc(rs_ready, 1)
                dve.wait_ge(rs_ready, n)
                nc.vector.tensor_scalar(probs[now.slot][:, t, 0:L], probs[now.slot][:, t, 0:L],
                                        rsum[now.slot][:, t:t + 1], None, ALU.mult).then_inc(scaled, 1)

            def body(new, now, old):
                for t in range(T + LAG):
                    if now is not None and t < T:
                        dve.wait_ge(s_full, now.n * T + t + 1)
                        if t < NS:
                            if t == 0:
                                dve.wait_ge(bias_in[now.slot], now.turn * (16 * NS) + 16 * NS)
                            s = s_ps[t % 2][:, L - SKEW_W[t]:L]
                            nc.vector.tensor_tensor(s, s, bias[now.slot][t][:], ALU.add).then_inc(biased, 1)
                            dve.wait_ge(biased, now.n * NS + t + 1)
                        if t == 0 and not now.early:
                            dve.wait_ge(exp_done, now.n * T - T)
                        nc.vector.tensor_reduce(nmax[now.slot][:, t:t + 1], s_ps[t % 2][:, 0:L], AX.X, ALU.max,
                                                negate=True).then_inc(max_ready, 1)
                    if now is not None and 1 <= t <= T:
                        scale(now, t - 1)
                    if now is not None and t >= LAG and t % 2 == 1:
                        copy_turned(dve, nc.vector.tensor_copy, now, t - LAG)
                if old is not None and old.slot == 1:
                    dve.wait_ge(o_full, old.n + 1)
                    if not old.early:
                        dve.wait_ge(o_stored, old.turn * 32)
                    nc.vector.tensor_copy(o_sb[:], o_ps[0:4 * HD, 0:HALF]).then_inc(o_copied, 1)

            for i in range(2):
                nc.vector.memset(probs[i][:, :, L:LP], 0.0).then_inc(filled, 1)
            turns(dve, body)


def rel_output(nc, io, K, scratch):
    hT = K["hT"]
    with ExitStack() as ctx:
        a = Alloc(nc, ctx, "relout")
        gavg = a.sb("gavg", [P, P])
        cols = a.sb("cols", [P, 2])
        o = a.sb("o", [P, B, L])
        y = [a.sb(f"y{i}", [P, L]) for i in range(2)]
        g_ps = a.ps("g_ps", [P, BANK])
        gn = GroupNorm(a, "out", gavg[:], cols[:], g_ps, K["eps4"][:, 0:1])
        w_in, scaled, added, chain = (a.sem(n) for n in ("w_in", "scaled", "added", "chain"))
        block = ctx.enter_context(nc.Block())

        @block.sync
        def _(sp):
            sp.dma_start(gavg[:], io["avg4"]).then_inc(w_in, 16)
            sp.dma_start(cols[:], io["relout_gn"]).then_inc(w_in, 16)
            sp.dma_start(o[:], scratch["rel_out"].rearrange("(b q) r h c -> (q r) b (h c)", b=B)).then_inc(w_in, 16)

        @block.tensor
        def _(pe):
            pe.wait_ge(w_in, 48)
            for b in range(B):
                gn.pe(nc, pe, b)

        @block.scalar
        def _(act):
            for b in range(B):
                gn.act(nc, act, b)
                act.wait_ge(gn.affine_ready, b + 1)
                if b >= 2:
                    act.wait_ge(added, b - 1)
                nc.scalar.activation(y[b % 2][:], o[:, b, :], ACT.Identity, bias=gn.work[:, 7:8],
                                     scale=gn.work[:, 6:7]).then_inc(scaled, 1)

        @block.vector
        def _(dve):
            dve.wait_ge(w_in, 48)
            c = Chain(dve, chain)
            for b in range(B):
                gn.dve(nc, dve, c, o[:, b, :], b)
                dve.wait_ge(scaled, b + 1)
                h = hT[:, b * L:(b + 1) * L]
                nc.vector.tensor_tensor(h, h, y[b % 2][:], ALU.add).then_inc(added, 1)
                dve.wait_ge(added, b + 1)


def stage1(nc, io, K, scratch):
    with ExitStack() as ctx:
        a = Alloc(nc, ctx, "stage1")
        v_tok = a.sb("v_tok", [P, TILES, PAIRS * HD])
        rel96 = a.sb("rel96", [2 * NPART * QD, BANK], BF16)
        relv = a.sb("relv", [P, SKEW_TILES, HD])
        scratch["rel_lhs"] = nc.dram_tensor("rel_lhs", (PAIRS, 2 * NPART * QD, LP), BF16, kind="Internal").ap()
        scratch["rel_rhs"] = nc.dram_tensor("rel_rhs", (PAIRS, NPART * QD, LP), BF16, kind="Internal").ap()
        scratch["rel_bias"] = nc.dram_tensor("rel_bias", (2, SKEW_TILES, P, SKEW_ROW), F32, kind="Internal").ap()
        scratch["rel_probs"] = nc.dram_tensor("rel_probs", (2, SKEW_TILES, P, SKEW_ROW), F32, kind="Internal").ap()
        scratch["rel_out"] = nc.dram_tensor("rel_out", (PAIRS // 2, 2 * HD, 2, HALF), F32, kind="Internal").ap()
        rel_projection(nc, io, K, scratch, v_tok, rel96, relv)
        rel_attention(nc, io, K, scratch, v_tok, rel96, relv)
        rel_output(nc, io, K, scratch)


STAGES[1] = stage1


def group_average(size):
    return np.kron(np.eye(P // size, dtype=np.float32), np.full((size, size), 1.0 / size, np.float32))


def stage1_layout(f):
    chan = np.arange(2 * P).reshape(HEADS0, 4, QD)
    qk = np.concatenate([chan[:, 0].ravel(), chan[:, 1].ravel()])
    v = chan[:, 2:].ravel()
    gn = np.stack([f["L0_attn_gn_qkv_scale"], f["L0_attn_gn_qkv_bias"]], 1)
    rel = f["L0_attn_rel_emb"]
    col = np.minimum(np.arange(BANK), REL)
    rev = np.where(col < REL, REL - 1 - col, REL)
    relq, relk, relv = rel[:QD], rel[QD:2 * QD], rel[2 * QD:]
    return {
        "rel_w": np.stack([f["L0_attn_W_qkv"][:, qk], f["L0_attn_W_qkv"][:, v]], 1),
        "rel_gn": np.stack([gn[qk], gn[v]], 1),
        "avg8": group_average(8),
        "avg4": group_average(4),
        "relout_gn": np.stack([f["L0_attn_gn_out_scale"], f["L0_attn_gn_out_bias"]], 1),
        "rel16": np.concatenate([relk, relq])[:, rev],
        "relv": relv[:, rev].T.reshape(SKEW_TILES, P, HD).transpose(1, 0, 2),
        "relv0": np.broadcast_to(relv[:, REL], (P, HD)),
        "relv_col": np.tile(relv[:, REL], HEADS0)[:, None],
    }


TOK_TILES = B * TILES
NCH = len(CHUNKS)
HID = 512
HJ = HID // P


def top2_gates(nc, K, a, block, lg, lg_ready, E, gates, pack, pack_ps, packT, gates_d):
    W = E if pack == "sum" else 4 * E
    best = a.sb("best", [P, TOK_TILES, 8])
    at = a.sb("at", [P, TOK_TILES, 8], U32)
    atf = a.sb("atf", [P, TOK_TILES, 2])
    iota = a.sb("iota", [P, TOK_TILES, E])
    g = a.sb("g", [P, 2, TOK_TILES])
    e = a.sb("e", [P, 2, TOK_TILES])
    one = a.sb("one", [P, TOK_TILES, E])
    iota_in, found, diff_ready, exp_ready, packed, turned, copied, chain = (a.sem(f"top2_{n}") for n in (
        "iota_in", "found", "diff_ready", "exp_ready", "packed", "turned", "copied", "chain"))
    gates_out = a.sem("top2_gates_out")

    @block.sync
    def _(sp):
        sp.dma_start(iota[:], K["iota_d"][:, :, 0:E]).then_inc(iota_in, 16)
        for b in range(B):
            sp.wait_ge(copied, b + 1)
            sp.dma_start(gates_d[:, b * LP:(b + 1) * LP], packT[:, b * LP:(b + 1) * LP]).then_inc(gates_out, 16)
        sp.wait_ge(gates_out, B * 16)

    @block.scalar
    def _(act):
        act.wait_ge(diff_ready, 1)
        nc.scalar.activation(e[:, 0, :], g[:, 0, :], ACT.Exp).then_inc(exp_ready, 1)

    @block.vector
    def _(dve):
        c = Chain(dve, chain)
        dve.wait_ge(lg_ready[0], lg_ready[1])
        for t in range(TOK_TILES):
            c.link(nc.vector.max(best[:, t, :], lg[:, t, :]))
            nc.vector.max_index(at[:, t, :], best[:, t, :], lg[:, t, :]).then_inc(found, 1)
        dve.wait_ge(found, TOK_TILES)
        nc.vector.tensor_tensor(g[:, 0, :].unsqueeze(2), best[:, :, 1:2], best[:, :, 0:1], ALU.subtract).then_inc(diff_ready, 1)
        c.link(nc.vector.tensor_copy(atf[:], at[:, :, 0:2]))
        dve.wait_ge(exp_ready, 1)
        c.link(nc.vector.tensor_scalar(e[:, 1, :], e[:, 0, :], 1.0, None, ALU.add))
        c.link(nc.vector.reciprocal(g[:, 0, :], e[:, 1, :]))
        c.link(nc.vector.tensor_tensor(g[:, 1, :], g[:, 0, :], e[:, 0, :], ALU.mult))
        dve.wait_ge(iota_in, 16)
        full = [P, TOK_TILES, E]
        for k in range(2):
            mask = one[:] if pack == "sum" else gates[:, :, k * E:(k + 1) * E]
            out = gates[:, :, 0:E] if pack == "sum" and k == 0 else one[:] if pack == "sum" else gates[:, :, (2 + k) * E:(3 + k) * E]
            c.link(nc.vector.tensor_tensor(mask, iota[:], atf[:, :, k:k + 1].to_broadcast(full), ALU.is_equal))
            c.link(nc.vector.tensor_tensor(out, mask, g[:, k, :].unsqueeze(2).to_broadcast(full), ALU.mult))
        if pack == "sum":
            c.link(nc.vector.tensor_tensor(gates[:], gates[:], one[:], ALU.add))
        dve.sem_inc(packed, 1)
        for b in range(B):
            dve.wait_ge(turned, b + 1)
            nc.vector.tensor_copy(packT[:, b * LP:(b + 1) * LP], pack_ps[0:W, 0:LP]).then_inc(copied, 1)

    @block.tensor
    def _(pe):
        pe.wait_ge(packed, 1)
        for b in range(B):
            if b >= 1:
                pe.wait_ge(copied, b)
            for t in range(TILES):
                mm = nc.tensor.transpose(pack_ps[0:W, t * P:(t + 1) * P], gates[:, b * TILES + t, :], K["ident"][:])
            mm.then_inc(turned, 1)


def experts(nc, K, scratch, name, E, kind, weights, b2, gates_d, y):
    zT = K["zT"]
    with ExitStack() as ctx:
        a = Alloc(nc, ctx, name)
        w = [a.sb(f"w{i}", [P, 2 * HID + HJ]) for i in range(2)]
        gate = [a.sb(f"gate{i}", [P, B * LP]) for i in range(2)]
        b2_sb = a.sb("b2", [E, P])
        gT = a.sb("gT", [E, B * LP])
        ex = [a.sb(f"ex{j}", [P, HALF]) for j in range(HJ)]
        hid = [a.sb(f"hid{i}", [P, HJ, HALF]) for i in range(2)]
        part = a.sb("part", [P, HALF])
        h_ps = [a.ps(f"h_ps{j}", [P, BANK]) for j in range(HJ)]
        o_ps = [a.ps(f"o_ps{i}", [P, BANK]) for i in range(2)]
        w_in = a.sems("w_in", 2)
        rows_in, b_full, y_set, h_full, ex_done, low_done, h_done, o_full, y_done, part_done = (a.sem(n) for n in (
            "rows_in", "b_full", "y_set", "h_full", "ex_done", "low_done", "h_done", "o_full", "y_done", "part_done"))
        block = ctx.enter_context(nc.Block())
        PAIR = 2 * NCH

        def zc(c):
            b, half = CHUNKS[c]
            return zT[:, LEAD + b * LP + half * HALF:LEAD + b * LP + half * HALF + HALF]

        def yc(c):
            return y[:, c * HALF:(c + 1) * HALF]

        def gc(s, c):
            b, half = CHUNKS[c]
            return gate[s][:, b * LP + half * HALF:b * LP + half * HALF + HALF]

        @block.sync
        def _(sp):
            sp.dma_start(b2_sb[:], b2).then_inc(rows_in, 16)
            sp.dma_start(gT[:], gates_d).then_inc(rows_in, 16)
            with sp.Fori(0, E // 2) as m:
                for s in range(2):
                    sp.wait_ge(y_done, m * PAIR + (s * NCH + NCH))
                    sp.dma_start(w[s][:], weights[bass.ds(m * 2 + s, 1), :, :].squeeze(0)).then_inc(w_in[s], 16)
                    sp.dma_start(gate[s][:], gates_d[bass.ds(m * 2 + s, 1), :].to_broadcast([P, B * LP])).then_inc(w_in[s], 16)

        @block.tensor
        def _(pe):
            pe.wait_ge(rows_in, 32)
            for c in range(NCH):
                if c >= 2:
                    pe.wait_ge(y_set, c - 1)
                b, half = CHUNKS[c]
                nc.tensor.matmul(o_ps[c % 2][:, 0:HALF], b2_sb[:], gT[:, b * LP + half * HALF:b * LP + half * HALF + HALF],
                                 start=True, stop=True).then_inc(b_full, 1)
            pe.wait_ge(y_set, NCH)

            def first(m, i):
                s, c = i // NCH, i % NCH
                if c == 0:
                    pe.wait_ge(w_in[s], m * 32 + 32)
                for j in range(HJ):
                    pe.wait_ge(h_done, m * (PAIR * HJ) + (i * HJ + j + 1))
                    nc.tensor.matmul(h_ps[j][:, 0:HALF], w[s][:, j * P:(j + 1) * P], zc(c),
                                     start=True, stop=True).then_inc(h_full, 1)

            def second(m, i):
                s = i // NCH
                pe.wait_ge(h_done, m * (PAIR * HJ) + (i * HJ + 2 * HJ))
                pe.wait_ge(y_done, m * PAIR + (i + PAIR - 1))
                for j in range(HJ):
                    mm = nc.tensor.matmul(o_ps[i % 2][:, 0:HALF], w[s][:, HID + j * P:HID + (j + 1) * P],
                                          hid[i % 2][:, j, :], start=(j == 0), stop=(j == HJ - 1))
                mm.then_inc(o_full, 1)

            with pe.Fori(0, E // 2) as m:
                for i in range(PAIR):
                    first(m, i)
                    if i >= 1:
                        second(m, i - 1)
                second(m, PAIR - 1)

        @block.scalar
        def _(act):
            with act.Fori(0, E // 2) as m:
                for i in range(PAIR):
                    s = i // NCH
                    if kind != "elu":
                        act.wait_ge(o_full, m * PAIR + (i + 1))
                    for j in range(HJ):
                        act.wait_ge(h_full, m * (PAIR * HJ) + (i * HJ + j + 1))
                        b1 = w[s][:, 2 * HID + j:2 * HID + j + 1]
                        if kind == "elu":
                            nc.scalar.activation(ex[j][:], h_ps[j][:, 0:HALF], ACT.Exp, bias=b1).then_inc(ex_done, 1)
                        else:
                            nc.scalar.activation(hid[i % 2][:, j, :], h_ps[j][:, 0:HALF], kind, bias=b1).then_inc(h_done, 1)

        @block.vector
        def _(dve):
            dve.sem_inc(h_done, HJ)
            dve.sem_inc(o_full, 2)
            dve.sem_inc(y_done, PAIR)
            for c in range(NCH):
                dve.wait_ge(b_full, c + 1)
                nc.vector.tensor_copy(yc(c), o_ps[c % 2][:, 0:HALF]).then_inc(y_set, 1)

            def gather(m, i):
                s, c = i // NCH, i % NCH
                if c == 0:
                    dve.wait_ge(w_in[s], m * 32 + 32)
                dve.wait_ge(y_done, m * PAIR + (i + PAIR))
                dve.wait_ge(o_full, m * PAIR + (i + 3))
                nc.vector.tensor_tensor(part[:], o_ps[i % 2][:, 0:HALF], gc(s, c), ALU.mult).then_inc(part_done, 1)
                dve.wait_ge(part_done, m * PAIR + (i + 1))
                nc.vector.tensor_tensor(yc(c), yc(c), part[:], ALU.add).then_inc(y_done, 1)

            with dve.Fori(0, E // 2) as m:
                for i in range(PAIR):
                    s = i // NCH
                    if kind == "elu":
                        dve.wait_ge(o_full, m * PAIR + (i + 1))
                        for j in range(HJ):
                            n = m * (PAIR * HJ) + (i * HJ + j + 1)
                            dve.wait_ge(ex_done, n)
                            nc.vector.tensor_scalar(ex[j][:], ex[j][:], 1.0, -1.0, ALU.min, ALU.add).then_inc(low_done, 1)
                            dve.wait_ge(low_done, n)
                            nc.vector.scalar_tensor_tensor(out=hid[i % 2][:, j, :], in0=h_ps[j][:, 0:HALF],
                                                           scalar=w[s][:, 2 * HID + j:2 * HID + j + 1], in1=ex[j][:],
                                                           op0=ALU.add, op1=ALU.max).then_inc(h_done, 1)
                    if i >= 1:
                        gather(m, i - 1)
                gather(m, PAIR - 1)


E0 = 10
TAPS_R, TAPS_S = 3, 9


def conv_router(nc, io, K, gates_d):
    zT = K["zT"]
    with ExitStack() as ctx:
        a = Alloc(nc, ctx, "router")
        w1 = a.sb("w1", [P, TAPS_R, P])
        w2 = a.sb("w2", [P, TAPS_R, E0])
        b1 = a.sb("b1", [P, 1])
        b2 = a.sb("b2", [P, E0])
        rc = a.sb("rc", [P, 1 + LP + 1])
        lg = a.sb("lg", [P, TOK_TILES, E0])
        gates = a.sb("gates", [P, TOK_TILES, E0])
        packT = a.sb("packT", [E0, B * LP])
        c_ps = [a.ps(f"c_ps{i}", [P, BANK]) for i in range(2)]
        l_ps = a.ps("l_ps", [P, TILES, E0])
        pack_ps = a.ps("pack_ps", [P, 2 * BANK])
        w_in, filled, conv_done, rc_done, l_done, lg_ready = (a.sem(n) for n in (
            "w_in", "filled", "conv_done", "rc_done", "l_done", "lg_ready"))
        block = ctx.enter_context(nc.Block())

        @block.sync
        def _(sp):
            for dst, src in ((w1, "rc_w1"), (w2, "rc_w2"), (b1, "rc_b1"), (b2, "rc_b2")):
                sp.dma_start(dst[:], io[src]).then_inc(w_in, 16)

        @block.tensor
        def _(pe):
            pe.wait_ge(w_in, 64)
            with pe.Fori(0, B) as b:
                for half in range(2):
                    pe.wait_ge(rc_done, b * 2 + half + 1)
                    for k in range(TAPS_R):
                        mm = nc.tensor.matmul(c_ps[half][:, 0:HALF], w1[:, k, :], z_chunk(zT, b, half, k - TAPS_R // 2),
                                              start=(k == 0), stop=(k == TAPS_R - 1))
                    mm.then_inc(conv_done, 1)
                pe.wait_ge(rc_done, b * 2 + 4)
                pe.wait_ge(lg_ready, b + 1)
                for t in range(TILES):
                    for k in range(TAPS_R):
                        mm = nc.tensor.matmul(l_ps[:, t, :], rc[:, t * P + k:t * P + k + P], w2[:, k, :],
                                              start=(k == 0), stop=(k == TAPS_R - 1))
                mm.then_inc(l_done, 1)

        @block.scalar
        def _(act):
            act.sem_inc(rc_done, 2)
            act.wait_ge(w_in, 64)
            act.wait_ge(filled, 1)
            with act.Fori(0, B) as b:
                act.wait_ge(lg_ready, b + 1)
                for half in range(2):
                    act.wait_ge(conv_done, b * 2 + half + 1)
                    nc.scalar.activation(rc[:, 1 + half * HALF:1 + half * HALF + HALF], c_ps[half][:, 0:HALF],
                                         ACT.Gelu, bias=b1[:, 0:1]).then_inc(rc_done, 1)

        @block.vector
        def _(dve):
            dve.sem_inc(lg_ready, 1)
            nc.vector.memset(rc[:], 0.0).then_inc(filled, 1)
            dve.wait_ge(w_in, 64)
            with dve.Fori(0, B) as b:
                dve.wait_ge(l_done, b + 1)
                nc.vector.tensor_tensor(lg[:, bass.ds(b * TILES, TILES), :], l_ps[:],
                                        b2[:, :].unsqueeze(1).to_broadcast([P, TILES, E0]), ALU.add).then_inc(lg_ready, 1)

        top2_gates(nc, K, a, block, lg, (lg_ready, B + 1), E0, gates, "sum", pack_ps, packT, gates_d)


def shared_conv(nc, io, K, y):
    zT = K["zT"]
    with ExitStack() as ctx:
        a = Alloc(nc, ctx, "shared")
        w1 = a.sb("w1", [P, TAPS_S, HID])
        w2 = a.sb("w2", [P, HJ, P])
        b1 = a.sb("b1", [P, HJ])
        b2 = a.sb("b2", [P, 1])
        hid = [a.sb(f"hid{i}", [P, HJ, HALF]) for i in range(2)]
        part = a.sb("part", [P, HALF])
        h_ps = [a.ps(f"h_ps{j}", [P, BANK]) for j in range(HJ)]
        o_ps = [a.ps(f"o_ps{i}", [P, BANK]) for i in range(2)]
        w_in, h_full, h_done, o_full, y_done, part_done = (a.sem(n) for n in (
            "w_in", "h_full", "h_done", "o_full", "y_done", "part_done"))
        block = ctx.enter_context(nc.Block())

        @block.sync
        def _(sp):
            for dst, src in ((w1, "sh_w1"), (w2, "sh_w2"), (b1, "sh_b1"), (b2, "sh_b2")):
                sp.dma_start(dst[:], io[src]).then_inc(w_in, 16)

        @block.tensor
        def _(pe):
            pe.wait_ge(w_in, 64)

            def first(b, i):
                for j in range(HJ):
                    pe.wait_ge(h_done, b * (2 * HJ) + (i * HJ + j + 1))
                    for k in range(TAPS_S):
                        mm = nc.tensor.matmul(h_ps[j][:, 0:HALF], w1[:, k, j * P:(j + 1) * P],
                                              z_chunk(zT, b, i, k - TAPS_S // 2), start=(k == 0), stop=(k == TAPS_S - 1))
                    mm.then_inc(h_full, 1)

            def second(b, i):
                pe.wait_ge(h_done, b * (2 * HJ) + (i * HJ + 2 * HJ))
                pe.wait_ge(y_done, b * 2 + (i + 1))
                for j in range(HJ):
                    mm = nc.tensor.matmul(o_ps[i][:, 0:HALF], w2[:, j, :], hid[i][:, j, :],
                                          start=(j == 0), stop=(j == HJ - 1))
                mm.then_inc(o_full, 1)

            with pe.Fori(0, B) as b:
                first(b, 0)
                first(b, 1)
                second(b, 0)
                second(b, 1)

        @block.scalar
        def _(act):
            act.sem_inc(h_done, HJ)
            act.sem_inc(o_full, 2)
            with act.Fori(0, B) as b:
                for i in range(2):
                    act.wait_ge(o_full, b * 2 + (i + 1))
                    for j in range(HJ):
                        act.wait_ge(h_full, b * (2 * HJ) + (i * HJ + j + 1))
                        nc.scalar.activation(hid[i][:, j, :], h_ps[j][:, 0:HALF], ACT.Silu,
                                             bias=b1[:, j:j + 1]).then_inc(h_done, 1)

        @block.vector
        def _(dve):
            dve.sem_inc(y_done, 2)
            dve.wait_ge(w_in, 64)
            with dve.Fori(0, B) as b:
                for i in range(2):
                    dve.wait_ge(y_done, b * 2 + (i + 2))
                    dve.wait_ge(o_full, b * 2 + (i + 3))
                    nc.vector.scalar_tensor_tensor(out=part[:], in0=o_ps[i][:, 0:HALF], scalar=b2[:, 0:1],
                                                   in1=z_chunk(zT, b, i), op0=ALU.add, op1=ALU.add).then_inc(part_done, 1)
                    dve.wait_ge(part_done, b * 2 + (i + 1))
                    nc.vector.tensor_tensor(h_chunk(y, b, i), h_chunk(y, b, i), part[:], ALU.add).then_inc(y_done, 1)


def stage2(nc, io, K, scratch):
    gates_d = nc.dram_tensor("gates0", (E0, B * LP), F32, kind="Internal").ap()
    conv_router(nc, io, K, gates_d)
    with ExitStack() as ctx:
        a = Alloc(nc, ctx, "stage2")
        y = a.sb("y", [P, B * L])
        cols = a.sb("ln_cols", [P, 2])
        experts(nc, K, scratch, "moe0", E0, "elu", io["moe0_w"], io["moe0_b2"], gates_d, y)
        shared_conv(nc, io, K, y)
        layer_norm(nc, K, "ln_ffn0", src=y, affine=cols, affine_d=io["ln_ffn0"], add=True)


STAGES[2] = stage2


def expert_layout(w1, b1, w2):
    n = w1.shape[0]
    return np.concatenate([w1, w2.reshape(n, HJ, P, P).transpose(0, 2, 1, 3).reshape(n, P, HID),
                           b1.reshape(n, HJ, P).transpose(0, 2, 1)], 2)


def stage2_layout(f):
    return {
        "iota": np.broadcast_to(np.arange(16, dtype=np.float32), (P, TOK_TILES, 16)),
        "rc_w1": f["L0_ffn_rc_w1"].transpose(1, 2, 0),
        "rc_w2": f["L0_ffn_rc_w2"].transpose(1, 2, 0),
        "rc_b1": f["L0_ffn_rc_b1"][:, None],
        "rc_b2": np.broadcast_to(f["L0_ffn_rc_b2"], (P, E0)),
        "sh_w1": f["L0_ffn_sh_w1"].transpose(1, 2, 0),
        "sh_w2": f["L0_ffn_sh_w2"][:, :, 0].T.reshape(HJ, P, P).transpose(1, 0, 2),
        "sh_b1": f["L0_ffn_sh_b1"].reshape(HJ, P).T,
        "sh_b2": f["L0_ffn_sh_b2"][:, None],
        "moe0_w": expert_layout(f["L0_ffn_e_w1"], f["L0_ffn_e_b1"], f["L0_ffn_e_w2"]),
        "moe0_b2": f["L0_ffn_e_b2"],
        "ln_ffn0": np.stack([f["L0_ffn_ln_g"], f["L0_ffn_ln_b"]], 1),
    }


E3 = 8


def plain_router(nc, io, K, name, E, w_name, b_name, gates_d, pack):
    zT = K["zT"]
    with ExitStack() as ctx:
        a = Alloc(nc, ctx, name)
        W = E if pack == "sum" else 4 * E
        w = a.sb("w", [P, E])
        bias = a.sb("bias", [P, E])
        lg = a.sb("lg", [P, TOK_TILES, E])
        gates = a.sb("gates", [P, TOK_TILES, W])
        packT = a.sb("packT", [W, B * LP])
        l_ps = a.ps("l_ps", [P, TOK_TILES, E])
        pack_ps = a.ps("pack_ps", [P, 2 * BANK])
        w_in, l_done, lg_ready = (a.sem(n) for n in ("w_in", "l_done", "lg_ready"))
        block = ctx.enter_context(nc.Block())

        @block.sync
        def _(sp):
            sp.dma_start(w[:], io[w_name]).then_inc(w_in, 16)
            if b_name:
                sp.dma_start(bias[:], io[b_name]).then_inc(w_in, 16)

        @block.tensor
        def _(pe):
            pe.wait_ge(w_in, 32 if b_name else 16)
            for b in range(B):
                for t in range(TILES):
                    at = LEAD + b * LP + t * P
                    mm = nc.tensor.matmul(l_ps[:, b * TILES + t, :], zT[:, at:at + P], w[:], start=True, stop=True)
            mm.then_inc(l_done, 1)

        @block.vector
        def _(dve):
            dve.wait_ge(l_done, 1)
            if b_name:
                dve.wait_ge(w_in, 32)
                nc.vector.tensor_tensor(lg[:], l_ps[:], bias[:, :].unsqueeze(1).to_broadcast([P, TOK_TILES, E]),
                                        ALU.add).then_inc(lg_ready, 1)
            else:
                nc.vector.tensor_copy(lg[:], l_ps[:]).then_inc(lg_ready, 1)

        top2_gates(nc, K, a, block, lg, (lg_ready, 1), E, gates, pack, pack_ps, packT, gates_d)


def stage8(nc, io, K, scratch):
    gates_d = nc.dram_tensor("gates3", (E3, B * LP), F32, kind="Internal").ap()
    with ExitStack() as ctx:
        a = Alloc(nc, ctx, "stage8")
        y = a.sb("y", [P, B * L])
        cols = a.sb("ln_cols", [P, 2])
        keep = a.sb("keep", [P, B * LP])
        with ExitStack() as ctx2:
            a2 = Alloc(nc, ctx2, "keepz")
            kept = a2.sem("kept")
            block = ctx2.enter_context(nc.Block())

            @block.vector
            def _(dve):
                nc.vector.tensor_copy(keep[:], K["zT"][:, LEAD:ZW]).then_inc(kept, 1)
                dve.wait_ge(kept, 1)

        layer_norm(nc, K, "ln_in3", affine=cols, affine_d=io["ln_in3"], src="zT")
        plain_router(nc, io, K, "router3", E3, "wg3", None, gates_d, "sum")
        experts(nc, K, scratch, "moe3", E3, ACT.Gelu_apprx_tanh, io["moe3_w"], io["moe3_b2"], gates_d, y)
        with ExitStack() as ctx2:
            a2 = Alloc(nc, ctx2, "resid3")
            done = a2.sem("done")
            block = ctx2.enter_context(nc.Block())

            @block.vector
            def _(dve):
                for b in range(B):
                    yb = y[:, b * L:(b + 1) * L]
                    nc.vector.tensor_tensor(yb, yb, keep[:, b * LP:b * LP + L], ALU.add).then_inc(done, 1)
                dve.wait_ge(done, B)
        layer_norm(nc, K, "ln_out3", src=y, affine=cols, affine_d=io["ln_out3"], add=True)


STAGES[8] = stage8


def stage8_layout(f):
    return {
        "wg3": f["L3_ffn_Wg"],
        "moe3_w": expert_layout(f["L3_ffn_W1"], f["L3_ffn_b1"], f["L3_ffn_W2"]),
        "moe3_b2": f["L3_ffn_b2"],
        "ln_in3": np.stack([f["L3_ffn_ln_g"], f["L3_ffn_ln_b"]], 1),
        "ln_out3": np.stack([f["L3_ffn_out_g"], f["L3_ffn_out_b"]], 1),
    }

def dense_attention(nc, io, K, name, R, w_name, b_name, scale):
    hT, zT = K["hT"], K["zT"]
    with ExitStack() as ctx:
        a = Alloc(nc, ctx, name)
        w = a.sb("w", [P, 2, R])
        bias = a.sb("bias", [R, 2])
        zb = a.sb("zb", [P, LP])
        z_tok = a.sb("z_tok", [P, TILES, P])
        qk = [a.sb(f"qk{j}", [R, LP]) for j in range(2)]
        probs = [a.sb(f"probs{i}", [P, LP]) for i in range(2)]
        probsT = a.sb("probsT", [P, TILES, LP])
        nmax = a.sb("nmax", [P, TILES])
        sums = a.sb("sums", [P, TILES])
        rsum = a.sb("rsum", [P, TILES])
        s_ps = [a.ps(f"s_ps{i}", [P, 2 * BANK]) for i in range(2)]
        t_ps = a.ps("t_ps", [P, 2 * BANK])
        o_ps = [a.ps(f"o_ps{i}", [P, BANK]) for i in range(2)]
        names = ("w_in", "filled", "zb_ready", "p_full", "p_copied", "zt_full", "zt_copied", "s_full", "max_ready", "exp_done",
                 "rs_ready", "scaled", "t_full", "t_copied", "o_full", "o_added")
        (w_in, filled, zb_ready, p_full, p_copied, zt_full, zt_copied, s_full, max_ready, exp_done,
         rs_ready, scaled, t_full, t_copied, o_full, o_added) = (a.sem(n) for n in names)
        block = ctx.enter_context(nc.Block())
        T = TILES

        @block.sync
        def _(sp):
            sp.dma_start(w[:], io[w_name]).then_inc(w_in, 16)
            if b_name:
                sp.dma_start(bias[:], io[b_name]).then_inc(w_in, 16)

        @block.tensor
        def _(pe):
            pe.wait_ge(w_in, 32 if b_name else 16)
            with pe.Fori(0, B) as b:
                pe.wait_ge(zb_ready, b + 1)
                for j in range(2):
                    for half in range(2):
                        if j == 0:
                            pe.wait_ge(o_added, b * 2 + (half + 1))
                        else:
                            pe.wait_ge(p_copied, b * 4 + (half + 1))
                        nc.tensor.matmul(o_ps[half][0:R, 0:HALF], w[:, j, :], zb[:, half * HALF:half * HALF + HALF],
                                         start=True, stop=True).then_inc(p_full, 1)
                pe.wait_ge(t_copied, b * T + 1)
                for t in range(T):
                    mm = nc.tensor.transpose(t_ps[:, t * P:(t + 1) * P], zb[:, t * P:(t + 1) * P], K["ident"][:])
                mm.then_inc(zt_full, 1)
                pe.wait_ge(p_copied, b * 4 + 4)
                for t in range(T + 1):
                    if t < T:
                        pe.wait_ge(exp_done, b * T + (t + 1))
                        nc.tensor.matmul(s_ps[t % 2][:, 0:BANK], qk[0][:, t * P:(t + 1) * P], qk[1][:, 0:BANK],
                                         start=True, stop=True)
                        nc.tensor.matmul(s_ps[t % 2][:, BANK:L], qk[0][:, t * P:(t + 1) * P], qk[1][:, BANK:L],
                                         start=True, stop=True).then_inc(s_full, 1)
                    if t >= 1:
                        i = t - 1
                        pe.wait_ge(scaled, b * T + (i + 1))
                        if i == 0:
                            pe.wait_ge(zt_copied, b + 1)
                        else:
                            pe.wait_ge(t_copied, b * T + (i + 1))
                        for j in range(T):
                            mm = nc.tensor.transpose(t_ps[:, j * P:(j + 1) * P], probs[i % 2][:, j * P:(j + 1) * P],
                                                     K["ident"][:])
                        mm.then_inc(t_full, 1)
                pe.wait_ge(t_copied, b * T + (T + 1))
                for half in range(2):
                    for j in range(T):
                        mm = nc.tensor.matmul(o_ps[half][:, 0:HALF], z_tok[:, j, :],
                                              probsT[:, j, half * HALF:half * HALF + HALF], start=(j == 0), stop=(j == T - 1))
                    mm.then_inc(o_full, 1)

        def copy_turned(eng, copy, b, t):
            eng.wait_ge(t_full, b * T + (t + 1))
            copy(probsT[:, :, t * P:(t + 1) * P], t_ps[:, 0:LP].rearrange("p (j i) -> p j i", j=T)).then_inc(t_copied, 1)

        @block.scalar
        def _(act):
            act.sem_inc(exp_done, 2)
            act.wait_ge(filled, 4)
            with act.Fori(0, B) as b:
                for t in range(T):
                    act.wait_ge(max_ready, b * T + (t + 1))
                    act.wait_ge(t_full, b * T + (t + 1 - 2)) if t >= 2 else act.wait_ge(o_full, b * 2 + 2)
                    nc.scalar.activation(probs[t % 2][:, 0:L], s_ps[t % 2][:, 0:L], ACT.Exp, bias=nmax[:, t:t + 1],
                                         accum_out=sums[:, t:t + 1]).then_inc(exp_done, 1)
                    if t >= 1 and t % 2 == 0:
                        copy_turned(act, nc.scalar.copy, b, t - 1)
                copy_turned(act, nc.scalar.copy, b, T - 1)

        @block.vector
        def _(dve):
            dve.sem_inc(o_added, 2)
            dve.sem_inc(t_copied, 1)
            dve.sem_inc(o_full, 2)
            for x in (probs[0][:, L:LP], probs[1][:, L:LP], qk[0][:, L:LP], bias[:] if not b_name else nmax[:]):
                nc.vector.memset(x, 0.0).then_inc(filled, 1)
            dve.wait_ge(filled, 4)
            dve.wait_ge(w_in, 32 if b_name else 16)
            with dve.Fori(0, B) as b:
                dve.wait_ge(o_full, b * 2 + 2)
                nc.vector.tensor_copy(zb[:], zT[:, bass.ds(b * LP + LEAD, LP)]).then_inc(zb_ready, 1)
                for j in range(2):
                    for half in range(2):
                        dve.wait_ge(p_full, b * 4 + (j * 2 + half + 1))
                        nc.vector.tensor_scalar(qk[j][:, half * HALF:half * HALF + HALF], o_ps[half][0:R, 0:HALF],
                                                bias[:, j:j + 1], (scale, 1.0)[j], ALU.add, ALU.mult).then_inc(p_copied, 1)
                dve.wait_ge(zt_full, b + 1)
                nc.vector.tensor_copy(z_tok[:], t_ps[:, 0:LP].rearrange("p (t c) -> p t c", t=T)).then_inc(zt_copied, 1)
                for t in range(T + 1):
                    if t < T:
                        dve.wait_ge(s_full, b * T + (t + 1))
                        nc.vector.tensor_reduce(nmax[:, t:t + 1], s_ps[t % 2][:, 0:L], AX.X, ALU.max,
                                                negate=True).then_inc(max_ready, 1)
                    if t >= 1:
                        i = t - 1
                        dve.wait_ge(exp_done, b * T + (i + 3))
                        nc.vector.reciprocal(rsum[:, i:i + 1], sums[:, i:i + 1]).then_inc(rs_ready, 1)
                        dve.wait_ge(rs_ready, b * T + (i + 1))
                        nc.vector.tensor_scalar(probs[i % 2][:, 0:L], probs[i % 2][:, 0:L], rsum[:, i:i + 1], None,
                                                ALU.mult).then_inc(scaled, 1)
                        if i % 2 == 0:
                            copy_turned(dve, nc.vector.tensor_copy, b, i)
                for half in range(2):
                    dve.wait_ge(o_full, b * 2 + (half + 3))
                    nc.vector.tensor_tensor(h_chunk(hT, b, half), h_chunk(hT, b, half), o_ps[half][:, 0:HALF],
                                            ALU.add).then_inc(o_added, 1)


STAGES[3] = lambda nc, io, K, scratch: dense_attention(nc, io, K, "attn1", P, "attn1_w", "attn1_b", float(P) ** -0.5)
STAGES[5] = lambda nc, io, K, scratch: dense_attention(nc, io, K, "attn2", 10, "attn2_w", None, 512.0 ** -0.5)


def dense_attention_layout(f):
    return {
        "attn1_w": np.stack([f["L1_attn_Wq"], f["L1_attn_Wk"]], 1),
        "attn1_b": np.stack([f["L1_attn_bq"], f["L1_attn_bk"]], 1),
        "attn2_w": np.stack([f["L2_attn_W1"], f["L2_attn_W2"].T], 1),
    }


E1 = 8
PICKS = 2 * B


def pooled_gates(nc, io, K, weight_cols, expert_at):
    zT = K["zT"]
    with ExitStack() as ctx:
        a = Alloc(nc, ctx, "pool")
        aw = a.sb("aw", [P, 1])
        ab = a.sb("ab", [1, 1])
        gw = a.sb("gw", [P, E1])
        gb = a.sb("gb", [1, E1])
        ones = a.sb("ones", [1, P])
        row = a.sb("row", [1, L])
        mx = a.sb("mx", [1, 4])
        aw_all = a.sb("aw_all", [P, L])
        prod = a.sb("prod", [P, L])
        pooled = a.sb("pooled", [P, B])
        g = a.sb("g", [1, E1])
        best = a.sb("best", [1, 8])
        at = a.sb("at", [1, 8], U32)
        w8 = a.sb("w8", [1, 4])
        wts = a.sb("wts", [1, PICKS])
        s_ps = a.ps("s_ps", [P, 2 * BANK])
        b_ps = a.ps("b_ps", [P, 2 * BANK])
        g_ps = a.ps("g_ps", [P, BANK])
        w_ps = a.ps("w_ps", [P, BANK])
        w_in, s_full, exp_in, exp_done, row_ready, b_full, pooled_ready, g_full, gexp_in, gexp_done, wts_ready, w_full, chain, chain2, filled = (
            a.sem(n) for n in ("w_in", "s_full", "exp_in", "exp_done", "row_ready", "b_full", "pooled_ready", "g_full",
                               "gexp_in", "gexp_done", "wts_ready", "w_full", "chain", "chain2", "filled"))
        block = ctx.enter_context(nc.Block())

        @block.sync
        def _(sp):
            for dst, src in ((aw, "pool_w"), (ab, "pool_b"), (gw, "gate1_w"), (gb, "gate1_b")):
                sp.dma_start(dst[:], io[src]).then_inc(w_in, 16)

        @block.tensor
        def _(pe):
            pe.wait_ge(w_in, 64)
            pe.wait_ge(filled, 1)
            for b in range(B):
                z0 = LEAD + b * LP
                if b >= 1:
                    pe.wait_ge(exp_done, b)
                nc.tensor.matmul(s_ps[0:1, 0:BANK], aw[:], zT[:, z0:z0 + BANK], start=True, stop=True)
                nc.tensor.matmul(s_ps[0:1, BANK:L], aw[:], zT[:, z0 + BANK:z0 + L], start=True, stop=True).then_inc(s_full, 1)
                pe.wait_ge(row_ready, b + 1)
                nc.tensor.matmul(b_ps[:, 0:BANK], ones[:], row[:, 0:BANK], start=True, stop=True)
                nc.tensor.matmul(b_ps[:, BANK:L], ones[:], row[:, BANK:L], start=True, stop=True).then_inc(b_full, 1)
                pe.wait_ge(pooled_ready, b + 1)
                nc.tensor.matmul(g_ps[0:1, 0:E1], pooled[:, b:b + 1], gw[:], start=True, stop=True).then_inc(g_full, 1)
            pe.wait_ge(wts_ready, 1)
            nc.tensor.matmul(w_ps[:, 0:PICKS], ones[:], wts[:], start=True, stop=True).then_inc(w_full, 1)

        @block.scalar
        def _(act):
            for b in range(B):
                act.wait_ge(exp_in, b + 1)
                nc.scalar.activation(row[:], row[:], ACT.Exp, bias=mx[:, 0:1],
                                     accum_out=mx[:, 1:2]).then_inc(exp_done, 1)
                act.wait_ge(gexp_in, b + 1)
                nc.scalar.activation(g[:], g[:], ACT.Exp, bias=mx[:, 2:3], accum_out=mx[:, 3:4]).then_inc(gexp_done, 1)

        @block.vector
        def _(dve):
            nc.vector.memset(ones[:], 1.0).then_inc(filled, 1)
            dve.wait_ge(w_in, 64)
            c = Chain(dve, chain)
            for b in range(B):
                dve.wait_ge(s_full, b + 1)
                c.link(nc.vector.tensor_scalar(row[:], s_ps[0:1, 0:L], ab[:, 0:1], None, ALU.add))
                nc.vector.tensor_reduce(mx[:, 0:1], row[:], AX.X, ALU.max, negate=True).then_inc(exp_in, 1)
                dve.wait_ge(exp_done, b + 1)
                c.link(nc.vector.reciprocal(w8[:, 0:1], mx[:, 1:2]))
                nc.vector.tensor_scalar(row[:], row[:], w8[:, 0:1], None, ALU.mult).then_inc(row_ready, 1)
                dve.wait_ge(b_full, b + 1)
                z0 = LEAD + b * LP
                c.link(nc.vector.tensor_tensor(prod[:], zT[:, z0:z0 + L], b_ps[:, 0:L], ALU.mult))
                nc.vector.reduce_sum(pooled[:, b:b + 1], prod[:], AX.X).then_inc(pooled_ready, 1)
                dve.wait_ge(g_full, b + 1)
                c.link(nc.vector.tensor_tensor(g[:], g_ps[0:1, 0:E1], gb[:], ALU.add))
                nc.vector.tensor_reduce(mx[:, 2:3], g[:], AX.X, ALU.max, negate=True).then_inc(gexp_in, 1)
                dve.wait_ge(gexp_done, b + 1)
                c.link(nc.vector.reciprocal(w8[:, 1:2], mx[:, 3:4]))
                c.link(nc.vector.tensor_scalar(g[:], g[:], w8[:, 1:2], None, ALU.mult))
                c.link(nc.vector.max(best[:], g[:]))
                c.link(nc.vector.max_index(at[:], best[:], g[:]))
                c.link(nc.vector.tensor_copy(expert_at[:, 2 * b:2 * b + 2], at[:, 0:2]))
                c.link(nc.vector.tensor_tensor(w8[:, 2:3], best[:, 0:1], best[:, 1:2], ALU.add))
                c.link(nc.vector.tensor_scalar(w8[:, 2:3], w8[:, 2:3], 1e-9, None, ALU.add))
                c.link(nc.vector.reciprocal(w8[:, 3:4], w8[:, 2:3]))
                c.link(nc.vector.tensor_scalar(wts[:, 2 * b:2 * b + 2], best[:, 0:2], w8[:, 3:4], None, ALU.mult))
            dve.sem_inc(wts_ready, 1)
            dve.wait_ge(w_full, 1)
            c.link(nc.vector.tensor_copy(weight_cols[:], w_ps[:, 0:PICKS]))


def picked_experts(nc, io, K, weight_cols, expert_at):
    hT, zT = K["hT"], K["zT"]
    with ExitStack() as ctx:
        a = Alloc(nc, ctx, "picked")
        WID = 2 * HID + HJ + 1
        w = [a.sb(f"w{i}", [P, WID]) for i in range(2)]
        hid = [a.sb(f"hid{i}", [P, HJ, HALF]) for i in range(2)]
        eo = [a.sb(f"eo{i}", [P, HALF]) for i in range(2)]
        h_ps = [a.ps(f"h_ps{j}", [P, BANK]) for j in range(HJ)]
        o_ps = [a.ps(f"o_ps{i}", [P, BANK]) for i in range(2)]
        w_in = a.sems("w_in", 2)
        h_full, h_done, o_full, eo_done, added, passed = (a.sem(n) for n in ("h_full", "h_done", "o_full", "eo_done", "added", "passed"))
        block = ctx.enter_context(nc.Block())

        @block.sync
        def _(sp):
            for n in range(PICKS):
                if n >= 2:
                    sp.wait_ge(added, 2 * (n - 1))
                e = sp.value_load(expert_at[0:1, n:n + 1], min_val=0, max_val=E1 - 1)
                sp.dma_start(w[n % 2][:], io["moe1_w"][bass.ds(e, 1), :, :].squeeze(0)).then_inc(w_in[n % 2], 16)

        @block.tensor
        def _(pe):
            def first(n, i):
                b, q = n // 2, 2 * n + i
                if i == 0:
                    pe.wait_ge(w_in[n % 2], 16 * (n // 2 + 1))
                for j in range(HJ):
                    if q >= 1:
                        pe.wait_ge(h_done, (q - 1) * HJ + j + 1)
                    at = LEAD + b * LP + i * HALF
                    nc.tensor.matmul(h_ps[j][:, 0:HALF], w[n % 2][:, j * P:(j + 1) * P], zT[:, at:at + HALF],
                                     start=True, stop=True).then_inc(h_full, 1)

            def second(n, i):
                q = 2 * n + i
                pe.wait_ge(h_done, q * HJ + HJ)
                if q >= 2:
                    pe.wait_ge(eo_done, q - 1)
                for j in range(HJ):
                    mm = nc.tensor.matmul(o_ps[i][:, 0:HALF], w[n % 2][:, HID + j * P:HID + (j + 1) * P],
                                          hid[i][:, j, :], start=(j == 0), stop=(j == HJ - 1))
                mm.then_inc(o_full, 1)

            items = [(n, i) for n in range(PICKS) for i in range(2)]
            for x, (n, i) in enumerate(items):
                first(n, i)
                if x >= 1:
                    second(*items[x - 1])
            second(*items[-1])

        @block.scalar
        def _(act):
            def output(q):
                n, i = q // 2, q % 2
                act.wait_ge(o_full, q + 1)
                if q >= 2:
                    act.wait_ge(added, q - 1)
                nc.scalar.activation(eo[i][:], o_ps[i][:, 0:HALF], ACT.Gelu,
                                     bias=w[n % 2][:, 2 * HID + HJ:2 * HID + HJ + 1]).then_inc(eo_done, 1)

            for q in range(2 * PICKS):
                n, i = q // 2, q % 2
                for j in range(HJ):
                    act.wait_ge(h_full, q * HJ + j + 1)
                    nc.scalar.activation(hid[i][:, j, :], h_ps[j][:, 0:HALF], ACT.Gelu,
                                         bias=w[n % 2][:, 2 * HID + j:2 * HID + j + 1]).then_inc(h_done, 1)
                if q >= 1:
                    output(q - 1)
            output(2 * PICKS - 1)

        @block.vector
        def _(dve):
            for q in range(2 * PICKS):
                n, i = q // 2, q % 2
                b = n // 2
                if q >= 2:
                    dve.wait_ge(added, q - 1)
                dve.wait_ge(eo_done, q + 1)
                h = hT[:, b * L + i * HALF:b * L + (i + 1) * HALF]
                nc.vector.scalar_tensor_tensor(out=h, in0=eo[i][:], scalar=weight_cols[:, n:n + 1], in1=h,
                                               op0=ALU.mult, op1=ALU.add).then_inc(added, 1)


def stage4(nc, io, K, scratch):
    with ExitStack() as ctx:
        a = Alloc(nc, ctx, "stage4")
        weight_cols = a.sb("weight_cols", [P, PICKS])
        expert_at = a.sb("expert_at", [1, PICKS], U32)
        pooled_gates(nc, io, K, weight_cols, expert_at)
        picked_experts(nc, io, K, weight_cols, expert_at)


STAGES[4] = stage4


def stage4_layout(f):
    w = expert_layout(f["L1_ffn_w1"], f["L1_ffn_b1"], f["L1_ffn_w2"])
    return {
        "pool_w": f["L1_ffn_attn_w"],
        "pool_b": f["L1_ffn_attn_b"][None, :],
        "gate1_w": f["L1_ffn_gate_w"],
        "gate1_b": f["L1_ffn_gate_b"][None, :],
        "moe1_w": np.concatenate([w, f["L1_ffn_b2"][:, :, None]], 2),
    }

E2 = 8
STEPS = B
GATES = (0, 2, 3, 1)
RING = 6


def recurrent_experts(nc, io, K, gates_d):
    hT, zT = K["hT"], K["zT"]
    with ExitStack() as ctx:
        a = Alloc(nc, ctx, "lstm")
        WID = 4 * P + 4 * P + P + 4
        w = [a.sb(f"w{i}", [P, WID]) for i in range(2)]
        rows = [[a.sb(f"row{i}_{r}", [P, B * LP]) for r in range(4)] for i in range(2)]
        bo = a.sb("bo", [2 * E2, P])
        gT = a.sb("gT", [2 * E2, B * LP])
        xm = [a.sb(f"xm{i}", [P, HALF]) for i in range(4)]
        gate = [[a.sb(f"gate{i}_{g}", [P, HALF]) for g in range(4)] for i in range(2)]
        cell = [a.sb(f"cell{i}", [P, HALF]) for i in range(4)]
        state = [a.sb(f"state{i}", [P, HALF]) for i in range(4)]
        wstate = [a.sb(f"wstate{i}", [P, HALF]) for i in range(4)]
        tc = [a.sb(f"tc{i}", [P, HALF]) for i in range(2)]
        tmp = a.sb("tmp", [P, HALF])
        g_ps = [a.ps(f"g_ps{i}", [P, BANK]) for i in range(RING)]
        o_ps = [a.ps(f"o_ps{i}", [P, BANK]) for i in range(2)]
        w_in = a.sems("w_in", 2)
        names = ("rows_in", "b_full", "b_added", "xm_ready", "g_full", "g_read", "c_ready", "tc_ready", "h_ready",
                 "hw_ready", "o_full", "y_done", "chain")
        (rows_in, b_full, b_added, xm_ready, g_full, g_read, c_ready, tc_ready, h_ready,
         hw_ready, o_full, y_done, chain) = (a.sem(n) for n in names)
        block = ctx.enter_context(nc.Block())

        PER = 4 * STEPS
        ITEMS = 2 * PER
        GPE = 3 * 4 + 4 * (PER - 4)
        GPT = 2 * GPE
        OPT = 2 * 2 * STEPS

        def parts(x):
            q = x % PER
            return x // PER, q // 4, q // 2 % 2, q % 2

        def gates_of(x):
            return GATES[:3] if parts(x)[1] == 0 else GATES

        def g_base(x):
            e, q = x // PER, x % PER
            return e * GPE + (3 * q if q < 4 else 12 + 4 * (q - 4))

        def out_index(e, s, i):
            return e * 2 * STEPS + 2 * s + i

        def cols(s, i):
            return slice(s * LP + i * HALF, s * LP + i * HALF + HALF)

        def h_cols(s, i):
            return hT[:, s * L + i * HALF:s * L + i * HALF + HALF]

        @block.sync
        def _(sp):
            sp.dma_start(bo[:], io["lstm_bo"]).then_inc(rows_in, 16)
            sp.dma_start(gT[:], gates_d[2 * E2:4 * E2, :]).then_inc(rows_in, 16)
            with sp.Fori(0, E2 // 2) as m:
                for e in range(2):
                    sp.wait_ge(y_done, m * OPT + (e * 2 * STEPS + 2 * STEPS))
                    sp.dma_start(w[e][:], io["lstm_w"][bass.ds(m * 2 + e, 1), :, :].squeeze(0)).then_inc(w_in[e], 16)
                    for r in range(4):
                        sp.dma_start(rows[e][r][:], gates_d[bass.ds(m * 2 + (r * E2 + e), 1), :].to_broadcast([P, B * LP])
                                     ).then_inc(w_in[e], 16)

        @block.gpsimd
        def _(pool):
            pool.sem_inc(hw_ready, 4)

            def mask(m, x):
                e, s, k, i = parts(x)
                if x % PER == 0:
                    pool.wait_ge(w_in[e], m * 80 + 80)
                back = g_base(x - 4) + len(gates_of(x - 4))
                pool.wait_ge(g_full, m * GPT + (back + GPT))
                nc.gpsimd.tensor_tensor(xm[x % 4][:], zT[:, LEAD + s * LP + i * HALF:LEAD + s * LP + i * HALF + HALF],
                                        rows[e][k][:, cols(s, i)], ALU.mult).then_inc(xm_ready, 1)

            def weigh(m, x):
                e, s, k, i = parts(x)
                pool.wait_ge(h_ready, m * ITEMS + (x + 3))
                pool.wait_ge(o_full, m * OPT + (out_index(e, s, i) + 1))
                nc.gpsimd.tensor_tensor(wstate[2 * k + i][:], state[2 * k + i][:], rows[e][2 + k][:, cols(s, i)],
                                        ALU.mult).then_inc(hw_ready, 1)

            with pool.Fori(0, E2 // 2) as m:
                mask(m, 0)
                mask(m, 1)
                for x in range(ITEMS):
                    if x + 2 < ITEMS:
                        mask(m, x + 2)
                    if x >= 1:
                        weigh(m, x - 1)
                weigh(m, ITEMS - 1)

        @block.tensor
        def _(pe):
            pe.wait_ge(rows_in, 32)
            for c, (b, half) in enumerate(CHUNKS):
                if c >= 2:
                    pe.wait_ge(b_added, c - 1)
                nc.tensor.matmul(o_ps[c % 2][:, 0:HALF], bo[:], gT[:, cols(b, half)], start=True, stop=True).then_inc(b_full, 1)
            pe.wait_ge(b_added, NCH)

            def gates(m, x):
                e, s, k, i = parts(x)
                if x % PER == 0:
                    pe.wait_ge(w_in[e], m * 80 + 80)
                pe.wait_ge(xm_ready, m * ITEMS + (x + 1))
                for y, g in enumerate(gates_of(x)):
                    n = g_base(x) + y
                    bank = g_ps[n % RING][:, 0:HALF]
                    pe.wait_ge(g_read, m * GPT + (n + 1))
                    mm = nc.tensor.matmul(bank, w[e][:, g * P:(g + 1) * P], xm[x % 4][:], start=True, stop=(s == 0))
                    if s > 0:
                        if y == 0:
                            pe.wait_ge(h_ready, m * ITEMS + (x - 4 + 3))
                        mm = nc.tensor.matmul(bank, w[e][:, 4 * P + g * P:4 * P + (g + 1) * P], state[2 * k + i][:],
                                              start=False, stop=True)
                    mm.then_inc(g_full, 1)

            def output(m, e, s, i):
                n = out_index(e, s, i)
                pe.wait_ge(hw_ready, m * ITEMS + (e * PER + 4 * s + 2 + i + 5))
                pe.wait_ge(y_done, m * OPT + (n + OPT - 1))
                for k in range(2):
                    mm = nc.tensor.matmul(o_ps[i][:, 0:HALF], w[e][:, 8 * P:9 * P], wstate[2 * k + i][:],
                                          start=(k == 0), stop=(k == 1))
                mm.then_inc(o_full, 1)

            with pe.Fori(0, E2 // 2) as m:
                for x in range(ITEMS):
                    gates(m, x)
                    if x >= 4 and x % 4 < 2:
                        e, s, k, i = parts(x - 4)
                        output(m, e, s, i)
                for i in range(2):
                    output(m, 1, STEPS - 1, i)

        @block.scalar
        def _(act):
            act.sem_inc(g_read, RING)
            act.sem_inc(tc_ready, 4)

            def squash(m, x):
                act.wait_ge(c_ready, m * ITEMS + (x + 1))
                nc.scalar.activation(tc[x % 2][:], cell[x % 4][:], ACT.Tanh).then_inc(tc_ready, 1)

            with act.Fori(0, E2 // 2) as m:
                for x in range(ITEMS):
                    e, s, k, i = parts(x)
                    act.wait_ge(h_ready, m * ITEMS + (x + 1))
                    for y, g in enumerate(gates_of(x)):
                        n = g_base(x) + y
                        act.wait_ge(g_full, m * GPT + (n + 1 + GPT))
                        nc.scalar.activation(gate[x % 2][g][:], g_ps[n % RING][:, 0:HALF], ACT.Tanh if g == 2 else ACT.Sigmoid,
                                             bias=w[e][:, 9 * P + g:9 * P + g + 1]).then_inc(g_read, 1)
                    if x >= 1:
                        squash(m, x - 1)
                squash(m, ITEMS - 1)

        @block.vector
        def _(dve):
            dve.sem_inc(g_full, GPT)
            dve.sem_inc(h_ready, 2)
            dve.sem_inc(o_full, 2)
            dve.sem_inc(y_done, OPT)
            for c, (b, half) in enumerate(CHUNKS):
                dve.wait_ge(b_full, c + 1)
                h = h_cols(b, half)
                nc.vector.tensor_tensor(h, h, o_ps[c % 2][:, 0:HALF], ALU.add).then_inc(b_added, 1)
            dve.wait_ge(b_added, NCH)

            def cells(m, x, c):
                e, s, k, i = parts(x)
                dve.wait_ge(g_read, m * GPT + (g_base(x) + len(gates_of(x)) + RING))
                dve.wait_ge(tc_ready, m * ITEMS + (x + 1))
                g = gate[x % 2]
                if s == 0:
                    nc.vector.tensor_tensor(cell[x % 4][:], g[0][:], g[2][:], ALU.mult).then_inc(c_ready, 1)
                else:
                    nc.vector.tensor_tensor(cell[x % 4][:], g[1][:], cell[x % 4][:], ALU.mult)
                    c.link(nc.vector.tensor_tensor(tmp[:], g[0][:], g[2][:], ALU.mult))
                    nc.vector.tensor_tensor(cell[x % 4][:], cell[x % 4][:], tmp[:], ALU.add).then_inc(c_ready, 1)

            def states(m, x):
                e, s, k, i = parts(x)
                dve.wait_ge(tc_ready, m * ITEMS + (x + 5))
                dve.wait_ge(hw_ready, m * ITEMS + (x + 1))
                nc.vector.tensor_tensor(state[x % 4][:], gate[x % 2][3][:], tc[x % 2][:], ALU.mult).then_inc(h_ready, 1)

            def add(m, e, s, i):
                n = out_index(e, s, i)
                dve.wait_ge(o_full, m * OPT + (n + 3))
                h = h_cols(s, i)
                nc.vector.tensor_tensor(h, h, o_ps[i][:, 0:HALF], ALU.add).then_inc(y_done, 1)

            with dve.Fori(0, E2 // 2) as m:
                c = Chain(dve, chain, m, 2 * (PER - 4))
                for x in range(ITEMS):
                    cells(m, x, c)
                    if x >= 1:
                        states(m, x - 1)
                    if x >= 5 and x % 4 in (1, 2):
                        e, s, k, i = parts(x - 5)
                        add(m, e, s, i)
                states(m, ITEMS - 1)
                for i in range(2):
                    add(m, 1, STEPS - 1, i)
                c.end()


def stage6(nc, io, K, scratch):
    gates_d = nc.dram_tensor("gates2", (4 * E2, B * LP), F32, kind="Internal").ap()
    plain_router(nc, io, K, "router2", E2, "router2_w", "router2_b", gates_d, "slots")
    recurrent_experts(nc, io, K, gates_d)


STAGES[6] = stage6


def stage6_layout(f):
    return {
        "router2_w": f["L2_ffn_router_w"],
        "router2_b": np.broadcast_to(f["L2_ffn_router_b"], (P, E2)),
        "lstm_w": np.concatenate([f["L2_ffn_Wi"], f["L2_ffn_Wh"], f["L2_ffn_Wo"],
                                  f["L2_ffn_b"].reshape(E2, 4, P).transpose(0, 2, 1)], 2),
        "lstm_bo": np.concatenate([f["L2_ffn_bo"], f["L2_ffn_bo"]], 0),
    }


HEADS3 = 16
D3 = P // 4
GROUPS = 4
HPG = HEADS3 // GROUPS
WM = 3 * P + 2


def causal_weights(nc, io, K, merged_d, z_d):
    with ExitStack() as ctx:
        a = Alloc(nc, ctx, "causw")
        wl = a.sb("wl", [P, HEADS3, P])
        bl = a.sb("bl", [P, HEADS3])
        wqkv = a.sb("wqkv", [P, HEADS3, 3 * D3])
        wo = a.sb("wo", [P, GROUPS, P])
        bo = a.sb("bo", [P, 1])
        merged = a.sb("merged", [P, GROUPS, WM])
        bv = a.sb("bv", [P, GROUPS])
        shift = a.sb("shift", [P, 1])
        m_ps = [a.ps(f"m_ps{g}", [P, BANK]) for g in range(GROUPS)]
        b_ps = [a.ps(f"b_ps{j}", [P, BANK]) for j in range(3)]
        o_ps = a.ps("o_ps", [P, BANK])
        w_in, m_full, b_full, m_copied, bv_ready, o_full, shifted, stored, chain = (a.sem(n) for n in (
            "w_in", "m_full", "b_full", "m_copied", "bv_ready", "o_full", "shifted", "stored", "chain"))
        block = ctx.enter_context(nc.Block())

        @block.sync
        def _(sp):
            for dst, src in ((wl, "caus_wl"), (bl, "caus_bl"), (wqkv, "caus_wqkv"), (wo, "caus_wo"), (bo, "caus_bo")):
                sp.dma_start(dst[:], io[src]).then_inc(w_in, 16)
            sp.dma_start(z_d.rearrange("b p c -> p b c"),
                         K["zT"][:, LEAD:LEAD + B * LP].rearrange("p (b c) -> p b c", b=B)).then_inc(stored, 16)
            sp.wait_ge(m_copied, GROUPS + 2)
            sp.dma_start(merged_d.rearrange("g p w -> p g w"), merged[:]).then_inc(stored, 16)
            sp.wait_ge(stored, 32)

        @block.tensor
        def _(pe):
            pe.wait_ge(w_in, 80)
            for g in range(GROUPS):
                for hh in range(HPG):
                    h = g * HPG + hh
                    mm = nc.tensor.matmul(m_ps[g][:, hh * 3 * D3:(hh + 1) * 3 * D3], wl[:, h, :], wqkv[:, h, :],
                                          start=True, stop=True)
                mm.then_inc(m_full, 1)
            for j in range(3):
                for h in range(HEADS3):
                    g, hh = h // HPG, h % HPG
                    mm = nc.tensor.matmul(b_ps[j][hh * D3:(hh + 1) * D3, g:g + 1], wqkv[:, h, j * D3:(j + 1) * D3],
                                          bl[:, h:h + 1], start=True, stop=True)
                mm.then_inc(b_full, 1)
            pe.wait_ge(bv_ready, 1)
            for g in range(GROUPS):
                mm = nc.tensor.matmul(o_ps[:, 0:1], wo[:, g, :], bv[:, g:g + 1], start=(g == 0), stop=(g == GROUPS - 1))
            mm.then_inc(o_full, 1)

        @block.vector
        def _(dve):
            for g in range(GROUPS):
                dve.wait_ge(m_full, g + 1)
                nc.vector.tensor_copy(merged[:, g, 0:3 * P].rearrange("p (j h d) -> p h j d", j=3, h=HPG),
                                      m_ps[g][:, 0:3 * P].rearrange("p (h j d) -> p h j d", h=HPG, j=3)).then_inc(m_copied, 1)
            dve.wait_ge(b_full, 3)
            for j in range(2):
                nc.vector.tensor_copy(merged[:, :, 3 * P + j:3 * P + j + 1], b_ps[j][:, 0:GROUPS].unsqueeze(2)).then_inc(m_copied, 1)
            nc.vector.tensor_copy(bv[:], b_ps[2][:, 0:GROUPS]).then_inc(bv_ready, 1)
            dve.wait_ge(o_full, 1)
            dve.wait_ge(w_in, 80)
            nc.vector.tensor_tensor(shift[:], o_ps[:, 0:1], bo[:], ALU.add).then_inc(chain, 1)
            dve.wait_ge(chain, 1)
            nc.vector.tensor_scalar(K["hT"][:], K["hT"][:], shift[:, 0:1], None, ALU.add).then_inc(shifted, 1)


def causal_attention(nc, io, K, merged_d, z_d):
    hT = K["hT"]
    with ExitStack() as ctx:
        a = Alloc(nc, ctx, "caus")
        T = TILES
        W = [min((t + 1) * P, L) for t in range(T)]
        PARTS = [1 if w <= BANK else 2 for w in W]
        wm = a.sb("wm", [P, WM])
        wo = a.sb("wo", [P, P])
        identb = a.sb("identb", [P, P], BF16)
        mask32 = a.sb("mask32", [P, P])
        mask = a.sb("mask", [P, P], BF16)
        zb = a.sb("zb", [P, LP])
        q_sb = a.sb("q_sb", [P, LP])
        k_sb = a.sb("k_sb", [P, LP])
        v_tok = a.sb("v_tok", [P, T, P])
        RING = 4
        probs = [a.sb(f"probs{i}", [P, LP]) for i in range(RING)]
        probsT = [a.sb(f"probsT{i}", [P, T, LP]) for i in range(2)]
        nmax = a.sb("nmax", [P, HPG * T])
        sums = a.sb("sums", [P, HPG * T])
        rsum = a.sb("rsum", [P, HPG * T])
        fT = a.sb("fT", [P, L])
        s_ps = [a.ps(f"s_ps{i}", [P, 2, BANK]) for i in range(2)]
        t_ps = [a.ps(f"t_ps{i}", [P, BANK]) for i in range(2)]
        f_ps = a.ps("f_ps", [P, 2 * BANK])
        t_copied = a.sems("t_copied", 2)
        names = ("w_in", "wo_in", "in_free", "masks_in", "filled", "s_full", "max_ready", "exp_done", "rs_ready", "scaled",
                 "t_full", "pv_full", "f_full", "f_copied0", "f_copied1", "passed")
        (w_in, wo_in, in_free, masks_in, filled, s_full, max_ready, exp_done, rs_ready, scaled, t_full,
         pv_full, f_full, f_copied0, f_copied1, passed) = (a.sem(n) for n in names)
        block = ctx.enter_context(nc.Block())
        X = HPG * T
        LAG = 2
        TURNS = B * GROUPS
        COLS = ((0, BANK), (BANK, L))

        def turned(x):
            t = x % T
            cuts = [0, t + 1] if t < 4 else [0, 3, t + 1]
            return [("turn", x, j0, j1) for j0, j1 in zip(cuts, cuts[1:])]

        first = [("qk", j, half) for j in range(2) for half in range(2)] + [("v", 0), ("v", 1)]
        plan = [c for x in range(X - 1) for c in turned(x)]
        plan += first[:1] + turned(X - 1) + first[1:] + [("out", 0), ("out", 1)]
        C = len(plan)
        START = len(first) // 2 + 1
        assert C % 2 == 0

        def emptied(n, through):
            last = plan.index(through)
            return [START + n * (C // 2) + len([c for c in range(last + 1) if c % 2 == i]) for i in range(2)]

        def scores_of(x, n_cols=None):
            t = x % T
            return s_ps[x % 2][:, 0:PARTS[t], 0:W[t] // PARTS[t]]

        @block.sync
        def _(sp):
            sp.dma_start(mask32[:], io["causal_mask"]).then_inc(masks_in, 16)
            sp.sem_inc(in_free, 1)
            with sp.Fori(0, B) as b:
                with sp.Fori(0, GROUPS) as g:
                    n = b * GROUPS + g
                    sp.wait_ge(in_free, n + 1)
                    sp.dma_start(wm[:], merged_d[bass.ds(g, 1), :, :].squeeze(0)).then_inc(w_in, 16)
                    sp.dma_start(zb[:], z_d[bass.ds(b, 1), :, :].squeeze(0)).then_inc(w_in, 16)
                    sp.wait_ge(in_free, n + 2)
                    sp.dma_start(wo[:], io["caus_wo_g"][bass.ds(g, 1), :, :].squeeze(0)).then_inc(wo_in, 16)
            sp.wait_ge(in_free, TURNS + 1)
            sp.dma_start(wm[:], merged_d[0]).then_inc(w_in, 16)
            sp.dma_start(zb[:], z_d[0]).then_inc(w_in, 16)

        @block.tensor
        def _(pe):
            def project(item, bank):
                if item[0] == "qk":
                    cols = slice(item[2] * HALF, (item[2] + 1) * HALF)
                    mm = nc.tensor.matmul(bank[:, 0:HALF], wm[:, item[1] * P:(item[1] + 1) * P], zb[:, cols],
                                          start=True, stop=True)
                else:
                    for i in range(T // 2):
                        t = item[1] * (T // 2) + i
                        mm = nc.tensor.matmul(bank[:, i * P:(i + 1) * P], zb[:, t * P:(t + 1) * P], wm[:, 2 * P:3 * P],
                                              start=True, stop=True)
                mm.then_inc(t_full, 1)

            pe.wait_ge(filled, RING + 4)
            pe.wait_ge(w_in, 32)
            for p, item in enumerate(first):
                if p >= 2:
                    pe.wait_ge(t_copied[p % 2], p // 2 + 1)
                project(item, t_ps[p % 2])

            with pe.Fori(0, TURNS) as n:
                def free_bank(c):
                    pe.wait_ge(t_copied[c % 2], n * (C // 2) + (START + c // 2))
                    return t_ps[c % 2]

                def scores(x):
                    hh, t = x // T, x % T
                    rows = slice(hh * D3, (hh + 1) * D3)
                    pe.wait_ge(exp_done, n * X + (x + 1))
                    wide = W[t] // PARTS[t]
                    for part in range(PARTS[t]):
                        diag = part == PARTS[t] - 1
                        mm = nc.tensor.matmul(s_ps[x % 2][:, part, 0:wide], q_sb[rows, t * P:(t + 1) * P],
                                              k_sb[rows, part * wide:(part + 1) * wide],
                                              start=True, stop=not diag, tile_position=(hh * D3, 0))
                        if diag:
                            late = W[t] - t * P
                            mm = nc.tensor.matmul(s_ps[x % 2][:, part, wide - late:wide], identb[:], mask[:, 0:late],
                                                  start=False, stop=True)
                    mm.then_inc(s_full, 1)

                def turn_probs(x):
                    pe.wait_ge(scaled, n * X + (x + 1))
                    for item in turned(x):
                        bank = free_bank(plan.index(item))
                        for i, j in enumerate(range(item[2], item[3])):
                            mm = nc.tensor.transpose(bank[:, i * P:(i + 1) * P], probs[x % RING][:, j * P:(j + 1) * P],
                                                     K["ident"][:])
                        mm.then_inc(t_full, 1)

                def values(hh, half, tiles):
                    if tiles[0] == 0:
                        last = turned(hh * T + (3, T - 1)[half])[-1]
                        for i, count in enumerate(emptied(n, last)):
                            pe.wait_ge(t_copied[i], count)
                    for j in tiles:
                        c0, c1 = max(COLS[half][0], j * P), COLS[half][1]
                        mm = nc.tensor.matmul(f_ps[hh * D3:(hh + 1) * D3, c0:c1], v_tok[:, j, hh * D3:(hh + 1) * D3],
                                              probsT[hh % 2][:, j, c0:c1], start=(j == 0), stop=(j == (3, T - 1)[half]))
                    if tiles[-1] == (3, T - 1)[half]:
                        if half == 1:
                            mm.then_inc(pv_full, 1)
                        elif hh == HPG - 1:
                            mm.then_inc(f_full, 1)

                spread = {0: [(0, [0])], 1: [(0, [1])], 2: [(0, [2, 3]), (1, [0, 1])], 3: [(1, [2, 3, 4])], 4: [(1, [5])], 5: []}
                for i in range(2):
                    pe.wait_ge(t_copied[i], n * (C // 2) + (START - 1))
                for x in range(X):
                    scores(x)
                    if x == LAG:
                        for i in range(2):
                            pe.wait_ge(t_copied[i], n * (C // 2) + START)
                        pe.sem_inc(in_free, 1)
                    if x >= LAG:
                        turn_probs(x - LAG)
                    if x >= T:
                        for half, tiles in spread[x % T]:
                            values(x // T - 1, half, tiles)
                hh = HPG - 1
                turn_probs(X - 2)
                values(hh, 0, [0, 1])
                pe.wait_ge(w_in, n * 32 + 64)
                project(first[0], free_bank(plan.index(first[0])))
                turn_probs(X - 1)
                values(hh, 0, [2, 3])
                for item in first[1:4]:
                    project(item, free_bank(plan.index(item)))
                values(hh, 1, list(range(T)))
                for item in first[4:]:
                    project(item, free_bank(plan.index(item)))
                pe.wait_ge(wo_in, n * 16 + 16)
                for half, (c0, c1) in enumerate(COLS):
                    bank = free_bank(plan.index(("out", half)))
                    pe.wait_ge((f_copied0, f_copied1)[half], n + 1)
                    nc.tensor.matmul(bank[:, 0:c1 - c0], wo[:], fT[:, c0:c1], start=True, stop=True).then_inc(t_full, 1)

        def empty_bank(eng, engine_add, copy, n, c, item, opening=False):
            bank = t_ps[c % 2]
            eng.wait_ge(t_full, c + 1 if opening else n * C + (len(first) + c + 1))
            if item[0] == "turn":
                _, x, j0, j1 = item
                hh, t = x // T, x % T
                if t < 2:
                    eng.wait_ge(pv_full, n * HPG + (hh + 1))
                wide = min(P, L - t * P)
                src = bank[:, 0:(j1 - j0) * P].rearrange("p (j i) -> p j i", j=j1 - j0)
                copy(probsT[hh % 2][:, j0:j1, t * P:t * P + wide], src[:, :, 0:wide]).then_inc(t_copied[c % 2], 1)
            elif item[0] == "qk":
                _, j, half = item
                if not opening:
                    eng.wait_ge(s_full, n * X + X)
                dst = (q_sb, k_sb)[j][:, half * HALF:(half + 1) * HALF]
                engine_add(dst, bank[:, 0:HALF], wm[:, 3 * P + j:3 * P + j + 1]).then_inc(t_copied[c % 2], 1)
            else:
                assert item[0] == "v"
                if not opening:
                    eng.wait_ge(pv_full, n * HPG + (HPG + 2))
                t0 = item[1] * (T // 2)
                copy(v_tok[:, t0:t0 + T // 2, :], bank[:, 0:T // 2 * P].rearrange("p (t c) -> p t c", c=P)).then_inc(
                    t_copied[c % 2], 1)

        @block.scalar
        def _(act):
            act.wait_ge(filled, RING + 4)

            def add(dst, src, col):
                return nc.scalar.activation(dst, src, ACT.Identity, bias=col)

            for p in (1, 3, 5):
                empty_bank(act, add, nc.scalar.copy, 0, p, first[p], opening=True)
            with act.Fori(0, TURNS) as n:
                done = 0

                def empty_through(last):
                    nonlocal done
                    end = plan.index(last) + 1
                    for c in range(done, end):
                        if c % 2 == 1:
                            empty_bank(act, add, nc.scalar.copy, n, c, plan[c])
                    done = end

                for x in range(X):
                    act.wait_ge(max_ready, n * X + (x + 1))
                    if x >= RING:
                        act.wait_ge(t_full, n * C + (len(first) + plan.index(turned(x - RING)[-1]) + 1))
                    t = x % T
                    nc.scalar.activation(probs[x % RING][:, 0:W[t]].rearrange("p (a c) -> p a c", a=PARTS[t]), scores_of(x),
                                         ACT.Exp, bias=nmax[:, x:x + 1], accum_out=sums[:, x:x + 1]).then_inc(exp_done, 1)
                    if x >= LAG:
                        empty_through(turned(x - LAG)[-1])
                empty_through(turned(X - 1)[-1])
                act.wait_ge(f_full, n + 1)
                nc.scalar.copy(fT[:, 0:BANK], f_ps[:, 0:BANK]).then_inc(f_copied0, 1)
                empty_through(first[-1])

        @block.vector
        def _(dve):
            dve.sem_inc(exp_done, 2)
            dve.sem_inc(pv_full, 2)
            for i in range(2):
                dve.sem_inc(t_copied[i], 1)
            for x in [q_sb[:, L:LP], k_sb[:, L:LP]] + [p[:, L:LP] for p in probs]:
                nc.vector.memset(x, 0.0).then_inc(filled, 1)
            nc.vector.tensor_copy(identb[:], K["ident"][:]).then_inc(filled, 1)
            dve.wait_ge(masks_in, 16)
            nc.vector.tensor_copy(mask[:], mask32[:]).then_inc(filled, 1)
            dve.wait_ge(filled, RING + 4)

            def add(dst, src, col):
                return nc.vector.tensor_scalar(dst, src, col, None, ALU.add)

            for p in (0, 2, 4):
                empty_bank(dve, add, nc.vector.tensor_copy, 0, p, first[p], opening=True)
            with dve.Fori(0, B) as b:
                with dve.Fori(0, GROUPS) as g:
                    n = b * GROUPS + g
                    done = 0

                    def empty_through(last):
                        nonlocal done
                        end = plan.index(last) + 1
                        for c in range(done, end):
                            if c % 2 == 0:
                                empty_bank(dve, add, nc.vector.tensor_copy, n, c, plan[c])
                        done = end

                    def scale(x):
                        dve.wait_ge(exp_done, n * X + (x + 3))
                        p = probs[x % RING][:, 0:W[x % T]]
                        nc.vector.reciprocal(rsum[:, x:x + 1], sums[:, x:x + 1]).then_inc(rs_ready, 1)
                        dve.wait_ge(rs_ready, n * X + (x + 1))
                        nc.vector.tensor_scalar(p, p, rsum[:, x:x + 1], None, ALU.mult).then_inc(scaled, 1)

                    for x in range(X):
                        dve.wait_ge(s_full, n * X + (x + 1))
                        nc.vector.tensor_reduce(nmax[:, x:x + 1], scores_of(x), AX.XY if PARTS[x % T] > 1 else AX.X, ALU.max,
                                                negate=True).then_inc(max_ready, 1)
                        if x >= 1:
                            scale(x - 1)
                        if x >= LAG:
                            empty_through(turned(x - LAG)[-1])
                    scale(X - 1)
                    empty_through(first[3])
                    dve.wait_ge(pv_full, n * HPG + (HPG + 2))
                    nc.vector.tensor_copy(fT[:, BANK:L], f_ps[:, BANK:L]).then_inc(f_copied1, 1)
                    empty_through(first[-1])
                    for half, (c0, c1) in enumerate(COLS):
                        c = plan.index(("out", half))
                        dve.wait_ge(t_full, n * C + (len(first) + c + 1))
                        h = hT[:, bass.ds(b * L + c0, c1 - c0)]
                        nc.vector.tensor_tensor(h, h, t_ps[c % 2][:, 0:c1 - c0], ALU.add).then_inc(t_copied[c % 2], 1)
                    dve.wait_ge(t_copied[1], n * (C // 2) + (START + C // 2))
                    apart(dve, passed)


def stage7(nc, io, K, scratch):
    merged_d = nc.dram_tensor("merged", (GROUPS, P, WM), F32, kind="Internal").ap()
    z_d = nc.dram_tensor("z_of_batch", (B, P, LP), F32, kind="Internal").ap()
    causal_weights(nc, io, K, merged_d, z_d)
    causal_attention(nc, io, K, merged_d, z_d)


STAGES[7] = stage7


def stage7_layout(f):
    qkv = np.concatenate([f["L3_attn_Wq"], f["L3_attn_Wk"], f["L3_attn_Wv"]], 2)
    wo = f["L3_attn_Wo"].T.reshape(GROUPS, P, P)
    late = np.arange(P)[None, :] > np.arange(P)[:, None]
    return {
        "caus_wl": f["L3_attn_Wl"].transpose(1, 0, 2),
        "caus_bl": f["L3_attn_bl"].T,
        "caus_wqkv": qkv.transpose(1, 0, 2),
        "caus_wo": wo.transpose(1, 0, 2),
        "caus_wo_g": wo,
        "caus_bo": f["L3_attn_bo"][:, None],
        "causal_mask": np.where(late, -1e30, 0.0).astype(np.float32),
    }


def laid_out(inputs):
    f = {k: np.asarray(v) for k, v in inputs.items()}
    io = {
        "ident": np.eye(P, dtype=np.float32),
        "mean_all": np.full((P, P), 1.0 / P, np.float32),
        "x": f["x"].transpose(2, 0, 1).reshape(P, B * S_IN),
        "tok_w": f["L0_tok_W"].reshape(P, CONTEXT, P).transpose(2, 1, 0),
        "tok_cols": np.stack([f["L0_tok_b"], f["L0_tok_gamma"], f["L0_tok_beta"]], 1),
    }
    for more in LAYOUTS:
        io.update(more(f))
    return {k: np.ascontiguousarray(v) for k, v in io.items()}


LAYOUTS = [stage1_layout, stage2_layout, stage8_layout, dense_attention_layout, stage4_layout,
           stage6_layout, stage7_layout]


def kernel(**inputs):
    import concourse.bacc as _bacc
    from concourse.bass_utils import run_bass_kernel_spmd as _run

    nc = _bacc.Bacc("TRN2", target_bir_lowering=False, num_devices=1)
    arrays, io = {}, {}
    for name, v in laid_out(inputs).items():
        arrays[f"in_{name}"] = v
        io[name] = nc.dram_tensor(f"in_{name}", v.shape, mybir.dt.from_np(v.dtype), kind="ExternalInput").ap()
    out = nc.dram_tensor("out_h", (P, B * L), F32, kind="ExternalOutput").ap()
    scratch = {}
    audio_tower(nc, io, out, scratch)
    r = _run(nc, [arrays], core_ids=[0])
    return r.results[0]["out_h"].reshape(P, B, L).transpose(1, 2, 0)
```

```python
from contextlib import ExitStack

import numpy as np

import concourse.bass as bass
from concourse import mybir

ALU = mybir.AluOpType
ACT = mybir.ActivationFunctionType
AX = mybir.AxisListType
F32 = mybir.dt.float32
BF16 = mybir.dt.bfloat16
U32 = mybir.dt.uint32
F32R = mybir.dt.float32r

P = 128
B = 4
S_IN = 750
CONTEXT = 5
L = S_IN - CONTEXT + 1
HALF = L // 2
CHUNKS = [(b, half) for b in range(B) for half in range(2)]
LN_GROUPS = ((0, 3), (3, 8))
GROUP_MAX = 5
TILES = -(-L // P)
LP = TILES * P
LEAD = 8
ZW = LEAD + B * LP
BANK = 512



class Chain:

    def __init__(self, eng, sem, turn=0, per_turn=0):
        self.eng, self.sem, self.base, self.per_turn, self.n = eng, sem, turn * per_turn, per_turn, 0

    def link(self, ins):
        self.n += 1
        ins.then_inc(self.sem, 1)
        self.eng.wait_ge(self.sem, self.base + self.n)

    def end(self):
        assert self.n == self.per_turn, (self.n, self.per_turn)


def apart(eng, passed):
    eng.sem_inc(passed, 1)


class Alloc:

    def __init__(self, nc, ctx, stage):
        self.nc, self.ctx, self.stage = nc, ctx, stage
        self.used = []
        ctx.callback(self.clear)

    def clear(self):
        if self.used:
            numbers = sorted(s.num for s in self.used)
            first = numbers[0]
            for n, after in zip(numbers, numbers[1:] + [None]):
                if after != n + 1:
                    self.nc.gpsimd.sem_clear(range(first, n + 1))
                    first = after
            self.nc.all_engine_barrier()

    def sb(self, name, shape, dt=F32):
        return self.ctx.enter_context(self.nc.sbuf_tensor(f"{self.stage}_{name}", shape, dt))

    def ps(self, name, shape, dt=F32):
        return self.ctx.enter_context(self.nc.psum_tensor(f"{self.stage}_{name}", shape, dt))

    def sem(self, name):
        self.used.append(self.ctx.enter_context(self.nc.semaphore(f"{self.stage}_{name}")))
        return self.used[-1]

    def sems(self, name, n):
        return [self.sem(f"{name}{i}") for i in range(n)]


def h_chunk(hT, b, half):
    return hT[:, bass.ds(b * L + half * HALF, HALF)]


def z_chunk(zT, b, half, shift=0):
    return zT[:, bass.ds(b * LP + (half * HALF + LEAD + shift), HALF)]


def load_constants(nc, io, K):
    with ExitStack() as ctx:
        a = Alloc(nc, ctx, "const")
        loaded = a.sem("loaded")
        filled = a.sem("filled")
        block = ctx.enter_context(nc.Block())

        @block.sync
        def _(sp):
            sp.dma_start(K["ident"][:], io["ident"]).then_inc(loaded, 16)
            sp.dma_start(K["mean_all"][:], io["mean_all"]).then_inc(loaded, 16)
            for name in ("center", "avg_rows", "spread_rows"):
                sp.dma_start(K[name][:], io[name]).then_inc(loaded, 16)
            sp.wait_ge(loaded, 80)

        @block.vector
        def _(dve):
            nc.vector.memset(K["zT"][:], 0.0).then_inc(filled, 1)
            nc.vector.memset(K["eps5"][:], 1e-5).then_inc(filled, 1)
            nc.vector.memset(K["eps4"][:], 1e-4).then_inc(filled, 1)
            dve.wait_ge(filled, 3)


def token_conv(nc, io, K):
    hT = K["hT"]
    with ExitStack() as ctx:
        a = Alloc(nc, ctx, "tok")
        x = a.sb("x", [P, B * S_IN])
        w = a.sb("w", [P, CONTEXT, P])
        cols = a.sb("cols", [P, 3])
        stats = a.sb("stats", [P, 2 * B * 6])
        mv = a.sb("mv", [P, 2])
        s = a.sb("s", [P, 4])
        acc = [a.ps(f"acc{i}", [P, BANK]) for i in range(2)]
        x_in, w_in = a.sem("x_in"), a.sem("w_in")
        conv_done, acc_used, y_done, var_done, sd_done, chain = (a.sem(n) for n in (
            "conv_done", "acc_used", "y_done", "var_done", "sd_done", "chain"))
        block = ctx.enter_context(nc.Block())

        @block.sync
        def _(sp):
            sp.dma_start(w[:], io["tok_w"]).then_inc(w_in, 16)
            sp.dma_start(cols[:], io["tok_cols"]).then_inc(w_in, 16)
            sp.dma_start(x[:], io["x"]).then_inc(x_in, 16)

        @block.tensor
        def _(pe):
            pe.wait_ge(w_in, 32)
            pe.wait_ge(x_in, 16)
            with pe.Fori(0, B) as b:
                for half in range(2):
                    pe.wait_ge(acc_used, b * 2 + half + 1)
                    for c in range(CONTEXT):
                        mm = nc.tensor.matmul(acc[half][:, 0:HALF], w[:, c, :],
                                              x[:, bass.ds(b * S_IN + (half * HALF + c), HALF)],
                                              start=(c == 0), stop=(c == CONTEXT - 1))
                    mm.then_inc(conv_done, 1)

        @block.scalar
        def _(act):
            act.sem_inc(acc_used, 2)
            act.wait_ge(w_in, 32)
            with act.Fori(0, B) as b:
                for half in range(2):
                    act.wait_ge(conv_done, b * 2 + half + 1)
                    nc.scalar.activation(h_chunk(hT, b, half), acc[half][:, 0:HALF], ACT.Relu,
                                         bias=cols[:, 0:1]).then_inc(acc_used, 1)
            act.wait_ge(var_done, 1)
            nc.scalar.activation(s[:, 0:1], mv[:, 1:2], ACT.Sqrt, bias=K["eps5"][:, 0:1]).then_inc(sd_done, 1)

        @block.vector
        def _(dve):
            with dve.Fori(0, B) as b:
                for half in range(2):
                    dve.wait_ge(acc_used, b * 2 + half + 3)
                    nc.vector.bn_stats(stats[:, bass.ds(b * 12 + half * 6, 6)],
                                       h_chunk(hT, b, half)).then_inc(y_done, 1)
            dve.wait_ge(y_done, 2 * B)
            nc.vector.bn_aggr(mv[:], stats[:]).then_inc(var_done, 1)
            dve.wait_ge(var_done, 1)
            dve.wait_ge(sd_done, 1)
            c = Chain(dve, chain)
            c.link(nc.vector.reciprocal(s[:, 1:2], s[:, 0:1]))
            c.link(nc.vector.tensor_tensor(s[:, 2:3], s[:, 1:2], cols[:, 1:2], ALU.mult))
            c.link(nc.vector.tensor_tensor(s[:, 3:4], s[:, 2:3], mv[:, 0:1], ALU.mult))
            c.link(nc.vector.tensor_tensor(s[:, 3:4], cols[:, 2:3], s[:, 3:4], ALU.subtract))
            c.link(nc.vector.tensor_scalar(hT[:], hT[:], s[:, 2:3], s[:, 3:4], ALU.mult, ALU.add))


def layer_norm(nc, K, name, src="hT", affine=None, affine_d=None, add=False):
    hT, zT = K["hT"], K["zT"]
    D, R = 4, 3

    def x_chunk(c):
        b, half = CHUNKS[c]
        return z_chunk(zT, b, half) if src == "zT" else h_chunk(hT if src == "hT" else src, b, half)

    with ExitStack() as ctx:
        a = Alloc(nc, ctx, name)
        N = len(CHUNKS)
        sq = [a.sb(f"sq{i}", [P, HALF]) for i in range(N)]
        dev = [a.sb(f"dev{i}", [P, HALF]) for i in range(N)]
        xn = [a.sb(f"xn{i}", [P, HALF]) for i in range(2)]
        sd = [a.sb(f"sd{g}", [GROUP_MAX, HALF]) for g in range(2)]
        rstd = [a.sb(f"rstd{g}", [GROUP_MAX, HALF]) for g in range(2)]
        d = [a.ps(f"d{i}", [P, BANK]) for i in range(D)]
        var = a.ps("var", [GROUP_MAX, BANK])
        r_ps = [a.ps(f"r_ps{i}", [P, BANK]) for i in range(R)]
        d_ready, sq_ready, var_ready, sd_ready, rstd_ready, spread, scaled, chain, cols_in, copied = (a.sem(n) for n in (
            "d_ready", "sq_ready", "var_ready", "sd_ready", "rstd_ready", "spread", "scaled", "chain", "cols_in",
            "copied"))
        block = ctx.enter_context(nc.Block())

        @block.sync
        def _(sp):
            if affine is not None:
                sp.dma_start(affine[:], affine_d).then_inc(cols_in, 16)

        @block.tensor
        def _(pe):
            def deviations(c):
                if c >= D:
                    pe.wait_ge(copied, c - D + 1)
                nc.tensor.matmul(d[c % D][:, 0:HALF], K["center"][:], x_chunk(c), start=True, stop=True).then_inc(d_ready, 1)

            def variance(g, c):
                first, end = LN_GROUPS[g]
                pe.wait_ge(sq_ready, c + 1)
                if g > 0 and c == first:
                    pe.wait_ge(sd_ready, g)
                mm = nc.tensor.matmul(var[:, 0:HALF], K["avg_rows"][:, c - first, :], sq[c][:], start=(c == first),
                                      stop=(c == end - 1))
                if c == end - 1:
                    mm.then_inc(var_ready, 1)

            def spread_row(g, c):
                first, end = LN_GROUPS[g]
                if c == first:
                    pe.wait_ge(rstd_ready, g + 1)
                if c >= R:
                    pe.wait_ge(scaled, c - R + 1)
                n = end - first
                nc.tensor.matmul(r_ps[c % R][:, 0:HALF], K["spread_rows"][0:n, c - first, :], rstd[g][0:n, :],
                                 start=True, stop=True).then_inc(spread, 1)

            for c in range(LN_GROUPS[0][1]):
                deviations(c)
            for c in range(LN_GROUPS[0][1]):
                variance(0, c)
            for c in range(D - 1, N - 1):
                deviations(c)
            variance(1, D - 1)
            deviations(N - 1)
            for c in range(D, N):
                variance(1, c)
            for g in range(2):
                for c in range(*LN_GROUPS[g]):
                    spread_row(g, c)

        @block.scalar
        def _(act):
            def squares(c0, c1):
                for c in range(c0, c1):
                    act.wait_ge(d_ready, c + 1)
                    nc.scalar.activation(sq[c][:], d[c % D][:, 0:HALF], ACT.Square).then_inc(sq_ready, 1)

            def copies(c0, c1):
                for c in range(c0, c1):
                    nc.scalar.copy(dev[c][:], d[c % D][:, 0:HALF]).then_inc(copied, 1)

            def roots(g):
                act.wait_ge(var_ready, g + 1)
                n = LN_GROUPS[g][1] - LN_GROUPS[g][0]
                nc.scalar.activation(sd[g][0:n, :], var[0:n, 0:HALF], ACT.Sqrt, bias=K["eps5"][0:n, 0:1]).then_inc(sd_ready, 1)

            squares(0, LN_GROUPS[0][1])
            copies(0, LN_GROUPS[0][1])
            roots(0)
            squares(LN_GROUPS[0][1], D)
            copies(LN_GROUPS[0][1], D)
            squares(D, N)
            roots(1)
            copies(D, N)

        @block.vector
        def _(dve):
            if affine is not None:
                dve.wait_ge(cols_in, 16)
            link = Chain(dve, chain)
            for g, (first, end) in enumerate(LN_GROUPS):
                n = end - first
                dve.wait_ge(sd_ready, g + 1)
                nc.vector.reciprocal(rstd[g][0:n, :], sd[g][0:n, :]).then_inc(rstd_ready, 1)
            for c, (b, half) in enumerate(CHUNKS):
                dve.wait_ge(spread, c + 1)
                x = xn[c % 2][:]
                out = z_chunk(zT, b, half) if affine is None else x
                dve.wait_ge(copied, c + 1)
                nc.vector.tensor_tensor(out, dev[c][:], r_ps[c % R][:, 0:HALF], ALU.mult).then_inc(scaled, 1)
                if affine is not None:
                    dve.wait_ge(scaled, c + 1)
                    out = x if add else z_chunk(zT, b, half)
                    link.link(nc.vector.tensor_scalar(out, x, affine[:, 0:1], affine[:, 1:2], ALU.mult, ALU.add))
                    if add:
                        h = h_chunk(hT, b, half)
                        link.link(nc.vector.tensor_tensor(h, h, x, ALU.add))


STAGES = {}


def audio_tower(nc, io, out, scratch):
    with ExitStack() as ctx:
        a = Alloc(nc, ctx, "tower")
        K = {
            "ident": a.sb("ident", [P, P]),
            "mean_all": a.sb("mean_all", [P, P]),
            "center": a.sb("center", [P, P]),
            "avg_rows": a.sb("avg_rows", [P, GROUP_MAX, GROUP_MAX]),
            "spread_rows": a.sb("spread_rows", [GROUP_MAX, GROUP_MAX, P]),
            "hT": a.sb("hT", [P, B * L]),
            "zT": a.sb("zT", [P, ZW]),
            "eps5": a.sb("eps5", [P, 1]),
            "eps4": a.sb("eps4", [P, 1]),
        }
        K["iota_d"] = io["iota"]
        load_constants(nc, io, K)
        for n in range(len(STAGES)):
            if n > 0:
                layer_norm(nc, K, f"ln{n}")
            STAGES[n](nc, io, K, scratch)
        written = a.sem("written")
        block = ctx.enter_context(nc.Block())

        @block.sync
        def _(sp):
            sp.dma_start(out, K["hT"][:]).then_inc(written, 16)
            sp.wait_ge(written, 16)


STAGES[0] = lambda nc, io, K, scratch: token_conv(nc, io, K)


HEADS0 = 8
HD = P // HEADS0
QD = HD // 2
PAIRS = B * HEADS0
REL_L = 256
REL = 2 * REL_L - 2
FAR = L - 1 - REL
SKEW_TILES = REL // P + 1
SKEW_W = [REL - P * t for t in range(SKEW_TILES)]
SKEW_PAD = [-(-w // P) * P for w in SKEW_W]
SKEW_ROW = BANK + P
LEFT_PART = (0, 0, 1, 1, 0, 2)
RIGHT_PART = (0, 1, 0, 1, 2, 0)
NPART = len(LEFT_PART)


def split3(nc, c, parts, src, rest, done):
    c.link(nc.vector.tensor_copy(parts[0], src))
    c.link(nc.vector.tensor_tensor(rest, src, parts[0], ALU.subtract))
    c.link(nc.vector.tensor_copy(parts[1], rest))
    c.link(nc.vector.tensor_tensor(rest, rest, parts[1], ALU.subtract))
    nc.vector.tensor_copy(parts[2], rest).then_inc(done, 1)


HIGH_BITS = 0xFFFFF000


def split2(nc, dve, src, masked, hi, lo, high, n):
    nc.vector.tensor_scalar(masked.bitcast(U32), src.bitcast(U32), HIGH_BITS, None, ALU.bitwise_and).then_inc(high, 1)
    dve.wait_ge(high, n)
    nc.vector.tensor_copy(hi, masked)
    return nc.vector.tensor_tensor(lo, src, masked, ALU.subtract)


def three_passes(nc, out, w, x, start, stop):
    terms = ((0, 0), (0, 1), (1, 0))
    for n, (i, j) in enumerate(terms):
        mm = nc.tensor.matmul(out, w[i], x[j], start=(start and n == 0),
                              stop=(stop and n == len(terms) - 1))
    return mm


class GroupNorm:

    def __init__(self, a, name, avg, cols, g_ps, eps):
        self.avg, self.cols, self.g_ps, self.eps = avg, cols, g_ps, eps
        self.passed = a.sem(f"{name}_passed")
        self.stats = a.sb(f"{name}_stats", [P, 12])
        self.work = a.sb(f"{name}_work", [P, 8])
        self.mean_in, self.g_mean, self.spread_in, self.g_var, self.sd_done, self.affine_ready = (
            a.sem(f"{name}_{s}") for s in ("mean_in", "g_mean", "spread_in", "g_var", "sd_done", "affine_ready"))

    LINKS = 6

    def dve(self, nc, dve, c, x, n):
        w, g = self.work, self.g_ps
        c.link(nc.vector.bn_stats(self.stats[:, 0:6], x[:, 0:HALF]))
        c.link(nc.vector.bn_stats(self.stats[:, 6:12], x[:, HALF:L]))
        apart(dve, self.passed)
        nc.vector.bn_aggr(w[:, 0:2], self.stats[:]).then_inc(self.mean_in, 1)
        dve.wait_ge(self.mean_in, n + 1)
        dve.wait_ge(self.g_mean, n + 1)
        c.link(nc.vector.tensor_tensor(w[:, 2:3], w[:, 0:1], g[:, 0:1], ALU.subtract))
        nc.vector.scalar_tensor_tensor(out=w[:, 3:4], in0=w[:, 2:3], scalar=w[:, 2:3], in1=w[:, 1:2],
                                       op0=ALU.mult, op1=ALU.add).then_inc(self.spread_in, 1)
        dve.wait_ge(self.sd_done, n + 1)
        c.link(nc.vector.reciprocal(w[:, 5:6], w[:, 4:5]))
        c.link(nc.vector.tensor_tensor(w[:, 6:7], w[:, 5:6], self.cols[:, 0:1], ALU.mult))
        c.link(nc.vector.tensor_tensor(w[:, 7:8], w[:, 6:7], g[:, 0:1], ALU.mult))
        nc.vector.tensor_tensor(w[:, 7:8], self.cols[:, 1:2], w[:, 7:8], ALU.subtract).then_inc(self.affine_ready, 1)

    def pe(self, nc, pe, n):
        pe.wait_ge(self.mean_in, n + 1)
        nc.tensor.matmul(self.g_ps[:, 0:1], self.avg, self.work[:, 0:1], start=True, stop=True).then_inc(self.g_mean, 1)
        pe.wait_ge(self.spread_in, n + 1)
        nc.tensor.matmul(self.g_ps[:, 1:2], self.avg, self.work[:, 3:4], start=True, stop=True).then_inc(self.g_var, 1)

    def act(self, nc, act, n):
        act.wait_ge(self.g_var, n + 1)
        nc.scalar.activation(self.work[:, 4:5], self.g_ps[:, 1:2], ACT.Sqrt, bias=self.eps).then_inc(self.sd_done, 1)


def rel_projection(nc, io, K, scratch, v_tok, rel96, relv):
    zT = K["zT"]
    lhs_d, rhs_d = scratch["rel_lhs"], scratch["rel_rhs"]
    with ExitStack() as ctx:
        a = Alloc(nc, ctx, "relproj")
        w = a.sb("w", [P, 2, P])
        cols = a.sb("cols", [P, 2, 2])
        gavg = a.sb("gavg", [P, P])
        rel16 = a.sb("rel16", [2 * QD, BANK])
        relc = a.sb("relc", [2 * QD, BANK])
        relp = a.sb("relp", [2 * QD, 3, BANK], BF16)
        relv0 = a.sb("relv0", [P, HD])
        relv_col = a.sb("relv_col", [P, 1])
        zeros = a.sb("zeros", [P, SKEW_ROW])
        qk = a.sb("qk", [P, LP])
        rest = a.sb("rest", [P, LP])
        parts = a.sb("parts", [P, 3, LP], BF16)
        v = a.sb("v", [P, LP])
        qk_ps = a.ps("qk_ps", [P, 2 * BANK])
        v_ps = a.ps("v_ps", [P, 2 * BANK])
        turn_ps = a.ps("turn_ps", [P, 2 * BANK])
        g_ps = [a.ps(f"g_ps{i}", [P, BANK]) for i in range(2)]
        gn = [GroupNorm(a, ("qk", "v")[j], gavg[:], cols[:, j, :], g_ps[j], K["eps4"][:, 0:1]) for j in range(2)]
        x_ps = (qk_ps, v_ps)
        w_in, proj_done, norm_done, split_done, turned, turn_used, chain, filled, stacked, rel_in, rel_split, zeroed, rel_stacked, once = (
            a.sem(n) for n in ("w_in", "proj_done", "norm_done", "split_done", "turned", "turn_used", "chain",
                               "filled", "stacked", "rel_in", "rel_split", "zeroed", "rel_stacked", "once"))
        block = ctx.enter_context(nc.Block())

        @block.sync
        def _(sp):
            sp.dma_start(w[:], io["rel_w"]).then_inc(w_in, 16)
            sp.dma_start(cols[:], io["rel_gn"]).then_inc(w_in, 16)
            sp.dma_start(gavg[:], io["avg8"]).then_inc(w_in, 16)
            sp.dma_start(relv_col[:], io["relv_col"]).then_inc(w_in, 16)
            sp.dma_start(rel16[:], io["rel16"]).then_inc(rel_in, 16)
            sp.dma_start(relv[:], io["relv"]).then_inc(rel_in, 16)
            sp.dma_start(relv0[:], io["relv0"]).then_inc(rel_in, 16)
            sp.wait_ge(filled, 3)
            for name in ("rel_bias", "rel_probs"):
                for slot in range(2):
                    for t in range(SKEW_TILES):
                        sp.dma_start(scratch[name][slot, t], zeros[:]).then_inc(zeroed, 16)
            sp.wait_ge(rel_split, 1)
            for side in range(2):
                for s in range(NPART):
                    row = (side * NPART + s) * QD
                    sp.dma_start(rel96[row:row + QD, :], relp[side * QD:side * QD + QD, RIGHT_PART[s], :]
                                 ).then_inc(rel_stacked, 16)
            with sp.Fori(0, B) as b:
                sp.wait_ge(split_done, b + 2)
                for s in range(NPART):
                    for row, src in ((s, 0), (s + NPART, 1)):
                        sp.dma_start(lhs_d[bass.ds(b * HEADS0, HEADS0), row * QD:row * QD + QD, :],
                                     parts[src * 64:src * 64 + 64, LEFT_PART[s], :]).then_inc(stacked, 16)
            sp.wait_ge(stacked, B * 3 * NPART * 16 + 16)
            sp.wait_ge(zeroed, 4 * SKEW_TILES * 16)
            sp.wait_ge(rel_stacked, 2 * NPART * 16)

        @block.tensor
        def _(pe):
            pe.wait_ge(w_in, 64)
            with pe.Fori(0, B) as b:
                pe.wait_ge(norm_done, b * 2 + 2)
                for j in range(2):
                    nc.tensor.matmul(x_ps[j][:, 0:BANK], w[:, j, :], zT[:, bass.ds(b * LP + LEAD, BANK)],
                                     start=True, stop=True)
                    nc.tensor.matmul(x_ps[j][:, BANK:L], w[:, j, :], zT[:, bass.ds(b * LP + (LEAD + BANK), L - BANK)],
                                     start=True, stop=True).then_inc(proj_done, 1)
                for j in range(2):
                    gn[j].pe(nc, pe, b)
                pe.wait_ge(norm_done, b * 2 + 4)
                pe.wait_ge(turn_used, b + 1)
                for t in range(TILES):
                    mm = nc.tensor.transpose(turn_ps[:, t * P:(t + 1) * P], v[:, t * P:(t + 1) * P], K["ident"][:])
                mm.then_inc(turned, 1)

        @block.scalar
        def _(act):
            act.sem_inc(norm_done, 2)
            act.wait_ge(filled, 3)
            with act.Fori(0, B) as b:
                for j in range(2):
                    gn[j].act(nc, act, b)
                act.wait_ge(gn[0].affine_ready, b + 1)
                act.wait_ge(split_done, b + 1)
                nc.scalar.activation(qk[:, 0:L], qk_ps[:, 0:L], ACT.Identity, bias=gn[0].work[:, 7:8],
                                     scale=gn[0].work[:, 6:7]).then_inc(norm_done, 1)
                act.wait_ge(gn[1].affine_ready, b + 1)
                act.wait_ge(turn_used, b + 1)
                nc.scalar.activation(v[:, 0:L], v_ps[:, 0:L], ACT.Identity, bias=gn[1].work[:, 7:8],
                                     scale=gn[1].work[:, 6:7]).then_inc(norm_done, 1)
                act.wait_ge(split_done, b + 2)
                for s in range(NPART):
                    act.dma_start(rhs_d[bass.ds(b * HEADS0, HEADS0), s * QD:s * QD + QD, :],
                                  parts[64:128, RIGHT_PART[s], :]).then_inc(stacked, 16)

        @block.vector
        def _(dve):
            dve.sem_inc(turn_used, 1)
            dve.sem_inc(split_done, 1)
            dve.sem_inc(stacked, 16)
            nc.vector.memset(zeros[:], 0.0).then_inc(filled, 1)
            nc.vector.memset(qk[:], 0.0).then_inc(filled, 1)
            nc.vector.memset(v[:], 0.0).then_inc(filled, 1)
            dve.wait_ge(rel_in, 48)
            dve.wait_ge(w_in, 64)
            c = Chain(dve, once)
            c.link(nc.vector.tensor_scalar(relc[:], rel16[:], rel16[:, REL:REL + 1], None, ALU.subtract))
            split3(nc, c, [relp[:, i, :] for i in range(3)], relc[:], rel16[:], rel_split)
            c.link(nc.vector.tensor_tensor(cols[:, 1, 1:2], cols[:, 1, 1:2], relv_col[:], ALU.add))
            for t in range(SKEW_TILES):
                c.link(nc.vector.tensor_tensor(relv[:, t, :], relv[:, t, :], relv0[:], ALU.subtract))
            with dve.Fori(0, B) as b:
                c = Chain(dve, chain, b, 2 * GroupNorm.LINKS + 4)
                for j in range(2):
                    dve.wait_ge(proj_done, b * 2 + j + 1)
                    gn[j].dve(nc, dve, c, x_ps[j], b)
                dve.wait_ge(norm_done, b * 2 + 3)
                dve.wait_ge(stacked, b * (3 * NPART * 16) + 16)
                split3(nc, c, [parts[:, i, :] for i in range(3)], qk[:], rest[:], split_done)
                dve.wait_ge(turned, b + 1)
                nc.vector.tensor_copy(v_tok[:, :, bass.ds(b * P, P)],
                                      turn_ps[:, 0:LP].rearrange("p (t c) -> p t c", t=TILES)).then_inc(turn_used, 1)
                c.end()


class Turn:

    def __init__(self, m, k):
        self.n, self.slot, self.turn = m * 2 + k, k % 2, m + k // 2
        self.first = isinstance(m, int) and self.n == 0
        self.early = isinstance(m, int) and self.n < 2


def rel_attention(nc, io, K, scratch, v_tok, rel96, relv):
    with ExitStack() as ctx:
        a = Alloc(nc, ctx, "rel")
        lhs = [a.sb(f"lhs{i}", [2 * NPART * QD, LP], BF16) for i in range(2)]
        rhs = [a.sb(f"rhs{i}", [NPART * QD, LP], BF16) for i in range(2)]
        r_sb = [a.sb(f"r_sb{i}", [P, SKEW_TILES, BANK]) for i in range(2)]
        bias = [[a.sb(f"bias{i}_{t}", [P, SKEW_W[t]]) for t in range(SKEW_TILES)] for i in range(2)]
        probs = [a.sb(f"probs{i}", [P, TILES, LP]) for i in range(2)]
        shear = [[a.sb(f"shear{i}_{t}", [P, SKEW_PAD[t]]) for t in range(SKEW_TILES)] for i in range(2)]
        probsT = [a.sb(f"probsT{i}", [P, TILES, LP]) for i in range(2)]
        shearT = a.sb("shearT", [P, SKEW_TILES, BANK])
        v_pad = [a.sb(f"v_pad{i}", [P, TILES, 2 * HD]) for i in range(2)]
        relv_pad = [a.sb(f"relv_pad{i}", [P, SKEW_TILES, 2 * HD]) for i in range(2)]
        o_sb = a.sb("o_sb", [4 * HD, HALF])
        nmax = [a.sb(f"nmax{i}", [P, TILES]) for i in range(2)]
        sums = [a.sb(f"sums{i}", [P, TILES]) for i in range(2)]
        rsum = [a.sb(f"rsum{i}", [P, TILES]) for i in range(2)]
        s_ps = [a.ps(f"s_ps{i}", [P, 2 * BANK]) for i in range(2)]
        t_ps = [a.ps(f"t_ps{i}", [P, BANK]) for i in range(2)]
        x_ps = a.ps("x_ps", [P, BANK])
        o_ps = a.ps("o_ps", [P, BANK])
        in_sem = a.sems("pair_in", 2)
        bias_out, bias_in = a.sems("bias_out", 2), a.sems("bias_in", 2)
        probs_out, shear_in = a.sems("probs_out", 2), a.sems("shear_in", 2)
        t_copied = a.sems("t_copied", 2)
        names = ("r_full", "r_copied", "a_full", "a_copied", "s_full", "max_ready", "exp_done", "rs_ready",
                 "scaled", "t_full", "v_ready", "o_full", "o_copied", "o_stored", "filled", "passed")
        (r_full, r_copied, a_full, a_copied, s_full, max_ready, exp_done, rs_ready,
         scaled, t_full, v_ready, o_full, o_copied, o_stored, filled, passed) = (a.sem(n) for n in names)
        NS, T = SKEW_TILES, TILES
        LAG = 2

        def turning(now, old, t):
            return (old, T - LAG + t) if t < LAG else (now, t - LAG)

        blocks_of = [w // P for w in SKEW_PAD]
        block = ctx.enter_context(nc.Block())

        def turns(eng, body):
            t = [Turn(0, k) for k in range(PAIRS)]
            body(t[0], None, None)
            body(t[1], t[0], None)
            body(t[2], t[1], t[0])
            with eng.Fori(0, (PAIRS - 4) // 2) as m:
                for k in range(2):
                    body(Turn(m, k + 3), Turn(m, k + 2), Turn(m, k + 1))
            body(t[PAIRS - 1], t[PAIRS - 2], t[PAIRS - 3])
            body(None, t[PAIRS - 1], t[PAIRS - 2])
            body(None, None, t[PAIRS - 1])

        def sheared(name, slot, t, step, width):
            rows = scratch[name]
            at = (slot * SKEW_TILES + t) * P * SKEW_ROW
            return bass.AP(rows.tensor, rows.offset + at, [[step, P], [1, width]])

        def copy_turned(eng, copy, pair, t, i):
            if t == 0 and not pair.early:
                eng.wait_ge(o_full, pair.n - 1)
            eng.wait_ge(t_full, pair.n * 2 * T + (2 * t + i + 1))
            j0 = i * (T // 2)
            copy(probsT[pair.slot][:, j0:j0 + T // 2, t * P:(t + 1) * P],
                 t_ps[i][:, 0:T // 2 * P].rearrange("p (j i) -> p j i", i=P)).then_inc(t_copied[i], 1)

        @block.sync
        def _(sp):
            def store_probs(now, t):
                sp.wait_ge(scaled, now.n * T + t + 1)
                sp.dma_start(scratch["rel_probs"][now.slot, t, :, 0:SKEW_W[t]],
                             probs[now.slot][:, t, L - SKEW_W[t]:L]).then_inc(probs_out[now.slot], 16)

            def body(new, now, old):
                if old is not None and new is not None:
                    sp.wait_ge(bias_in[new.slot], new.turn * (16 * NS))
                if old is not None and now is not None and not now.early:
                    sp.wait_ge(shear_in[now.slot], now.turn * (16 * NS))
                for t in range(NS):
                    if new is not None:
                        sp.wait_ge(r_copied, new.n * NS + t + 1)
                        sp.dma_start(scratch["rel_bias"][new.slot, t, :, 0:SKEW_W[t]], r_sb[new.slot][:, t, 0:SKEW_W[t]]
                                     ).then_inc(bias_out[new.slot], 16)
                    if now is not None and t > 0:
                        store_probs(now, t - 1)
                if new is not None:
                    sp.wait_ge(bias_out[new.slot], new.turn * (16 * NS) + 16 * NS)
                    apart(sp, passed)
                    if old is not None:
                        sp.wait_ge(s_full, old.n * T + NS)
                    for t in range(NS):
                        sp.dma_start(bias[new.slot][t][:], sheared("rel_bias", new.slot, t, SKEW_ROW - 1, SKEW_W[t])
                                     ).then_inc(bias_in[new.slot], 16)
                if now is not None:
                    store_probs(now, NS - 1)
                if now is not None:
                    sp.wait_ge(probs_out[now.slot], now.turn * (16 * NS) + 16 * NS)
                    apart(sp, passed)
                    if not now.early:
                        sp.wait_ge(a_full, now.n * NS - NS)
                    for t in range(NS):
                        sp.dma_start(shear[now.slot][t][:], sheared("rel_probs", now.slot, t, SKEW_ROW + 1, SKEW_PAD[t])
                                     ).then_inc(shear_in[now.slot], 16)
                if old is not None and old.slot == 1:
                    sp.wait_ge(o_copied, old.turn + 1)
                    for half in range(2):
                        sp.dma_start(scratch["rel_out"][bass.ds(old.turn, 1), :, half, :].squeeze(0),
                                     o_sb[half * 2 * HD:(half + 1) * 2 * HD, :]).then_inc(o_stored, 16)

            turns(sp, body)
            sp.wait_ge(o_stored, PAIRS * 16)

        @block.gpsimd
        def _(pool):
            for i in range(2):
                nc.gpsimd.memset(v_pad[i][:], 0.0).then_inc(filled, 1)
                nc.gpsimd.memset(relv_pad[i][:], 0.0).then_inc(filled, 1)
            pool.wait_ge(filled, 6)
            for i in range(2):
                nc.gpsimd.tensor_copy(relv_pad[i][:, :, i * HD:(i + 1) * HD], relv[:]).then_inc(filled, 1)

            def body(new, now, old):
                if now is None:
                    return
                if not now.early:
                    pool.wait_ge(o_full, now.n - 1)
                    apart(pool, passed)
                nc.gpsimd.tensor_copy(v_pad[now.slot][:, :, now.slot * HD:(now.slot + 1) * HD],
                                      v_tok[:, :, bass.ds(now.n * HD, HD)]).then_inc(v_ready, 1)

            turns(pool, body)

        @block.tensor
        def _(pe):
            def position(new, now, old, t):
                if now is not None or t > 0:
                    pe.wait_ge(r_copied, new.n * NS + t)
                sheared_before = max(t - LAG, 0)
                if old is not None and (sheared_before > 0 or not old.first):
                    pe.wait_ge(a_copied, old.n * NS + sheared_before)
                if t == 0:
                    pe.wait_ge(in_sem[new.slot], new.turn * 32 + 32)
                nc.tensor.matmul(x_ps[:, 0:SKEW_W[t]], lhs[new.slot][:, t * P:(t + 1) * P], rel96[:, 0:SKEW_W[t]],
                                 start=True, stop=True).then_inc(r_full, 1)

            def scores(now, t):
                i = t % 2
                if t >= 2 or not now.first:
                    pe.wait_ge(exp_done, now.n * T + t - 1)
                if t == 0:
                    pe.wait_ge(bias_in[now.slot], now.turn * (16 * NS) + 16 * NS)
                for c0, c1 in ((0, BANK), (BANK, L)):
                    first = max(c0, L - SKEW_W[t]) if t < NS else L
                    mm = nc.tensor.matmul(s_ps[i][:, c0:c1], lhs[now.slot][0:NPART * QD, t * P:(t + 1) * P],
                                          rhs[now.slot][:, c0:c1], start=True, stop=first >= c1)
                    if first < c1:
                        b0 = first - (L - SKEW_W[t])
                        mm = nc.tensor.matmul(s_ps[i][:, first:c1], K["ident"][:], bias[now.slot][t][:, b0:b0 + c1 - first],
                                              start=False, stop=True)
                mm.then_inc(s_full, 1)

            def turn_probs(pair, t):
                pe.wait_ge(scaled, pair.n * T + t + 1)
                for i in range(2):
                    if t > 0 or not pair.first:
                        pe.wait_ge(t_copied[i], pair.n * T + t)
                    for j in range(T // 2):
                        k = i * (T // 2) + j
                        mm = nc.tensor.transpose(t_ps[i][:, j * P:(j + 1) * P], probs[pair.slot][:, t, k * P:(k + 1) * P],
                                                 K["ident"][:])
                    mm.then_inc(t_full, 1)

            def turn_shear(new, old, t):
                if t == 0:
                    pe.wait_ge(shear_in[old.slot], old.turn * (16 * NS) + 16 * NS)
                if new is not None:
                    pe.wait_ge(r_copied, new.n * NS + min(t + LAG + 1, NS))
                if t > 0 or not old.first:
                    pe.wait_ge(a_copied, old.n * NS + t)
                for j in range(blocks_of[t]):
                    mm = nc.tensor.transpose(x_ps[:, j * P:(j + 1) * P], shear[old.slot][t][:, j * P:(j + 1) * P],
                                             K["ident"][:])
                mm.then_inc(a_full, 1)

            def values(old, tiles):
                if tiles[0] == 0:
                    for i in range(2):
                        pe.wait_ge(t_copied[i], old.n * T + T)
                    pe.wait_ge(v_ready, old.n + 1)
                    if old.slot == 0 and not old.first:
                        pe.wait_ge(o_copied, old.turn)
                for j in tiles:
                    for half in range(2):
                        nc.tensor.matmul(o_ps[half * 2 * HD:(half + 1) * 2 * HD, 0:HALF], v_pad[old.slot][:, j, :],
                                         probsT[old.slot][:, j, half * HALF:(half + 1) * HALF],
                                         start=(j == 0 and old.slot == 0), stop=False, skip_group_check=True)

            def positions(old):
                pe.wait_ge(a_copied, old.n * NS + NS)
                for j in range(NS):
                    for half in range(2):
                        lo, hi = half * HALF, min((half + 1) * HALF, (NS - j) * P)
                        if lo < hi:
                            mm = nc.tensor.matmul(o_ps[half * 2 * HD:(half + 1) * 2 * HD, 0:hi - lo], relv_pad[old.slot][:, j, :],
                                                  shearT[:, j, lo:hi], start=False, stop=(old.slot == 1), skip_group_check=True)
                mm.then_inc(o_full, 1)

            value_steps = {2: [0, 1], 3: [2, 3], 4: [4], 5: [5]}

            def body(new, now, old):
                for t in range(T):
                    if now is not None and (t > 0 or now.first):
                        scores(now, t)
                    if new is not None and LAG <= t < NS:
                        position(new, now, old, t)
                    if old is not None and LAG <= t < NS + LAG:
                        turn_shear(new, old, t - LAG)
                    pair, tile = turning(now, old, t)
                    if pair is not None:
                        turn_probs(pair, tile)
                    if old is not None and t in value_steps:
                        values(old, value_steps[t])
                    if new is not None and t < LAG:
                        position(new, now, old, t)
                if new is not None and now is not None:
                    scores(new, 0)
                if old is not None:
                    positions(old)

            pe.wait_ge(filled, 8)
            turns(pe, body)

        @block.scalar
        def _(act):
            def load(pair):
                act.dma_start(lhs[pair.slot][:], scratch["rel_lhs"][bass.ds(pair.n, 1), :, :].squeeze(0)).then_inc(in_sem[pair.slot], 16)
                act.dma_start(rhs[pair.slot][:], scratch["rel_rhs"][bass.ds(pair.n, 1), :, :].squeeze(0)).then_inc(in_sem[pair.slot], 16)

            def copy_position(new, old, t):
                if t == 0 and old is not None:
                    act.wait_ge(bias_out[new.slot], new.turn * (16 * NS))
                act.wait_ge(r_full, new.n * NS + t + 1)
                nc.scalar.copy(r_sb[new.slot][:, t, 0:SKEW_W[t]], x_ps[:, 0:SKEW_W[t]]).then_inc(r_copied, 1)

            def body(new, now, old):
                if new is not None:
                    if old is not None:
                        act.wait_ge(s_full, old.n * T + T)
                    load(new)
                for t in range(T):
                    if new is not None and LAG <= t < NS:
                        copy_position(new, old, t)
                    if now is not None:
                        act.wait_ge(max_ready, now.n * T + t + 1)
                        if t == 0 and not now.early:
                            act.wait_ge(t_full, now.n * 2 * T - 2 * T)
                            act.wait_ge(probs_out[now.slot], now.turn * (16 * NS))
                            act.wait_ge(rs_ready, now.n * T - T)
                        nc.scalar.activation(probs[now.slot][:, t, 0:L], s_ps[t % 2][:, 0:L], ACT.Exp,
                                             bias=nmax[now.slot][:, t:t + 1],
                                             accum_out=sums[now.slot][:, t:t + 1]).then_inc(exp_done, 1)
                    if old is not None and LAG <= t < NS + LAG:
                        k = t - LAG
                        if k == 0 and not old.first:
                            act.wait_ge(o_full, old.n)
                        act.wait_ge(a_full, old.n * NS + k + 1)
                        n = blocks_of[k]
                        nc.scalar.copy(shearT[:, 0:n, k * P:(k + 1) * P],
                                       x_ps[:, 0:n * P].rearrange("p (j i) -> p j i", j=n)).then_inc(a_copied, 1)
                    pair, tile = turning(now, old, t)
                    if pair is not None:
                        copy_turned(act, nc.scalar.copy, pair, tile, 1)
                    if new is not None and t < LAG:
                        copy_position(new, old, t)

            turns(act, body)

        @block.vector
        def _(dve):
            def scale(now, t):
                n = now.n * T + t + 1
                dve.wait_ge(exp_done, n)
                nc.vector.reciprocal(rsum[now.slot][:, t:t + 1], sums[now.slot][:, t:t + 1]).then_inc(rs_ready, 1)
                dve.wait_ge(rs_ready, n)
                nc.vector.tensor_scalar(probs[now.slot][:, t, 0:L], probs[now.slot][:, t, 0:L],
                                        rsum[now.slot][:, t:t + 1], None, ALU.mult).then_inc(scaled, 1)

            def body(new, now, old):
                for t in range(T):
                    if now is not None:
                        dve.wait_ge(s_full, now.n * T + t + 1)
                        if t == 0 and not now.early:
                            dve.wait_ge(exp_done, now.n * T - T)
                        nc.vector.tensor_reduce(nmax[now.slot][:, t:t + 1], s_ps[t % 2][:, 0:L], AX.X, ALU.max,
                                                negate=True).then_inc(max_ready, 1)
                    pair, tile = (old, T - 1) if t == 0 else (now, t - 1)
                    if pair is not None:
                        scale(pair, tile)
                    pair, tile = turning(now, old, t)
                    if pair is not None:
                        copy_turned(dve, nc.vector.tensor_copy, pair, tile, 0)
                if old is not None and old.slot == 1:
                    dve.wait_ge(o_full, old.n + 1)
                    if not old.early:
                        dve.wait_ge(o_stored, old.turn * 32)
                    nc.vector.tensor_copy(o_sb[:], o_ps[0:4 * HD, 0:HALF]).then_inc(o_copied, 1)

            for i in range(2):
                nc.vector.memset(probs[i][:, :, L:LP], 0.0).then_inc(filled, 1)
            turns(dve, body)


def rel_output(nc, io, K, scratch):
    hT = K["hT"]
    with ExitStack() as ctx:
        a = Alloc(nc, ctx, "relout")
        gavg = a.sb("gavg", [P, P])
        cols = a.sb("cols", [P, 2])
        o = a.sb("o", [P, B, L])
        y = [a.sb(f"y{i}", [P, L]) for i in range(2)]
        g_ps = a.ps("g_ps", [P, BANK])
        gn = GroupNorm(a, "out", gavg[:], cols[:], g_ps, K["eps4"][:, 0:1])
        w_in, scaled, added, chain = (a.sem(n) for n in ("w_in", "scaled", "added", "chain"))
        block = ctx.enter_context(nc.Block())

        @block.sync
        def _(sp):
            sp.dma_start(gavg[:], io["avg4"]).then_inc(w_in, 16)
            sp.dma_start(cols[:], io["relout_gn"]).then_inc(w_in, 16)
            sp.dma_start(o[:], scratch["rel_out"].rearrange("(b q) r h c -> (q r) b (h c)", b=B)).then_inc(w_in, 16)

        @block.tensor
        def _(pe):
            pe.wait_ge(w_in, 48)
            for b in range(B):
                gn.pe(nc, pe, b)

        @block.scalar
        def _(act):
            for b in range(B):
                gn.act(nc, act, b)
                act.wait_ge(gn.affine_ready, b + 1)
                if b >= 2:
                    act.wait_ge(added, b - 1)
                nc.scalar.activation(y[b % 2][:], o[:, b, :], ACT.Identity, bias=gn.work[:, 7:8],
                                     scale=gn.work[:, 6:7]).then_inc(scaled, 1)

        @block.vector
        def _(dve):
            dve.wait_ge(w_in, 48)
            c = Chain(dve, chain)
            for b in range(B):
                gn.dve(nc, dve, c, o[:, b, :], b)
                dve.wait_ge(scaled, b + 1)
                h = hT[:, b * L:(b + 1) * L]
                nc.vector.tensor_tensor(h, h, y[b % 2][:], ALU.add).then_inc(added, 1)
                dve.wait_ge(added, b + 1)


def stage1(nc, io, K, scratch):
    with ExitStack() as ctx:
        a = Alloc(nc, ctx, "stage1")
        v_tok = a.sb("v_tok", [P, TILES, PAIRS * HD])
        rel96 = a.sb("rel96", [2 * NPART * QD, BANK], BF16)
        relv = a.sb("relv", [P, SKEW_TILES, HD])
        scratch["rel_lhs"] = nc.dram_tensor("rel_lhs", (PAIRS, 2 * NPART * QD, LP), BF16, kind="Internal").ap()
        scratch["rel_rhs"] = nc.dram_tensor("rel_rhs", (PAIRS, NPART * QD, LP), BF16, kind="Internal").ap()
        scratch["rel_bias"] = nc.dram_tensor("rel_bias", (2, SKEW_TILES, P, SKEW_ROW), F32, kind="Internal").ap()
        scratch["rel_probs"] = nc.dram_tensor("rel_probs", (2, SKEW_TILES, P, SKEW_ROW), F32, kind="Internal").ap()
        scratch["rel_out"] = nc.dram_tensor("rel_out", (PAIRS // 2, 2 * HD, 2, HALF), F32, kind="Internal").ap()
        rel_projection(nc, io, K, scratch, v_tok, rel96, relv)
        rel_attention(nc, io, K, scratch, v_tok, rel96, relv)
        rel_output(nc, io, K, scratch)


STAGES[1] = stage1


def group_average(size):
    return np.kron(np.eye(P // size, dtype=np.float32), np.full((size, size), 1.0 / size, np.float32))


def stage1_layout(f):
    chan = np.arange(2 * P).reshape(HEADS0, 4, QD)
    qk = np.concatenate([chan[:, 0].ravel(), chan[:, 1].ravel()])
    v = chan[:, 2:].ravel()
    gn = np.stack([f["L0_attn_gn_qkv_scale"], f["L0_attn_gn_qkv_bias"]], 1)
    rel = f["L0_attn_rel_emb"]
    col = np.minimum(np.arange(BANK), REL)
    rev = np.where(col < REL, REL - 1 - col, REL)
    relq, relk, relv = rel[:QD], rel[QD:2 * QD], rel[2 * QD:]
    return {
        "rel_w": np.stack([f["L0_attn_W_qkv"][:, qk], f["L0_attn_W_qkv"][:, v]], 1),
        "rel_gn": np.stack([gn[qk], gn[v]], 1),
        "avg8": group_average(8),
        "avg4": group_average(4),
        "relout_gn": np.stack([f["L0_attn_gn_out_scale"], f["L0_attn_gn_out_bias"]], 1),
        "rel16": np.concatenate([relk, relq])[:, rev],
        "relv": relv[:, rev].T.reshape(SKEW_TILES, P, HD).transpose(1, 0, 2),
        "relv0": np.broadcast_to(relv[:, REL], (P, HD)),
        "relv_col": np.tile(relv[:, REL], HEADS0)[:, None],
    }


TOK_TILES = B * TILES
NCH = len(CHUNKS)
HID = 512
HJ = HID // P


def top2_gates(nc, K, a, block, lg, lg_ready, E, gates, pack, pack_ps, packT, gates_d):
    W = E if pack == "sum" else 4 * E
    best = a.sb("best", [P, TOK_TILES, 8])
    at = a.sb("at", [P, TOK_TILES, 8], U32)
    atf = a.sb("atf", [P, TOK_TILES, 2])
    iota = a.sb("iota", [P, TOK_TILES, E])
    g = a.sb("g", [P, 2, TOK_TILES])
    e = a.sb("e", [P, 2, TOK_TILES])
    one = a.sb("one", [P, TOK_TILES, E])
    iota_in, found, diff_ready, exp_ready, packed, turned, copied, chain = (a.sem(f"top2_{n}") for n in (
        "iota_in", "found", "diff_ready", "exp_ready", "packed", "turned", "copied", "chain"))
    gates_out = a.sem("top2_gates_out")
    best_ready = a.sem("top2_best_ready")

    @block.sync
    def _(sp):
        sp.dma_start(iota[:], K["iota_d"][:, :, 0:E]).then_inc(iota_in, 16)
        for b in range(B):
            sp.wait_ge(copied, b + 1)
            sp.dma_start(gates_d[:, b * LP:(b + 1) * LP], packT[:, b * LP:(b + 1) * LP]).then_inc(gates_out, 16)
        sp.wait_ge(gates_out, B * 16)

    @block.scalar
    def _(act):
        act.wait_ge(diff_ready, 1)
        nc.scalar.activation(e[:, 0, :], g[:, 0, :], ACT.Exp).then_inc(exp_ready, 1)

    @block.vector
    def _(dve):
        c = Chain(dve, chain)
        dve.wait_ge(lg_ready[0], lg_ready[1])
        for t in range(TOK_TILES):
            nc.vector.max(best[:, t, :], lg[:, t, :]).then_inc(best_ready, 1)
        dve.wait_ge(best_ready, TOK_TILES)
        for t in range(TOK_TILES):
            nc.vector.max_index(at[:, t, :], best[:, t, :], lg[:, t, :]).then_inc(found, 1)
        dve.wait_ge(found, TOK_TILES)
        nc.vector.tensor_tensor(g[:, 0, :].unsqueeze(2), best[:, :, 1:2], best[:, :, 0:1], ALU.subtract).then_inc(diff_ready, 1)
        c.link(nc.vector.tensor_copy(atf[:], at[:, :, 0:2]))
        dve.wait_ge(exp_ready, 1)
        c.link(nc.vector.tensor_scalar(e[:, 1, :], e[:, 0, :], 1.0, None, ALU.add))
        c.link(nc.vector.reciprocal(g[:, 0, :], e[:, 1, :]))
        c.link(nc.vector.tensor_tensor(g[:, 1, :], g[:, 0, :], e[:, 0, :], ALU.mult))
        dve.wait_ge(iota_in, 16)
        full = [P, TOK_TILES, E]
        for k in range(2):
            mask = one[:] if pack == "sum" else gates[:, :, k * E:(k + 1) * E]
            out = gates[:, :, 0:E] if pack == "sum" and k == 0 else one[:] if pack == "sum" else gates[:, :, (2 + k) * E:(3 + k) * E]
            c.link(nc.vector.tensor_tensor(mask, iota[:], atf[:, :, k:k + 1].to_broadcast(full), ALU.is_equal))
            c.link(nc.vector.tensor_tensor(out, mask, g[:, k, :].unsqueeze(2).to_broadcast(full), ALU.mult))
        if pack == "sum":
            c.link(nc.vector.tensor_tensor(gates[:], gates[:], one[:], ALU.add))
        dve.sem_inc(packed, 1)
        for b in range(B):
            dve.wait_ge(turned, b + 1)
            nc.vector.tensor_copy(packT[:, b * LP:(b + 1) * LP], pack_ps[0:W, 0:LP]).then_inc(copied, 1)

    @block.tensor
    def _(pe):
        pe.wait_ge(packed, 1)
        for b in range(B):
            if b >= 1:
                pe.wait_ge(copied, b)
            for t in range(TILES):
                mm = nc.tensor.transpose(pack_ps[0:W, t * P:(t + 1) * P], gates[:, b * TILES + t, :], K["ident"][:])
            mm.then_inc(turned, 1)


def experts(nc, K, scratch, name, E, kind, weights, b2, gates_d, y, z_parts):
    zT = K["zT"]
    with ExitStack() as ctx:
        a = Alloc(nc, ctx, name)
        w = [a.sb(f"w{i}", [P, 2 * HID + HJ]) for i in range(2)]
        gate = [a.sb(f"gate{i}", [P, B * LP]) for i in range(2)]
        masked = a.sb("masked", [P, ZW])
        wh = [a.sb(f"wh{i}", [P, HID], F32R) for i in range(2)]
        wl = [a.sb(f"wl{i}", [P, HID], F32R) for i in range(2)]
        b2_sb = a.sb("b2", [E, P])
        gT = a.sb("gT", [E, B * LP])
        ex = [a.sb(f"ex{j}", [P, HALF]) for j in range(HJ)]
        hid = [a.sb(f"hid{i}", [P, HJ, HALF]) for i in range(2)]
        part = a.sb("part", [P, HALF])
        h_ps = [a.ps(f"h_ps{j}", [P, BANK]) for j in range(HJ)]
        o_ps = [a.ps(f"o_ps{i}", [P, BANK]) for i in range(2)]
        w_in = a.sems("w_in", 2)
        rows_in, b_full, y_set, h_full, ex_done, low_done, h_done, o_full, y_done, part_done, high, w_split = (
            a.sem(n) for n in ("rows_in", "b_full", "y_set", "h_full", "ex_done", "low_done", "h_done", "o_full", "y_done",
                               "part_done", "high", "w_split"))
        block = ctx.enter_context(nc.Block())
        PAIR = 2 * NCH

        def zc(c):
            b, half = CHUNKS[c]
            start = LEAD + b * LP + half * HALF
            return [z[:, start:start + HALF + 1] for z in z_parts]

        def yc(c):
            return y[:, c * HALF:(c + 1) * HALF]

        def gc(s, c):
            b, half = CHUNKS[c]
            return gate[s][:, b * LP + half * HALF:b * LP + half * HALF + HALF]

        @block.sync
        def _(sp):
            sp.dma_start(b2_sb[:], b2).then_inc(rows_in, 16)
            sp.dma_start(gT[:], gates_d).then_inc(rows_in, 16)
            with sp.Fori(0, E // 2) as m:
                for s in range(2):
                    sp.wait_ge(y_done, m * PAIR + (s * NCH + NCH))
                    sp.dma_start(w[s][:], weights[bass.ds(m * 2 + s, 1), :, :].squeeze(0)).then_inc(w_in[s], 16)
                    sp.dma_start(gate[s][:], gates_d[bass.ds(m * 2 + s, 1), :].to_broadcast([P, B * LP])).then_inc(w_in[s], 16)
            sp.wait_ge(y_done, (E // 2) * PAIR + NCH)
            for part in (slice(0, HID // 2), slice(HID // 2, HID)):
                sp.dma_start(w[0][:, part], weights[0][:, part]).then_inc(w_in[0], 16)

        @block.tensor
        def _(pe):
            pe.wait_ge(rows_in, 32)
            for c in range(NCH):
                if c >= 2:
                    pe.wait_ge(y_set, c - 1)
                b, half = CHUNKS[c]
                nc.tensor.matmul(o_ps[c % 2][:, 0:HALF], b2_sb[:], gT[:, b * LP + half * HALF:b * LP + half * HALF + HALF],
                                 start=True, stop=True).then_inc(b_full, 1)
            pe.wait_ge(y_set, NCH)

            def first(m, i):
                s, c = i // NCH, i % NCH
                if c == 0:
                    pe.wait_ge(w_split, m * 2 + (s + 2))
                for j in range(HJ):
                    pe.wait_ge(h_done, m * (PAIR * HJ) + (i * HJ + j + 1))
                    js = slice(j * P, (j + 1) * P)
                    three_passes(nc, h_ps[j][:, 0:HALF + 1], (wh[s][:, js], wl[s][:, js]), zc(c),
                                 start=True, stop=True).then_inc(h_full, 1)

            def second(m, i):
                s = i // NCH
                pe.wait_ge(h_done, m * (PAIR * HJ) + (i * HJ + 2 * HJ))
                pe.wait_ge(y_done, m * PAIR + (i + PAIR - 1))
                for j in range(HJ):
                    mm = nc.tensor.matmul(o_ps[i % 2][:, 0:HALF], w[s][:, HID + j * P:HID + (j + 1) * P],
                                          hid[i % 2][:, j, :], start=(j == 0), stop=(j == HJ - 1))
                mm.then_inc(o_full, 1)

            with pe.Fori(0, E // 2) as m:
                for i in range(PAIR):
                    first(m, i)
                    if i >= 1:
                        second(m, i - 1)
                second(m, PAIR - 1)

        @block.scalar
        def _(act):
            for c in range(NCH):
                act.wait_ge(b_full, c + 1)
                nc.scalar.copy(yc(c), o_ps[c % 2][:, 0:HALF]).then_inc(y_set, 1)
            with act.Fori(0, E // 2) as m:
                for i in range(PAIR):
                    s = i // NCH
                    if kind != "elu":
                        act.wait_ge(o_full, m * PAIR + (i + 1))
                    for j in range(HJ):
                        act.wait_ge(h_full, m * (PAIR * HJ) + (i * HJ + j + 1))
                        b1 = w[s][:, 2 * HID + j:2 * HID + j + 1]
                        if kind == "elu":
                            nc.scalar.activation(ex[j][:], h_ps[j][:, 0:HALF], ACT.Exp, bias=b1).then_inc(ex_done, 1)
                        else:
                            nc.scalar.activation(hid[i % 2][:, j, :], h_ps[j][:, 0:HALF], kind, bias=b1).then_inc(h_done, 1)

        @block.vector
        def _(dve):
            dve.sem_inc(h_done, HJ)
            dve.sem_inc(o_full, 2)
            dve.sem_inc(y_done, PAIR)

            def split_weights(s, loads, n):
                dve.wait_ge(w_in[s], loads)
                dve.wait_ge(w_split, n)
                split2(nc, dve, w[s][:, 0:HID], masked[:, 0:HID], wh[s][:], wl[s][:], high, n + 1).then_inc(w_split, 1)

            split2(nc, dve, zT[:], masked[:], z_parts[0], z_parts[1], high, 1).then_inc(w_split, 1)
            split_weights(0, 32, 1)
            dve.wait_ge(y_set, NCH)

            def gather(m, i):
                s, c = i // NCH, i % NCH
                if c == 0:
                    dve.wait_ge(w_in[s], m * 32 + 32)
                dve.wait_ge(y_done, m * PAIR + (i + PAIR))
                dve.wait_ge(o_full, m * PAIR + (i + 3))
                nc.vector.tensor_tensor(part[:], o_ps[i % 2][:, 0:HALF], gc(s, c), ALU.mult).then_inc(part_done, 1)
                dve.wait_ge(part_done, m * PAIR + (i + 1))
                nc.vector.tensor_tensor(yc(c), yc(c), part[:], ALU.add).then_inc(y_done, 1)

            with dve.Fori(0, E // 2) as m:
                for i in range(PAIR):
                    s = i // NCH
                    if kind == "elu":
                        dve.wait_ge(o_full, m * PAIR + (i + 1))
                        for j in range(HJ):
                            n = m * (PAIR * HJ) + (i * HJ + j + 1)
                            dve.wait_ge(ex_done, n)
                            nc.vector.tensor_scalar(ex[j][:], ex[j][:], 1.0, -1.0, ALU.min, ALU.add).then_inc(low_done, 1)
                            dve.wait_ge(low_done, n)
                            nc.vector.scalar_tensor_tensor(out=hid[i % 2][:, j, :], in0=h_ps[j][:, 0:HALF],
                                                           scalar=w[s][:, 2 * HID + j:2 * HID + j + 1], in1=ex[j][:],
                                                           op0=ALU.add, op1=ALU.max).then_inc(h_done, 1)
                    if i >= 1:
                        gather(m, i - 1)
                    if i % NCH == NCH - 2:
                        ahead = i // NCH + 1
                        split_weights(ahead % 2, m * 32 + (ahead // 2 * 32 + 32), m * 2 + (ahead + 1))
                gather(m, PAIR - 1)


E0 = 10
TAPS_R, TAPS_S = 3, 9


def conv_router(nc, io, K, gates_d):
    zT = K["zT"]
    with ExitStack() as ctx:
        a = Alloc(nc, ctx, "router")
        w1 = a.sb("w1", [P, TAPS_R, P])
        w2 = a.sb("w2", [P, TAPS_R, E0])
        b1 = a.sb("b1", [P, 1])
        b2 = a.sb("b2", [P, E0])
        rc = a.sb("rc", [P, 1 + LP + 1])
        lg = a.sb("lg", [P, TOK_TILES, E0])
        gates = a.sb("gates", [P, TOK_TILES, E0])
        packT = a.sb("packT", [E0, B * LP])
        c_ps = [a.ps(f"c_ps{i}", [P, BANK]) for i in range(2)]
        l_ps = a.ps("l_ps", [P, TILES, E0])
        pack_ps = a.ps("pack_ps", [P, 2 * BANK])
        w_in, filled, conv_done, rc_done, l_done, lg_ready = (a.sem(n) for n in (
            "w_in", "filled", "conv_done", "rc_done", "l_done", "lg_ready"))
        block = ctx.enter_context(nc.Block())

        @block.sync
        def _(sp):
            for dst, src in ((w1, "rc_w1"), (w2, "rc_w2"), (b1, "rc_b1"), (b2, "rc_b2")):
                sp.dma_start(dst[:], io[src]).then_inc(w_in, 16)

        @block.tensor
        def _(pe):
            pe.wait_ge(w_in, 64)
            with pe.Fori(0, B) as b:
                for half in range(2):
                    pe.wait_ge(rc_done, b * 2 + half + 1)
                    for k in range(TAPS_R):
                        mm = nc.tensor.matmul(c_ps[half][:, 0:HALF], w1[:, k, :], z_chunk(zT, b, half, k - TAPS_R // 2),
                                              start=(k == 0), stop=(k == TAPS_R - 1))
                    mm.then_inc(conv_done, 1)
                pe.wait_ge(rc_done, b * 2 + 4)
                pe.wait_ge(lg_ready, b + 1)
                for t in range(TILES):
                    for k in range(TAPS_R):
                        mm = nc.tensor.matmul(l_ps[:, t, :], rc[:, t * P + k:t * P + k + P], w2[:, k, :],
                                              start=(k == 0), stop=(k == TAPS_R - 1))
                mm.then_inc(l_done, 1)

        @block.scalar
        def _(act):
            act.sem_inc(rc_done, 2)
            act.wait_ge(w_in, 64)
            act.wait_ge(filled, 1)
            with act.Fori(0, B) as b:
                act.wait_ge(lg_ready, b + 1)
                for half in range(2):
                    act.wait_ge(conv_done, b * 2 + half + 1)
                    nc.scalar.activation(rc[:, 1 + half * HALF:1 + half * HALF + HALF], c_ps[half][:, 0:HALF],
                                         ACT.Gelu, bias=b1[:, 0:1]).then_inc(rc_done, 1)

        @block.vector
        def _(dve):
            dve.sem_inc(lg_ready, 1)
            nc.vector.memset(rc[:], 0.0).then_inc(filled, 1)
            dve.wait_ge(w_in, 64)
            with dve.Fori(0, B) as b:
                dve.wait_ge(l_done, b + 1)
                nc.vector.tensor_tensor(lg[:, bass.ds(b * TILES, TILES), :], l_ps[:],
                                        b2[:, :].unsqueeze(1).to_broadcast([P, TILES, E0]), ALU.add).then_inc(lg_ready, 1)

        top2_gates(nc, K, a, block, lg, (lg_ready, B + 1), E0, gates, "sum", pack_ps, packT, gates_d)


def shared_conv(nc, io, K, y, z_parts):
    zT = K["zT"]
    with ExitStack() as ctx:
        a = Alloc(nc, ctx, "shared")
        w1 = a.sb("w1", [P, TAPS_S, HID])
        masked = a.sb("masked", [P, HID])
        w1h = a.sb("w1h", [P, TAPS_S, HID], F32R)
        w1l = a.sb("w1l", [P, TAPS_S, HID], F32R)
        w2 = a.sb("w2", [P, HJ, P])
        b1 = a.sb("b1", [P, HJ])
        b2 = a.sb("b2", [P, 1])
        hid = [a.sb(f"hid{i}", [P, HJ, HALF]) for i in range(2)]
        part = a.sb("part", [P, HALF])
        h_ps = [a.ps(f"h_ps{j}", [P, BANK]) for j in range(HJ)]
        o_ps = [a.ps(f"o_ps{i}", [P, BANK]) for i in range(2)]
        w_in, h_full, h_done, o_full, y_done, part_done, high, w_split = (a.sem(n) for n in (
            "w_in", "h_full", "h_done", "o_full", "y_done", "part_done", "high", "w_split"))
        w1_in = a.sems("w1_in", TAPS_S)
        block = ctx.enter_context(nc.Block())

        @block.sync
        def _(sp):
            for k in range(TAPS_S):
                sp.dma_start(w1[:, k, :], io["sh_w1"][:, k, :]).then_inc(w1_in[k], 16)
            for dst, src in ((w2, "sh_w2"), (b1, "sh_b1"), (b2, "sh_b2")):
                sp.dma_start(dst[:], io[src]).then_inc(w_in, 16)

        @block.tensor
        def _(pe):
            pe.wait_ge(w_in, 48)

            def first(b, i):
                for j in range(HJ):
                    pe.wait_ge(h_done, b * (2 * HJ) + (i * HJ + j + 1))
                    for k in range(TAPS_S):
                        if i == 0 and j == 0:
                            pe.wait_ge(w_split, k + 1)
                        js = slice(j * P, (j + 1) * P)
                        start = i * HALF + LEAD + k - TAPS_S // 2
                        z = [part[:, bass.ds(b * LP + start, HALF + 1)] for part in z_parts]
                        mm = three_passes(nc, h_ps[j][:, 0:HALF + 1], (w1h[:, k, js], w1l[:, k, js]), z,
                                          start=(k == 0), stop=(k == TAPS_S - 1))
                    mm.then_inc(h_full, 1)

            def second(b, i):
                pe.wait_ge(h_done, b * (2 * HJ) + (i * HJ + 2 * HJ))
                pe.wait_ge(y_done, b * 2 + (i + 1))
                for j in range(HJ):
                    mm = nc.tensor.matmul(o_ps[i][:, 0:HALF], w2[:, j, :], hid[i][:, j, :],
                                          start=(j == 0), stop=(j == HJ - 1))
                mm.then_inc(o_full, 1)

            with pe.Fori(0, B) as b:
                first(b, 0)
                first(b, 1)
                second(b, 0)
                second(b, 1)

        @block.scalar
        def _(act):
            act.sem_inc(h_done, HJ)
            act.sem_inc(o_full, 2)
            with act.Fori(0, B) as b:
                for i in range(2):
                    act.wait_ge(o_full, b * 2 + (i + 1))
                    for j in range(HJ):
                        act.wait_ge(h_full, b * (2 * HJ) + (i * HJ + j + 1))
                        nc.scalar.activation(hid[i][:, j, :], h_ps[j][:, 0:HALF], ACT.Silu,
                                             bias=b1[:, j:j + 1]).then_inc(h_done, 1)

        @block.vector
        def _(dve):
            dve.sem_inc(y_done, 2)
            for k in range(TAPS_S):
                dve.wait_ge(w1_in[k], 16)
                if k > 0:
                    dve.wait_ge(w_split, k)
                split2(nc, dve, w1[:, k, :], masked[:], w1h[:, k, :], w1l[:, k, :], high, k + 1).then_inc(w_split, 1)
            dve.wait_ge(w_in, 48)
            with dve.Fori(0, B) as b:
                for i in range(2):
                    dve.wait_ge(y_done, b * 2 + (i + 2))
                    dve.wait_ge(o_full, b * 2 + (i + 3))
                    nc.vector.scalar_tensor_tensor(out=part[:], in0=o_ps[i][:, 0:HALF], scalar=b2[:, 0:1],
                                                   in1=z_chunk(zT, b, i), op0=ALU.add, op1=ALU.add).then_inc(part_done, 1)
                    dve.wait_ge(part_done, b * 2 + (i + 1))
                    nc.vector.tensor_tensor(h_chunk(y, b, i), h_chunk(y, b, i), part[:], ALU.add).then_inc(y_done, 1)


def stage2(nc, io, K, scratch):
    gates_d = nc.dram_tensor("gates0", (E0, B * LP), F32, kind="Internal").ap()
    conv_router(nc, io, K, gates_d)
    with ExitStack() as ctx:
        a = Alloc(nc, ctx, "stage2")
        y = a.sb("y", [P, B * L])
        cols = a.sb("ln_cols", [P, 2])
        z_parts = [a.sb(f"z_part{i}", [P, ZW], F32R)[:] for i in range(2)]
        experts(nc, K, scratch, "moe0", E0, "elu", io["moe0_w"], io["moe0_b2"], gates_d, y, z_parts)
        shared_conv(nc, io, K, y, z_parts)
        layer_norm(nc, K, "ln_ffn0", src=y, affine=cols, affine_d=io["ln_ffn0"], add=True)


STAGES[2] = stage2


def expert_layout(w1, b1, w2):
    n = w1.shape[0]
    return np.concatenate([w1, w2.reshape(n, HJ, P, P).transpose(0, 2, 1, 3).reshape(n, P, HID),
                           b1.reshape(n, HJ, P).transpose(0, 2, 1)], 2)


def stage2_layout(f):
    return {
        "iota": np.broadcast_to(np.arange(16, dtype=np.float32), (P, TOK_TILES, 16)),
        "rc_w1": f["L0_ffn_rc_w1"].transpose(1, 2, 0),
        "rc_w2": f["L0_ffn_rc_w2"].transpose(1, 2, 0),
        "rc_b1": f["L0_ffn_rc_b1"][:, None],
        "rc_b2": np.broadcast_to(f["L0_ffn_rc_b2"], (P, E0)),
        "sh_w1": f["L0_ffn_sh_w1"].transpose(1, 2, 0),
        "sh_w2": f["L0_ffn_sh_w2"][:, :, 0].T.reshape(HJ, P, P).transpose(1, 0, 2),
        "sh_b1": f["L0_ffn_sh_b1"].reshape(HJ, P).T,
        "sh_b2": f["L0_ffn_sh_b2"][:, None],
        "moe0_w": expert_layout(f["L0_ffn_e_w1"], f["L0_ffn_e_b1"], f["L0_ffn_e_w2"]),
        "moe0_b2": f["L0_ffn_e_b2"],
        "ln_ffn0": np.stack([f["L0_ffn_ln_g"], f["L0_ffn_ln_b"]], 1),
    }


E3 = 8


def plain_router(nc, io, K, name, E, w_name, b_name, gates_d, pack):
    zT = K["zT"]
    with ExitStack() as ctx:
        a = Alloc(nc, ctx, name)
        W = E if pack == "sum" else 4 * E
        w = a.sb("w", [P, E])
        bias = a.sb("bias", [P, E])
        lg = a.sb("lg", [P, TOK_TILES, E])
        gates = a.sb("gates", [P, TOK_TILES, W])
        packT = a.sb("packT", [W, B * LP])
        l_ps = a.ps("l_ps", [P, TOK_TILES, E])
        pack_ps = a.ps("pack_ps", [P, 2 * BANK])
        w_in, l_done, lg_ready = (a.sem(n) for n in ("w_in", "l_done", "lg_ready"))
        block = ctx.enter_context(nc.Block())

        @block.sync
        def _(sp):
            sp.dma_start(w[:], io[w_name]).then_inc(w_in, 16)
            if b_name:
                sp.dma_start(bias[:], io[b_name]).then_inc(w_in, 16)

        @block.tensor
        def _(pe):
            pe.wait_ge(w_in, 32 if b_name else 16)
            for b in range(B):
                for t in range(TILES):
                    at = LEAD + b * LP + t * P
                    mm = nc.tensor.matmul(l_ps[:, b * TILES + t, :], zT[:, at:at + P], w[:], start=True, stop=True)
            mm.then_inc(l_done, 1)

        @block.vector
        def _(dve):
            dve.wait_ge(l_done, 1)
            if b_name:
                dve.wait_ge(w_in, 32)
                nc.vector.tensor_tensor(lg[:], l_ps[:], bias[:, :].unsqueeze(1).to_broadcast([P, TOK_TILES, E]),
                                        ALU.add).then_inc(lg_ready, 1)
            else:
                nc.vector.tensor_copy(lg[:], l_ps[:]).then_inc(lg_ready, 1)

        top2_gates(nc, K, a, block, lg, (lg_ready, 1), E, gates, pack, pack_ps, packT, gates_d)


def stage8(nc, io, K, scratch):
    gates_d = nc.dram_tensor("gates3", (E3, B * LP), F32, kind="Internal").ap()
    with ExitStack() as ctx:
        a = Alloc(nc, ctx, "stage8")
        y = a.sb("y", [P, B * L])
        cols = a.sb("ln_cols", [P, 2])
        keep = a.sb("keep", [P, B * LP])
        with ExitStack() as ctx2:
            a2 = Alloc(nc, ctx2, "keepz")
            kept = a2.sem("kept")
            block = ctx2.enter_context(nc.Block())

            @block.vector
            def _(dve):
                nc.vector.tensor_copy(keep[:], K["zT"][:, LEAD:ZW]).then_inc(kept, 1)
                dve.wait_ge(kept, 1)

        layer_norm(nc, K, "ln_in3", affine=cols, affine_d=io["ln_in3"], src="zT")
        plain_router(nc, io, K, "router3", E3, "wg3", None, gates_d, "sum")
        z_parts = [a.sb(f"z_part{i}", [P, ZW], F32R)[:] for i in range(2)]
        experts(nc, K, scratch, "moe3", E3, ACT.Gelu_apprx_tanh, io["moe3_w"], io["moe3_b2"], gates_d, y, z_parts)
        with ExitStack() as ctx2:
            a2 = Alloc(nc, ctx2, "resid3")
            done = a2.sem("done")
            block = ctx2.enter_context(nc.Block())

            @block.vector
            def _(dve):
                for b in range(B):
                    yb = y[:, b * L:(b + 1) * L]
                    nc.vector.tensor_tensor(yb, yb, keep[:, b * LP:b * LP + L], ALU.add).then_inc(done, 1)
                dve.wait_ge(done, B)
        layer_norm(nc, K, "ln_out3", src=y, affine=cols, affine_d=io["ln_out3"], add=True)


STAGES[8] = stage8


def stage8_layout(f):
    return {
        "wg3": f["L3_ffn_Wg"],
        "moe3_w": expert_layout(f["L3_ffn_W1"], f["L3_ffn_b1"], f["L3_ffn_W2"]),
        "moe3_b2": f["L3_ffn_b2"],
        "ln_in3": np.stack([f["L3_ffn_ln_g"], f["L3_ffn_ln_b"]], 1),
        "ln_out3": np.stack([f["L3_ffn_out_g"], f["L3_ffn_out_b"]], 1),
    }

def dense_attention(nc, io, K, name, R, w_name, b_name, scale):
    hT, zT = K["hT"], K["zT"]
    with ExitStack() as ctx:
        a = Alloc(nc, ctx, name)
        w = a.sb("w", [P, 2, R])
        bias = a.sb("bias", [R, 2])
        zb = a.sb("zb", [P, LP])
        z_tok = a.sb("z_tok", [P, TILES, P])
        qk = [a.sb(f"qk{j}", [R, LP]) for j in range(2)]
        SLOTS, LAG = 3, 2
        probs = [a.sb(f"probs{i}", [P, LP]) for i in range(SLOTS)]
        probsT = a.sb("probsT", [P, TILES, LP])
        nmax = a.sb("nmax", [P, TILES])
        sums = a.sb("sums", [P, TILES])
        rsum = a.sb("rsum", [P, TILES])
        s_ps = [a.ps(f"s_ps{i}", [P, 2 * BANK]) for i in range(2)]
        t_ps = a.ps("t_ps", [P, 2 * BANK])
        o_ps = [a.ps(f"o_ps{i}", [P, BANK]) for i in range(2)]
        names = ("w_in", "filled", "zb_ready", "p_full", "p_copied", "zt_full", "zt_copied", "s_full", "max_ready", "exp_done",
                 "rs_ready", "scaled", "t_full", "t_copied", "o_full", "o_added", "passed")
        (w_in, filled, zb_ready, p_full, p_copied, zt_full, zt_copied, s_full, max_ready, exp_done,
         rs_ready, scaled, t_full, t_copied, o_full, o_added, passed) = (a.sem(n) for n in names)
        block = ctx.enter_context(nc.Block())
        T = TILES

        @block.sync
        def _(sp):
            sp.dma_start(w[:], io[w_name]).then_inc(w_in, 16)
            if b_name:
                sp.dma_start(bias[:], io[b_name]).then_inc(w_in, 16)

        @block.tensor
        def _(pe):
            pe.wait_ge(w_in, 32 if b_name else 16)
            with pe.Fori(0, B) as b:
                pe.wait_ge(zb_ready, b + 1)
                for j in range(2):
                    for half in range(2):
                        if j == 0:
                            pe.wait_ge(o_added, b * 2 + (half + 1))
                        else:
                            pe.wait_ge(p_copied, b * 4 + (half + 1))
                        nc.tensor.matmul(o_ps[half][0:R, 0:HALF], w[:, j, :], zb[:, half * HALF:half * HALF + HALF],
                                         start=True, stop=True).then_inc(p_full, 1)
                pe.wait_ge(t_copied, b * T + 1)
                for t in range(T):
                    mm = nc.tensor.transpose(t_ps[:, t * P:(t + 1) * P], zb[:, t * P:(t + 1) * P], K["ident"][:])
                mm.then_inc(zt_full, 1)
                pe.wait_ge(p_copied, b * 4 + 4)
                for t in range(T + LAG):
                    if t < T:
                        pe.wait_ge(exp_done, b * T + (t + 1))
                        nc.tensor.matmul(s_ps[t % 2][:, 0:BANK], qk[0][:, t * P:(t + 1) * P], qk[1][:, 0:BANK],
                                         start=True, stop=True)
                        nc.tensor.matmul(s_ps[t % 2][:, BANK:L], qk[0][:, t * P:(t + 1) * P], qk[1][:, BANK:L],
                                         start=True, stop=True).then_inc(s_full, 1)
                    if t >= LAG:
                        i = t - LAG
                        pe.wait_ge(scaled, b * T + (i + 1))
                        if i == 0:
                            pe.wait_ge(zt_copied, b + 1)
                        else:
                            pe.wait_ge(t_copied, b * T + (i + 1))
                        for j in range(T):
                            mm = nc.tensor.transpose(t_ps[:, j * P:(j + 1) * P], probs[i % SLOTS][:, j * P:(j + 1) * P],
                                                     K["ident"][:])
                        mm.then_inc(t_full, 1)
                pe.wait_ge(t_copied, b * T + (T + 1))
                for half in range(2):
                    for j in range(T):
                        mm = nc.tensor.matmul(o_ps[half][:, 0:HALF], z_tok[:, j, :],
                                              probsT[:, j, half * HALF:half * HALF + HALF], start=(j == 0), stop=(j == T - 1))
                    mm.then_inc(o_full, 1)

        def copy_turned(eng, copy, b, t):
            eng.wait_ge(t_full, b * T + (t + 1))
            copy(probsT[:, :, t * P:(t + 1) * P], t_ps[:, 0:LP].rearrange("p (j i) -> p j i", j=T)).then_inc(t_copied, 1)

        @block.scalar
        def _(act):
            act.sem_inc(exp_done, 2)
            act.wait_ge(filled, SLOTS + 2)
            with act.Fori(0, B) as b:
                for t in range(T):
                    act.wait_ge(max_ready, b * T + (t + 1))
                    act.wait_ge(t_full, b * T + (t + 1 - SLOTS)) if t >= SLOTS else act.wait_ge(o_full, b * 2 + 2)
                    nc.scalar.activation(probs[t % SLOTS][:, 0:L], s_ps[t % 2][:, 0:L], ACT.Exp, bias=nmax[:, t:t + 1],
                                         accum_out=sums[:, t:t + 1]).then_inc(exp_done, 1)
                    if t >= LAG and t % 2 == 1:
                        copy_turned(act, nc.scalar.copy, b, t - LAG)
                copy_turned(act, nc.scalar.copy, b, T - 1)

        @block.gpsimd
        def _(pool):
            pool.sem_inc(zt_full, 1)
            with pool.Fori(0, B) as b:
                pool.wait_ge(zt_full, b + 1)
                apart(pool, passed)
                nc.gpsimd.tensor_copy(zb[:], zT[:, bass.ds(b * LP + LEAD, LP)]).then_inc(zb_ready, 1)

        @block.vector
        def _(dve):
            dve.sem_inc(o_added, 2)
            dve.sem_inc(t_copied, 1)
            dve.sem_inc(o_full, 2)
            for x in [p[:, L:LP] for p in probs] + [qk[0][:, L:LP], bias[:] if not b_name else nmax[:]]:
                nc.vector.memset(x, 0.0).then_inc(filled, 1)
            dve.wait_ge(filled, SLOTS + 2)
            dve.wait_ge(w_in, 32 if b_name else 16)
            with dve.Fori(0, B) as b:
                for j in range(2):
                    for half in range(2):
                        dve.wait_ge(p_full, b * 4 + (j * 2 + half + 1))
                        nc.vector.tensor_scalar(qk[j][:, half * HALF:half * HALF + HALF], o_ps[half][0:R, 0:HALF],
                                                bias[:, j:j + 1], (scale, 1.0)[j], ALU.add, ALU.mult).then_inc(p_copied, 1)
                dve.wait_ge(zt_full, b + 2)
                nc.vector.tensor_copy(z_tok[:], t_ps[:, 0:LP].rearrange("p (t c) -> p t c", t=T)).then_inc(zt_copied, 1)
                for t in range(T + LAG):
                    if t < T:
                        dve.wait_ge(s_full, b * T + (t + 1))
                        nc.vector.tensor_reduce(nmax[:, t:t + 1], s_ps[t % 2][:, 0:L], AX.X, ALU.max,
                                                negate=True).then_inc(max_ready, 1)
                    if 1 <= t <= T:
                        i = t - 1
                        dve.wait_ge(exp_done, b * T + (i + 3))
                        nc.vector.reciprocal(rsum[:, i:i + 1], sums[:, i:i + 1]).then_inc(rs_ready, 1)
                        dve.wait_ge(rs_ready, b * T + (i + 1))
                        p = probs[i % SLOTS][:, 0:L]
                        nc.vector.tensor_scalar(p, p, rsum[:, i:i + 1], None,
                                                ALU.mult).then_inc(scaled, 1)
                    if t >= LAG and t % 2 == 0:
                        copy_turned(dve, nc.vector.tensor_copy, b, t - LAG)
                for half in range(2):
                    dve.wait_ge(o_full, b * 2 + (half + 3))
                    nc.vector.tensor_tensor(h_chunk(hT, b, half), h_chunk(hT, b, half), o_ps[half][:, 0:HALF],
                                            ALU.add).then_inc(o_added, 1)


STAGES[3] = lambda nc, io, K, scratch: dense_attention(nc, io, K, "attn1", P, "attn1_w", "attn1_b", float(P) ** -0.5)
STAGES[5] = lambda nc, io, K, scratch: dense_attention(nc, io, K, "attn2", 10, "attn2_w", None, 512.0 ** -0.5)


def dense_attention_layout(f):
    return {
        "attn1_w": np.stack([f["L1_attn_Wq"], f["L1_attn_Wk"]], 1),
        "attn1_b": np.stack([f["L1_attn_bq"], f["L1_attn_bk"]], 1),
        "attn2_w": np.stack([f["L2_attn_W1"], f["L2_attn_W2"].T], 1),
    }


E1 = 8
PICKS = 2 * B


def pooled_gates(nc, io, K, weight_cols, expert_at):
    zT = K["zT"]
    with ExitStack() as ctx:
        a = Alloc(nc, ctx, "pool")
        aw = a.sb("aw", [P, 1])
        ab = a.sb("ab", [1, 1])
        gw = a.sb("gw", [P, E1])
        gb = a.sb("gb", [1, E1])
        ones = a.sb("ones", [1, P])
        row = a.sb("row", [1, L])
        mx = a.sb("mx", [1, 4])
        aw_all = a.sb("aw_all", [P, L])
        prod = a.sb("prod", [P, L])
        pooled = a.sb("pooled", [P, B])
        g = a.sb("g", [1, E1])
        best = a.sb("best", [1, 8])
        at = a.sb("at", [1, 8], U32)
        w8 = a.sb("w8", [1, 4])
        wts = a.sb("wts", [1, PICKS])
        s_ps = a.ps("s_ps", [P, 2 * BANK])
        b_ps = a.ps("b_ps", [P, 2 * BANK])
        g_ps = a.ps("g_ps", [P, BANK])
        w_ps = a.ps("w_ps", [P, BANK])
        w_in, s_full, exp_in, exp_done, row_ready, b_full, pooled_ready, g_full, gexp_in, gexp_done, wts_ready, w_full, chain, chain2, filled = (
            a.sem(n) for n in ("w_in", "s_full", "exp_in", "exp_done", "row_ready", "b_full", "pooled_ready", "g_full",
                               "gexp_in", "gexp_done", "wts_ready", "w_full", "chain", "chain2", "filled"))
        block = ctx.enter_context(nc.Block())

        @block.sync
        def _(sp):
            for dst, src in ((aw, "pool_w"), (ab, "pool_b"), (gw, "gate1_w"), (gb, "gate1_b")):
                sp.dma_start(dst[:], io[src]).then_inc(w_in, 16)

        @block.tensor
        def _(pe):
            pe.wait_ge(w_in, 64)
            pe.wait_ge(filled, 1)
            for b in range(B):
                z0 = LEAD + b * LP
                if b >= 1:
                    pe.wait_ge(exp_done, b)
                nc.tensor.matmul(s_ps[0:1, 0:BANK], aw[:], zT[:, z0:z0 + BANK], start=True, stop=True)
                nc.tensor.matmul(s_ps[0:1, BANK:L], aw[:], zT[:, z0 + BANK:z0 + L], start=True, stop=True).then_inc(s_full, 1)
                pe.wait_ge(row_ready, b + 1)
                nc.tensor.matmul(b_ps[:, 0:BANK], ones[:], row[:, 0:BANK], start=True, stop=True)
                nc.tensor.matmul(b_ps[:, BANK:L], ones[:], row[:, BANK:L], start=True, stop=True).then_inc(b_full, 1)
                pe.wait_ge(pooled_ready, b + 1)
                nc.tensor.matmul(g_ps[0:1, 0:E1], pooled[:, b:b + 1], gw[:], start=True, stop=True).then_inc(g_full, 1)
            pe.wait_ge(wts_ready, 1)
            nc.tensor.matmul(w_ps[:, 0:PICKS], ones[:], wts[:], start=True, stop=True).then_inc(w_full, 1)

        @block.scalar
        def _(act):
            for b in range(B):
                act.wait_ge(exp_in, b + 1)
                nc.scalar.activation(row[:], row[:], ACT.Exp, bias=mx[:, 0:1],
                                     accum_out=mx[:, 1:2]).then_inc(exp_done, 1)
                act.wait_ge(gexp_in, b + 1)
                nc.scalar.activation(g[:], g[:], ACT.Exp, bias=mx[:, 2:3], accum_out=mx[:, 3:4]).then_inc(gexp_done, 1)

        @block.vector
        def _(dve):
            nc.vector.memset(ones[:], 1.0).then_inc(filled, 1)
            dve.wait_ge(w_in, 64)
            c = Chain(dve, chain)
            for b in range(B):
                dve.wait_ge(s_full, b + 1)
                c.link(nc.vector.tensor_scalar(row[:], s_ps[0:1, 0:L], ab[:, 0:1], None, ALU.add))
                nc.vector.tensor_reduce(mx[:, 0:1], row[:], AX.X, ALU.max, negate=True).then_inc(exp_in, 1)
                dve.wait_ge(exp_done, b + 1)
                c.link(nc.vector.reciprocal(w8[:, 0:1], mx[:, 1:2]))
                nc.vector.tensor_scalar(row[:], row[:], w8[:, 0:1], None, ALU.mult).then_inc(row_ready, 1)
                dve.wait_ge(b_full, b + 1)
                z0 = LEAD + b * LP
                c.link(nc.vector.tensor_tensor(prod[:], zT[:, z0:z0 + L], b_ps[:, 0:L], ALU.mult))
                nc.vector.reduce_sum(pooled[:, b:b + 1], prod[:], AX.X).then_inc(pooled_ready, 1)
                dve.wait_ge(g_full, b + 1)
                c.link(nc.vector.tensor_tensor(g[:], g_ps[0:1, 0:E1], gb[:], ALU.add))
                nc.vector.tensor_reduce(mx[:, 2:3], g[:], AX.X, ALU.max, negate=True).then_inc(gexp_in, 1)
                dve.wait_ge(gexp_done, b + 1)
                c.link(nc.vector.reciprocal(w8[:, 1:2], mx[:, 3:4]))
                c.link(nc.vector.tensor_scalar(g[:], g[:], w8[:, 1:2], None, ALU.mult))
                c.link(nc.vector.max(best[:], g[:]))
                c.link(nc.vector.max_index(at[:], best[:], g[:]))
                c.link(nc.vector.tensor_copy(expert_at[:, 2 * b:2 * b + 2], at[:, 0:2]))
                c.link(nc.vector.tensor_tensor(w8[:, 2:3], best[:, 0:1], best[:, 1:2], ALU.add))
                c.link(nc.vector.tensor_scalar(w8[:, 2:3], w8[:, 2:3], 1e-9, None, ALU.add))
                c.link(nc.vector.reciprocal(w8[:, 3:4], w8[:, 2:3]))
                c.link(nc.vector.tensor_scalar(wts[:, 2 * b:2 * b + 2], best[:, 0:2], w8[:, 3:4], None, ALU.mult))
            dve.sem_inc(wts_ready, 1)
            dve.wait_ge(w_full, 1)
            c.link(nc.vector.tensor_copy(weight_cols[:], w_ps[:, 0:PICKS]))


def picked_experts(nc, io, K, weight_cols, expert_at):
    hT, zT = K["hT"], K["zT"]
    with ExitStack() as ctx:
        a = Alloc(nc, ctx, "picked")
        WID = 2 * HID + HJ + 1
        w = [a.sb(f"w{i}", [P, WID]) for i in range(2)]
        hid = [a.sb(f"hid{i}", [P, HJ, HALF]) for i in range(2)]
        eo = [a.sb(f"eo{i}", [P, HALF]) for i in range(2)]
        h_ps = [a.ps(f"h_ps{j}", [P, BANK]) for j in range(HJ)]
        o_ps = [a.ps(f"o_ps{i}", [P, BANK]) for i in range(2)]
        w_in = a.sems("w_in", 2)
        h_full, h_done, o_full, eo_done, added, passed = (a.sem(n) for n in ("h_full", "h_done", "o_full", "eo_done", "added", "passed"))
        block = ctx.enter_context(nc.Block())

        @block.sync
        def _(sp):
            for n in range(PICKS):
                if n >= 2:
                    sp.wait_ge(added, 2 * (n - 1))
                e = sp.value_load(expert_at[0:1, n:n + 1], min_val=0, max_val=E1 - 1)
                sp.dma_start(w[n % 2][:], io["moe1_w"][bass.ds(e, 1), :, :].squeeze(0)).then_inc(w_in[n % 2], 16)

        @block.tensor
        def _(pe):
            def first(n, i):
                b, q = n // 2, 2 * n + i
                if i == 0:
                    pe.wait_ge(w_in[n % 2], 16 * (n // 2 + 1))
                for j in range(HJ):
                    if q >= 1:
                        pe.wait_ge(h_done, (q - 1) * HJ + j + 1)
                    at = LEAD + b * LP + i * HALF
                    nc.tensor.matmul(h_ps[j][:, 0:HALF], w[n % 2][:, j * P:(j + 1) * P], zT[:, at:at + HALF],
                                     start=True, stop=True).then_inc(h_full, 1)

            def second(n, i):
                q = 2 * n + i
                pe.wait_ge(h_done, q * HJ + HJ)
                if q >= 2:
                    pe.wait_ge(eo_done, q - 1)
                for j in range(HJ):
                    mm = nc.tensor.matmul(o_ps[i][:, 0:HALF], w[n % 2][:, HID + j * P:HID + (j + 1) * P],
                                          hid[i][:, j, :], start=(j == 0), stop=(j == HJ - 1))
                mm.then_inc(o_full, 1)

            items = [(n, i) for n in range(PICKS) for i in range(2)]
            for x, (n, i) in enumerate(items):
                first(n, i)
                if x >= 1:
                    second(*items[x - 1])
            second(*items[-1])

        @block.scalar
        def _(act):
            def output(q):
                n, i = q // 2, q % 2
                act.wait_ge(o_full, q + 1)
                if q >= 2:
                    act.wait_ge(added, q - 1)
                nc.scalar.activation(eo[i][:], o_ps[i][:, 0:HALF], ACT.Gelu,
                                     bias=w[n % 2][:, 2 * HID + HJ:2 * HID + HJ + 1]).then_inc(eo_done, 1)

            for q in range(2 * PICKS):
                n, i = q // 2, q % 2
                for j in range(HJ):
                    act.wait_ge(h_full, q * HJ + j + 1)
                    nc.scalar.activation(hid[i][:, j, :], h_ps[j][:, 0:HALF], ACT.Gelu,
                                         bias=w[n % 2][:, 2 * HID + j:2 * HID + j + 1]).then_inc(h_done, 1)
                if q >= 1:
                    output(q - 1)
            output(2 * PICKS - 1)

        @block.vector
        def _(dve):
            for q in range(2 * PICKS):
                n, i = q // 2, q % 2
                b = n // 2
                if q >= 2:
                    dve.wait_ge(added, q - 1)
                dve.wait_ge(eo_done, q + 1)
                h = hT[:, b * L + i * HALF:b * L + (i + 1) * HALF]
                nc.vector.scalar_tensor_tensor(out=h, in0=eo[i][:], scalar=weight_cols[:, n:n + 1], in1=h,
                                               op0=ALU.mult, op1=ALU.add).then_inc(added, 1)


def stage4(nc, io, K, scratch):
    with ExitStack() as ctx:
        a = Alloc(nc, ctx, "stage4")
        weight_cols = a.sb("weight_cols", [P, PICKS])
        expert_at = a.sb("expert_at", [1, PICKS], U32)
        pooled_gates(nc, io, K, weight_cols, expert_at)
        picked_experts(nc, io, K, weight_cols, expert_at)


STAGES[4] = stage4


def stage4_layout(f):
    w = expert_layout(f["L1_ffn_w1"], f["L1_ffn_b1"], f["L1_ffn_w2"])
    return {
        "pool_w": f["L1_ffn_attn_w"],
        "pool_b": f["L1_ffn_attn_b"][None, :],
        "gate1_w": f["L1_ffn_gate_w"],
        "gate1_b": f["L1_ffn_gate_b"][None, :],
        "moe1_w": np.concatenate([w, f["L1_ffn_b2"][:, :, None]], 2),
    }

E2 = 8
STEPS = B
GATES = (0, 2, 3, 1)
RING = 6


def recurrent_experts(nc, io, K, gates_d):
    hT, zT = K["hT"], K["zT"]
    with ExitStack() as ctx:
        a = Alloc(nc, ctx, "lstm")
        WID = 4 * P + 4 * P + P + 4
        w = [a.sb(f"w{i}", [P, WID]) for i in range(2)]
        rows = [[a.sb(f"row{i}_{r}", [P, B * LP]) for r in range(4)] for i in range(2)]
        bo = a.sb("bo", [2 * E2, P])
        gT = a.sb("gT", [2 * E2, B * LP])
        xm = [a.sb(f"xm{i}", [P, HALF]) for i in range(4)]
        gate = [[a.sb(f"gate{i}_{g}", [P, HALF]) for g in range(4)] for i in range(2)]
        cell = [a.sb(f"cell{i}", [P, HALF]) for i in range(4)]
        state = [a.sb(f"state{i}", [P, HALF]) for i in range(4)]
        wstate = [a.sb(f"wstate{i}", [P, HALF]) for i in range(4)]
        tc = [a.sb(f"tc{i}", [P, HALF]) for i in range(2)]
        tmp = a.sb("tmp", [P, HALF])
        g_ps = [a.ps(f"g_ps{i}", [P, BANK]) for i in range(RING)]
        o_ps = [a.ps(f"o_ps{i}", [P, BANK]) for i in range(2)]
        w_in = a.sems("w_in", 2)
        names = ("rows_in", "b_full", "b_added", "xm_ready", "g_full", "g_read", "c_ready", "tc_ready", "h_ready",
                 "hw_ready", "o_full", "y_done", "chain")
        (rows_in, b_full, b_added, xm_ready, g_full, g_read, c_ready, tc_ready, h_ready,
         hw_ready, o_full, y_done, chain) = (a.sem(n) for n in names)
        block = ctx.enter_context(nc.Block())

        PER = 4 * STEPS
        ITEMS = 2 * PER
        GPE = 3 * 4 + 4 * (PER - 4)
        GPT = 2 * GPE
        OPT = 2 * 2 * STEPS

        def parts(x):
            q = x % PER
            return x // PER, q // 4, q // 2 % 2, q % 2

        def gates_of(x):
            return GATES[:3] if parts(x)[1] == 0 else GATES

        def g_base(x):
            e, q = x // PER, x % PER
            return e * GPE + (3 * q if q < 4 else 12 + 4 * (q - 4))

        def out_index(e, s, i):
            return e * 2 * STEPS + 2 * s + i

        def cols(s, i):
            return slice(s * LP + i * HALF, s * LP + i * HALF + HALF)

        def h_cols(s, i):
            return hT[:, s * L + i * HALF:s * L + i * HALF + HALF]

        @block.sync
        def _(sp):
            sp.dma_start(bo[:], io["lstm_bo"]).then_inc(rows_in, 16)
            sp.dma_start(gT[:], gates_d[2 * E2:4 * E2, :]).then_inc(rows_in, 16)
            with sp.Fori(0, E2 // 2) as m:
                for e in range(2):
                    sp.wait_ge(y_done, m * OPT + (e * 2 * STEPS + 2 * STEPS))
                    sp.dma_start(w[e][:], io["lstm_w"][bass.ds(m * 2 + e, 1), :, :].squeeze(0)).then_inc(w_in[e], 16)
                    for r in range(4):
                        sp.dma_start(rows[e][r][:], gates_d[bass.ds(m * 2 + (r * E2 + e), 1), :].to_broadcast([P, B * LP])
                                     ).then_inc(w_in[e], 16)

        @block.gpsimd
        def _(pool):
            pool.sem_inc(hw_ready, 4)

            def mask(m, x):
                e, s, k, i = parts(x)
                if x % PER == 0:
                    pool.wait_ge(w_in[e], m * 80 + 80)
                back = g_base(x - 4) + len(gates_of(x - 4))
                pool.wait_ge(g_full, m * GPT + (back + GPT))
                nc.gpsimd.tensor_tensor(xm[x % 4][:], zT[:, LEAD + s * LP + i * HALF:LEAD + s * LP + i * HALF + HALF],
                                        rows[e][k][:, cols(s, i)], ALU.mult).then_inc(xm_ready, 1)

            def weigh(m, x):
                e, s, k, i = parts(x)
                pool.wait_ge(h_ready, m * ITEMS + (x + 3))
                pool.wait_ge(o_full, m * OPT + (out_index(e, s, i) + 1))
                nc.gpsimd.tensor_tensor(wstate[2 * k + i][:], state[2 * k + i][:], rows[e][2 + k][:, cols(s, i)],
                                        ALU.mult).then_inc(hw_ready, 1)

            with pool.Fori(0, E2 // 2) as m:
                mask(m, 0)
                mask(m, 1)
                for x in range(ITEMS):
                    if x + 2 < ITEMS:
                        mask(m, x + 2)
                    if x >= 1:
                        weigh(m, x - 1)
                weigh(m, ITEMS - 1)

        @block.tensor
        def _(pe):
            pe.wait_ge(rows_in, 32)
            for c, (b, half) in enumerate(CHUNKS):
                if c >= 2:
                    pe.wait_ge(b_added, c - 1)
                nc.tensor.matmul(o_ps[c % 2][:, 0:HALF], bo[:], gT[:, cols(b, half)], start=True, stop=True).then_inc(b_full, 1)
            pe.wait_ge(b_added, NCH)

            def gates(m, x):
                e, s, k, i = parts(x)
                if x % PER == 0:
                    pe.wait_ge(w_in[e], m * 80 + 80)
                pe.wait_ge(xm_ready, m * ITEMS + (x + 1))
                for y, g in enumerate(gates_of(x)):
                    n = g_base(x) + y
                    bank = g_ps[n % RING][:, 0:HALF]
                    pe.wait_ge(g_read, m * GPT + (n + 1))
                    mm = nc.tensor.matmul(bank, w[e][:, g * P:(g + 1) * P], xm[x % 4][:], start=True, stop=(s == 0))
                    if s > 0:
                        if y == 0:
                            pe.wait_ge(h_ready, m * ITEMS + (x - 4 + 3))
                        mm = nc.tensor.matmul(bank, w[e][:, 4 * P + g * P:4 * P + (g + 1) * P], state[2 * k + i][:],
                                              start=False, stop=True)
                    mm.then_inc(g_full, 1)

            def output(m, e, s, i):
                n = out_index(e, s, i)
                pe.wait_ge(hw_ready, m * ITEMS + (e * PER + 4 * s + 2 + i + 5))
                pe.wait_ge(y_done, m * OPT + (n + OPT - 1))
                for k in range(2):
                    mm = nc.tensor.matmul(o_ps[i][:, 0:HALF], w[e][:, 8 * P:9 * P], wstate[2 * k + i][:],
                                          start=(k == 0), stop=(k == 1))
                mm.then_inc(o_full, 1)

            with pe.Fori(0, E2 // 2) as m:
                for x in range(ITEMS):
                    gates(m, x)
                    if x >= 4 and x % 4 < 2:
                        e, s, k, i = parts(x - 4)
                        output(m, e, s, i)
                for i in range(2):
                    output(m, 1, STEPS - 1, i)

        @block.scalar
        def _(act):
            act.sem_inc(g_read, RING)
            act.sem_inc(tc_ready, 4)

            def squash(m, x):
                act.wait_ge(c_ready, m * ITEMS + (x + 1))
                nc.scalar.activation(tc[x % 2][:], cell[x % 4][:], ACT.Tanh).then_inc(tc_ready, 1)

            with act.Fori(0, E2 // 2) as m:
                for x in range(ITEMS):
                    e, s, k, i = parts(x)
                    act.wait_ge(h_ready, m * ITEMS + (x + 1))
                    for y, g in enumerate(gates_of(x)):
                        n = g_base(x) + y
                        act.wait_ge(g_full, m * GPT + (n + 1 + GPT))
                        nc.scalar.activation(gate[x % 2][g][:], g_ps[n % RING][:, 0:HALF], ACT.Tanh if g == 2 else ACT.Sigmoid,
                                             bias=w[e][:, 9 * P + g:9 * P + g + 1]).then_inc(g_read, 1)
                    if x >= 1:
                        squash(m, x - 1)
                squash(m, ITEMS - 1)

        @block.vector
        def _(dve):
            dve.sem_inc(g_full, GPT)
            dve.sem_inc(h_ready, 2)
            dve.sem_inc(o_full, 2)
            dve.sem_inc(y_done, OPT)
            for c, (b, half) in enumerate(CHUNKS):
                dve.wait_ge(b_full, c + 1)
                h = h_cols(b, half)
                nc.vector.tensor_tensor(h, h, o_ps[c % 2][:, 0:HALF], ALU.add).then_inc(b_added, 1)
            dve.wait_ge(b_added, NCH)

            def cells(m, x, c):
                e, s, k, i = parts(x)
                dve.wait_ge(g_read, m * GPT + (g_base(x) + len(gates_of(x)) + RING))
                dve.wait_ge(tc_ready, m * ITEMS + (x + 1))
                g = gate[x % 2]
                if s == 0:
                    nc.vector.tensor_tensor(cell[x % 4][:], g[0][:], g[2][:], ALU.mult).then_inc(c_ready, 1)
                else:
                    nc.vector.tensor_tensor(cell[x % 4][:], g[1][:], cell[x % 4][:], ALU.mult)
                    c.link(nc.vector.tensor_tensor(tmp[:], g[0][:], g[2][:], ALU.mult))
                    nc.vector.tensor_tensor(cell[x % 4][:], cell[x % 4][:], tmp[:], ALU.add).then_inc(c_ready, 1)

            def states(m, x):
                e, s, k, i = parts(x)
                dve.wait_ge(tc_ready, m * ITEMS + (x + 5))
                dve.wait_ge(hw_ready, m * ITEMS + (x + 1))
                nc.vector.tensor_tensor(state[x % 4][:], gate[x % 2][3][:], tc[x % 2][:], ALU.mult).then_inc(h_ready, 1)

            def add(m, e, s, i):
                n = out_index(e, s, i)
                dve.wait_ge(o_full, m * OPT + (n + 3))
                h = h_cols(s, i)
                nc.vector.tensor_tensor(h, h, o_ps[i][:, 0:HALF], ALU.add).then_inc(y_done, 1)

            with dve.Fori(0, E2 // 2) as m:
                c = Chain(dve, chain, m, 2 * (PER - 4))
                for x in range(ITEMS):
                    cells(m, x, c)
                    if x >= 1:
                        states(m, x - 1)
                    if x >= 5 and x % 4 in (1, 2):
                        e, s, k, i = parts(x - 5)
                        add(m, e, s, i)
                states(m, ITEMS - 1)
                for i in range(2):
                    add(m, 1, STEPS - 1, i)
                c.end()


def stage6(nc, io, K, scratch):
    gates_d = nc.dram_tensor("gates2", (4 * E2, B * LP), F32, kind="Internal").ap()
    plain_router(nc, io, K, "router2", E2, "router2_w", "router2_b", gates_d, "slots")
    recurrent_experts(nc, io, K, gates_d)


STAGES[6] = stage6


def stage6_layout(f):
    return {
        "router2_w": f["L2_ffn_router_w"],
        "router2_b": np.broadcast_to(f["L2_ffn_router_b"], (P, E2)),
        "lstm_w": np.concatenate([f["L2_ffn_Wi"], f["L2_ffn_Wh"], f["L2_ffn_Wo"],
                                  f["L2_ffn_b"].reshape(E2, 4, P).transpose(0, 2, 1)], 2),
        "lstm_bo": np.concatenate([f["L2_ffn_bo"], f["L2_ffn_bo"]], 0),
    }


HEADS3 = 16
D3 = P // 4
GROUPS = 4
HPG = HEADS3 // GROUPS
WM = 3 * P + 2


def causal_weights(nc, io, K, merged_d, z_d):
    with ExitStack() as ctx:
        a = Alloc(nc, ctx, "causw")
        wl = a.sb("wl", [P, HEADS3, P])
        bl = a.sb("bl", [P, HEADS3])
        wqkv = a.sb("wqkv", [P, HEADS3, 3 * D3])
        wo = a.sb("wo", [P, GROUPS, P])
        bo = a.sb("bo", [P, 1])
        merged = a.sb("merged", [P, GROUPS, WM])
        bv = a.sb("bv", [P, GROUPS])
        shift = a.sb("shift", [P, 1])
        m_ps = [a.ps(f"m_ps{g}", [P, BANK]) for g in range(GROUPS)]
        b_ps = [a.ps(f"b_ps{j}", [P, BANK]) for j in range(3)]
        o_ps = a.ps("o_ps", [P, BANK])
        w_in, m_full, b_full, m_copied, bv_ready, o_full, shifted, stored, chain = (a.sem(n) for n in (
            "w_in", "m_full", "b_full", "m_copied", "bv_ready", "o_full", "shifted", "stored", "chain"))
        block = ctx.enter_context(nc.Block())

        @block.sync
        def _(sp):
            for dst, src in ((wl, "caus_wl"), (bl, "caus_bl"), (wqkv, "caus_wqkv"), (wo, "caus_wo"), (bo, "caus_bo")):
                sp.dma_start(dst[:], io[src]).then_inc(w_in, 16)
            sp.dma_start(z_d.rearrange("b p c -> p b c"),
                         K["zT"][:, LEAD:LEAD + B * LP].rearrange("p (b c) -> p b c", b=B)).then_inc(stored, 16)
            sp.wait_ge(m_copied, GROUPS + 2)
            sp.dma_start(merged_d.rearrange("g p w -> p g w"), merged[:]).then_inc(stored, 16)
            sp.wait_ge(stored, 32)

        @block.tensor
        def _(pe):
            pe.wait_ge(w_in, 80)
            for g in range(GROUPS):
                for hh in range(HPG):
                    h = g * HPG + hh
                    mm = nc.tensor.matmul(m_ps[g][:, hh * 3 * D3:(hh + 1) * 3 * D3], wl[:, h, :], wqkv[:, h, :],
                                          start=True, stop=True)
                mm.then_inc(m_full, 1)
            for j in range(3):
                for h in range(HEADS3):
                    g, hh = h // HPG, h % HPG
                    mm = nc.tensor.matmul(b_ps[j][hh * D3:(hh + 1) * D3, g:g + 1], wqkv[:, h, j * D3:(j + 1) * D3],
                                          bl[:, h:h + 1], start=True, stop=True)
                mm.then_inc(b_full, 1)
            pe.wait_ge(bv_ready, 1)
            for g in range(GROUPS):
                mm = nc.tensor.matmul(o_ps[:, 0:1], wo[:, g, :], bv[:, g:g + 1], start=(g == 0), stop=(g == GROUPS - 1))
            mm.then_inc(o_full, 1)

        @block.vector
        def _(dve):
            for g in range(GROUPS):
                dve.wait_ge(m_full, g + 1)
                nc.vector.tensor_copy(merged[:, g, 0:3 * P].rearrange("p (j h d) -> p h j d", j=3, h=HPG),
                                      m_ps[g][:, 0:3 * P].rearrange("p (h j d) -> p h j d", h=HPG, j=3)).then_inc(m_copied, 1)
            dve.wait_ge(b_full, 3)
            for j in range(2):
                nc.vector.tensor_copy(merged[:, :, 3 * P + j:3 * P + j + 1], b_ps[j][:, 0:GROUPS].unsqueeze(2)).then_inc(m_copied, 1)
            nc.vector.tensor_copy(bv[:], b_ps[2][:, 0:GROUPS]).then_inc(bv_ready, 1)
            dve.wait_ge(o_full, 1)
            dve.wait_ge(w_in, 80)
            nc.vector.tensor_tensor(shift[:], o_ps[:, 0:1], bo[:], ALU.add).then_inc(chain, 1)
            dve.wait_ge(chain, 1)
            nc.vector.tensor_scalar(K["hT"][:], K["hT"][:], shift[:, 0:1], None, ALU.add).then_inc(shifted, 1)


def causal_attention(nc, io, K, merged_d, z_d):
    hT = K["hT"]
    with ExitStack() as ctx:
        a = Alloc(nc, ctx, "caus")
        T = TILES
        W = [min((t + 1) * P, L) for t in range(T)]
        PARTS = [1 if w <= BANK else 2 for w in W]
        wm = a.sb("wm", [P, WM])
        wo = a.sb("wo", [P, P])
        identb = a.sb("identb", [P, P], BF16)
        mask32 = a.sb("mask32", [P, P])
        mask = a.sb("mask", [P, P], BF16)
        zb = a.sb("zb", [P, LP])
        q_sb = a.sb("q_sb", [P, LP])
        k_sb = a.sb("k_sb", [P, LP])
        v_tok = a.sb("v_tok", [P, T, P])
        RING = 4
        probs = [a.sb(f"probs{i}", [P, LP]) for i in range(RING)]
        probsT = [a.sb(f"probsT{i}", [P, T, LP]) for i in range(2)]
        nmax = a.sb("nmax", [P, HPG * T])
        sums = a.sb("sums", [P, HPG * T])
        rsum = a.sb("rsum", [P, HPG * T])
        fT = a.sb("fT", [P, L])
        s_ps = [a.ps(f"s_ps{i}", [P, 2, BANK]) for i in range(2)]
        t_ps = [a.ps(f"t_ps{i}", [P, BANK]) for i in range(2)]
        f_ps = a.ps("f_ps", [P, 2 * BANK])
        t_copied = a.sems("t_copied", 2)
        names = ("w_in", "wo_in", "in_free", "masks_in", "filled", "s_full", "max_ready", "exp_done", "rs_ready", "scaled",
                 "t_full", "pv_full", "f_full", "f_copied0", "f_copied1", "passed")
        (w_in, wo_in, in_free, masks_in, filled, s_full, max_ready, exp_done, rs_ready, scaled, t_full,
         pv_full, f_full, f_copied0, f_copied1, passed) = (a.sem(n) for n in names)
        block = ctx.enter_context(nc.Block())
        X = HPG * T
        LAG = 2
        TURNS = B * GROUPS
        COLS = ((0, BANK), (BANK, L))

        def turned(x):
            t = x % T
            cuts = [0, t + 1] if t < 4 else [0, 3, t + 1]
            return [("turn", x, j0, j1) for j0, j1 in zip(cuts, cuts[1:])]

        first = [("qk", j, half) for j in range(2) for half in range(2)] + [("v", 0), ("v", 1)]
        plan = [c for x in range(X - 1) for c in turned(x)]
        plan += first[:1] + turned(X - 1) + first[1:] + [("out", 0), ("out", 1)]
        C = len(plan)
        START = len(first) // 2 + 1
        assert C % 2 == 0

        def emptied(n, through):
            last = plan.index(through)
            return [START + n * (C // 2) + len([c for c in range(last + 1) if c % 2 == i]) for i in range(2)]

        def scores_of(x, n_cols=None):
            t = x % T
            return s_ps[x % 2][:, 0:PARTS[t], 0:W[t] // PARTS[t]]

        @block.sync
        def _(sp):
            sp.dma_start(mask32[:], io["causal_mask"]).then_inc(masks_in, 16)
            sp.sem_inc(in_free, 1)
            with sp.Fori(0, B) as b:
                with sp.Fori(0, GROUPS) as g:
                    n = b * GROUPS + g
                    sp.wait_ge(in_free, n + 1)
                    sp.dma_start(wm[:], merged_d[bass.ds(g, 1), :, :].squeeze(0)).then_inc(w_in, 16)
                    sp.dma_start(zb[:], z_d[bass.ds(b, 1), :, :].squeeze(0)).then_inc(w_in, 16)
                    sp.wait_ge(in_free, n + 2)
                    sp.dma_start(wo[:], io["caus_wo_g"][bass.ds(g, 1), :, :].squeeze(0)).then_inc(wo_in, 16)
            sp.wait_ge(in_free, TURNS + 1)
            sp.dma_start(wm[:], merged_d[0]).then_inc(w_in, 16)
            sp.dma_start(zb[:], z_d[0]).then_inc(w_in, 16)

        @block.tensor
        def _(pe):
            def project(item, bank):
                if item[0] == "qk":
                    cols = slice(item[2] * HALF, (item[2] + 1) * HALF)
                    mm = nc.tensor.matmul(bank[:, 0:HALF], wm[:, item[1] * P:(item[1] + 1) * P], zb[:, cols],
                                          start=True, stop=True)
                else:
                    for i in range(T // 2):
                        t = item[1] * (T // 2) + i
                        mm = nc.tensor.matmul(bank[:, i * P:(i + 1) * P], zb[:, t * P:(t + 1) * P], wm[:, 2 * P:3 * P],
                                              start=True, stop=True)
                mm.then_inc(t_full, 1)

            pe.wait_ge(filled, RING + 4)
            pe.wait_ge(w_in, 32)
            for p, item in enumerate(first):
                if p >= 2:
                    pe.wait_ge(t_copied[p % 2], p // 2 + 1)
                project(item, t_ps[p % 2])

            with pe.Fori(0, TURNS) as n:
                def free_bank(c):
                    pe.wait_ge(t_copied[c % 2], n * (C // 2) + (START + c // 2))
                    return t_ps[c % 2]

                def scores(x):
                    hh, t = x // T, x % T
                    rows = slice(hh * D3, (hh + 1) * D3)
                    pe.wait_ge(exp_done, n * X + (x + 1))
                    wide = W[t] // PARTS[t]
                    for part in range(PARTS[t]):
                        diag = part == PARTS[t] - 1
                        mm = nc.tensor.matmul(s_ps[x % 2][:, part, 0:wide], q_sb[rows, t * P:(t + 1) * P],
                                              k_sb[rows, part * wide:(part + 1) * wide],
                                              start=True, stop=not diag, tile_position=(hh * D3, 0))
                        if diag:
                            late = W[t] - t * P
                            mm = nc.tensor.matmul(s_ps[x % 2][:, part, wide - late:wide], identb[:], mask[:, 0:late],
                                                  start=False, stop=True)
                    mm.then_inc(s_full, 1)

                def turn_probs(x):
                    pe.wait_ge(scaled, n * X + (x + 1))
                    for item in turned(x):
                        bank = free_bank(plan.index(item))
                        for i, j in enumerate(range(item[2], item[3])):
                            mm = nc.tensor.transpose(bank[:, i * P:(i + 1) * P], probs[x % RING][:, j * P:(j + 1) * P],
                                                     K["ident"][:])
                        mm.then_inc(t_full, 1)

                def values(hh, half, tiles):
                    if tiles[0] == 0:
                        last = turned(hh * T + (3, T - 1)[half])[-1]
                        for i, count in enumerate(emptied(n, last)):
                            pe.wait_ge(t_copied[i], count)
                    for j in tiles:
                        c0, c1 = max(COLS[half][0], j * P), COLS[half][1]
                        mm = nc.tensor.matmul(f_ps[hh * D3:(hh + 1) * D3, c0:c1], v_tok[:, j, hh * D3:(hh + 1) * D3],
                                              probsT[hh % 2][:, j, c0:c1], start=(j == 0), stop=(j == (3, T - 1)[half]))
                    if tiles[-1] == (3, T - 1)[half]:
                        if half == 1:
                            mm.then_inc(pv_full, 1)
                        elif hh == HPG - 1:
                            mm.then_inc(f_full, 1)

                spread = {0: [(0, [0])], 1: [(0, [1])], 2: [(0, [2, 3]), (1, [0, 1])], 3: [(1, [2, 3, 4])], 4: [(1, [5])], 5: []}
                for i in range(2):
                    pe.wait_ge(t_copied[i], n * (C // 2) + (START - 1))
                for x in range(X):
                    scores(x)
                    if x == LAG:
                        for i in range(2):
                            pe.wait_ge(t_copied[i], n * (C // 2) + START)
                        pe.sem_inc(in_free, 1)
                    if x >= LAG:
                        turn_probs(x - LAG)
                    if x >= T:
                        for half, tiles in spread[x % T]:
                            values(x // T - 1, half, tiles)
                hh = HPG - 1
                turn_probs(X - 2)
                values(hh, 0, [0, 1])
                pe.wait_ge(w_in, n * 32 + 64)
                project(first[0], free_bank(plan.index(first[0])))
                turn_probs(X - 1)
                values(hh, 0, [2, 3])
                for item in first[1:4]:
                    project(item, free_bank(plan.index(item)))
                values(hh, 1, list(range(T)))
                for item in first[4:]:
                    project(item, free_bank(plan.index(item)))
                pe.wait_ge(wo_in, n * 16 + 16)
                for half, (c0, c1) in enumerate(COLS):
                    bank = free_bank(plan.index(("out", half)))
                    pe.wait_ge((f_copied0, f_copied1)[half], n + 1)
                    nc.tensor.matmul(bank[:, 0:c1 - c0], wo[:], fT[:, c0:c1], start=True, stop=True).then_inc(t_full, 1)

        def empty_bank(eng, engine_add, copy, n, c, item, opening=False):
            bank = t_ps[c % 2]
            eng.wait_ge(t_full, c + 1 if opening else n * C + (len(first) + c + 1))
            if item[0] == "turn":
                _, x, j0, j1 = item
                hh, t = x // T, x % T
                if t < 2:
                    eng.wait_ge(pv_full, n * HPG + (hh + 1))
                wide = min(P, L - t * P)
                src = bank[:, 0:(j1 - j0) * P].rearrange("p (j i) -> p j i", j=j1 - j0)
                copy(probsT[hh % 2][:, j0:j1, t * P:t * P + wide], src[:, :, 0:wide]).then_inc(t_copied[c % 2], 1)
            elif item[0] == "qk":
                _, j, half = item
                if not opening:
                    eng.wait_ge(s_full, n * X + X)
                dst = (q_sb, k_sb)[j][:, half * HALF:(half + 1) * HALF]
                engine_add(dst, bank[:, 0:HALF], wm[:, 3 * P + j:3 * P + j + 1]).then_inc(t_copied[c % 2], 1)
            else:
                assert item[0] == "v"
                if not opening:
                    eng.wait_ge(pv_full, n * HPG + (HPG + 2))
                t0 = item[1] * (T // 2)
                copy(v_tok[:, t0:t0 + T // 2, :], bank[:, 0:T // 2 * P].rearrange("p (t c) -> p t c", c=P)).then_inc(
                    t_copied[c % 2], 1)

        @block.scalar
        def _(act):
            act.wait_ge(filled, RING + 4)

            def add(dst, src, col):
                return nc.scalar.activation(dst, src, ACT.Identity, bias=col)

            for p in (1, 3, 5):
                empty_bank(act, add, nc.scalar.copy, 0, p, first[p], opening=True)
            with act.Fori(0, TURNS) as n:
                done = 0

                def empty_through(last):
                    nonlocal done
                    end = plan.index(last) + 1
                    for c in range(done, end):
                        if c % 2 == 1:
                            empty_bank(act, add, nc.scalar.copy, n, c, plan[c])
                    done = end

                for x in range(X):
                    act.wait_ge(max_ready, n * X + (x + 1))
                    if x >= RING:
                        act.wait_ge(t_full, n * C + (len(first) + plan.index(turned(x - RING)[-1]) + 1))
                    t = x % T
                    nc.scalar.activation(probs[x % RING][:, 0:W[t]].rearrange("p (a c) -> p a c", a=PARTS[t]), scores_of(x),
                                         ACT.Exp, bias=nmax[:, x:x + 1], accum_out=sums[:, x:x + 1]).then_inc(exp_done, 1)
                    if x >= LAG:
                        empty_through(turned(x - LAG)[-1])
                empty_through(turned(X - 1)[-1])
                act.wait_ge(f_full, n + 1)
                nc.scalar.copy(fT[:, 0:BANK], f_ps[:, 0:BANK]).then_inc(f_copied0, 1)
                empty_through(first[-1])

        @block.vector
        def _(dve):
            dve.sem_inc(exp_done, 2)
            dve.sem_inc(pv_full, 2)
            for i in range(2):
                dve.sem_inc(t_copied[i], 1)
            for x in [q_sb[:, L:LP], k_sb[:, L:LP]] + [p[:, L:LP] for p in probs]:
                nc.vector.memset(x, 0.0).then_inc(filled, 1)
            nc.vector.tensor_copy(identb[:], K["ident"][:]).then_inc(filled, 1)
            dve.wait_ge(masks_in, 16)
            nc.vector.tensor_copy(mask[:], mask32[:]).then_inc(filled, 1)
            dve.wait_ge(filled, RING + 4)

            def add(dst, src, col):
                return nc.vector.tensor_scalar(dst, src, col, None, ALU.add)

            for p in (0, 2, 4):
                empty_bank(dve, add, nc.vector.tensor_copy, 0, p, first[p], opening=True)
            with dve.Fori(0, B) as b:
                with dve.Fori(0, GROUPS) as g:
                    n = b * GROUPS + g
                    done = 0

                    def empty_through(last):
                        nonlocal done
                        end = plan.index(last) + 1
                        for c in range(done, end):
                            if c % 2 == 0:
                                empty_bank(dve, add, nc.vector.tensor_copy, n, c, plan[c])
                        done = end

                    def scale(x):
                        dve.wait_ge(exp_done, n * X + (x + 3))
                        p = probs[x % RING][:, 0:W[x % T]]
                        nc.vector.reciprocal(rsum[:, x:x + 1], sums[:, x:x + 1]).then_inc(rs_ready, 1)
                        dve.wait_ge(rs_ready, n * X + (x + 1))
                        nc.vector.tensor_scalar(p, p, rsum[:, x:x + 1], None, ALU.mult).then_inc(scaled, 1)

                    for x in range(X):
                        dve.wait_ge(s_full, n * X + (x + 1))
                        nc.vector.tensor_reduce(nmax[:, x:x + 1], scores_of(x), AX.XY if PARTS[x % T] > 1 else AX.X, ALU.max,
                                                negate=True).then_inc(max_ready, 1)
                        if x >= 1:
                            scale(x - 1)
                        if x >= LAG:
                            empty_through(turned(x - LAG)[-1])
                    scale(X - 1)
                    empty_through(first[3])
                    dve.wait_ge(pv_full, n * HPG + (HPG + 2))
                    nc.vector.tensor_copy(fT[:, BANK:L], f_ps[:, BANK:L]).then_inc(f_copied1, 1)
                    empty_through(first[-1])
                    for half, (c0, c1) in enumerate(COLS):
                        c = plan.index(("out", half))
                        dve.wait_ge(t_full, n * C + (len(first) + c + 1))
                        h = hT[:, bass.ds(b * L + c0, c1 - c0)]
                        nc.vector.tensor_tensor(h, h, t_ps[c % 2][:, 0:c1 - c0], ALU.add).then_inc(t_copied[c % 2], 1)
                    dve.wait_ge(t_copied[1], n * (C // 2) + (START + C // 2))
                    apart(dve, passed)


def stage7(nc, io, K, scratch):
    merged_d = nc.dram_tensor("merged", (GROUPS, P, WM), F32, kind="Internal").ap()
    z_d = nc.dram_tensor("z_of_batch", (B, P, LP), F32, kind="Internal").ap()
    causal_weights(nc, io, K, merged_d, z_d)
    causal_attention(nc, io, K, merged_d, z_d)


STAGES[7] = stage7


def stage7_layout(f):
    qkv = np.concatenate([f["L3_attn_Wq"], f["L3_attn_Wk"], f["L3_attn_Wv"]], 2)
    wo = f["L3_attn_Wo"].T.reshape(GROUPS, P, P)
    late = np.arange(P)[None, :] > np.arange(P)[:, None]
    return {
        "caus_wl": f["L3_attn_Wl"].transpose(1, 0, 2),
        "caus_bl": f["L3_attn_bl"].T,
        "caus_wqkv": qkv.transpose(1, 0, 2),
        "caus_wo": wo.transpose(1, 0, 2),
        "caus_wo_g": wo,
        "caus_bo": f["L3_attn_bo"][:, None],
        "causal_mask": np.where(late, -1e30, 0.0).astype(np.float32),
    }


def laid_out(inputs):
    f = {k: np.asarray(v) for k, v in inputs.items()}
    io = {
        "ident": np.eye(P, dtype=np.float32),
        "mean_all": np.full((P, P), 1.0 / P, np.float32),
        "center": (np.eye(P) - 1.0 / P).astype(np.float32),
        "avg_rows": np.repeat(np.eye(GROUP_MAX, dtype=np.float32)[None] / P, P, 0),
        "spread_rows": np.repeat(np.eye(GROUP_MAX, dtype=np.float32)[:, :, None], P, 2),
        "x": f["x"].transpose(2, 0, 1).reshape(P, B * S_IN),
        "tok_w": f["L0_tok_W"].reshape(P, CONTEXT, P).transpose(2, 1, 0),
        "tok_cols": np.stack([f["L0_tok_b"], f["L0_tok_gamma"], f["L0_tok_beta"]], 1),
    }
    for more in LAYOUTS:
        io.update(more(f))
    return {k: np.ascontiguousarray(v) for k, v in io.items()}


LAYOUTS = [stage1_layout, stage2_layout, stage8_layout, dense_attention_layout, stage4_layout,
           stage6_layout, stage7_layout]


def kernel(**inputs):
    import concourse.bacc as _bacc
    from concourse.bass_utils import run_bass_kernel_spmd as _run

    nc = _bacc.Bacc("TRN2", target_bir_lowering=False, num_devices=1)
    arrays, io = {}, {}
    for name, v in laid_out(inputs).items():
        arrays[f"in_{name}"] = v
        io[name] = nc.dram_tensor(f"in_{name}", v.shape, mybir.dt.from_np(v.dtype), kind="ExternalInput").ap()
    out = nc.dram_tensor("out_h", (P, B * L), F32, kind="ExternalOutput").ap()
    scratch = {}
    audio_tower(nc, io, out, scratch)
    r = _run(nc, [arrays], core_ids=[0])
    return r.results[0]["out_h"].reshape(P, B, L).transpose(1, 2, 0)
```
